# Optimizing a Trainium2 kernel written in Bass

```python
import numpy as np
import jax
import jax.numpy as jnp

def _softmax(x, axis=-1):
    return jax.nn.softmax(x, axis=axis)

def _gelu(x):
    return jax.nn.gelu(x, approximate=True)

def _silu(x):
    return jax.nn.silu(x)

def _sigmoid(x):
    return jax.nn.sigmoid(x)

def _layernorm(x, axis=-1, eps=1e-05):
    m = jnp.mean(x, axis=axis, keepdims=True)
    v = jnp.var(x, axis=axis, keepdims=True)
    return (x - m) / jnp.sqrt(v + eps)

def _scatter_add(tgt, idx, src, axis=0):
    return tgt.at[idx].add(src)

def _segment_sum(src, seg, n):
    return jax.ops.segment_sum(src, seg, n)
kernel_name = 'mk_recurrent_d4_jaxref_r8_ced132'

def setup_inputs(seed: int=0):
    np.random.seed(seed)
    _w = jnp.asarray

    def _L0_attn_setup():
        import jax, jax.numpy as jnp
        import numpy as np
        HIDDEN = 128
        HEADS = 16
        HEAD_DIM = HIDDEN // HEADS
        B, S = (4, 256)
        key = jax.random.key(seed)
        ks = jax.random.split(key, 10)
        scale = 1.0 / np.sqrt(HIDDEN)

        def lin(k):
            return jax.random.uniform(k, (HIDDEN, HIDDEN), jnp.float32, -scale, scale)
        return {'x': jax.random.normal(ks[0], (B, S, HIDDEN), jnp.float32), 'Wq': lin(ks[1]), 'bq': jnp.zeros((HIDDEN,), jnp.float32), 'Wk': lin(ks[2]), 'bk': jnp.zeros((HIDDEN,), jnp.float32), 'Wv': lin(ks[3]), 'bv': jnp.zeros((HIDDEN,), jnp.float32), 'Wo': lin(ks[4]), 'bo': jnp.zeros((HIDDEN,), jnp.float32), 'head_mask': jnp.ones((HEADS,), jnp.float32)}
    _L0_attn_in = _L0_attn_setup()

    def _L0_ffn_setup():
        import jax, jax.numpy as jnp
        import numpy as np
        B, T, C, H, E, K = (4, 128, 128, 128, 8, 2)

        def _swiglu(x):
            a, b = jnp.split(x, 2, axis=-1)
            return jax.nn.silu(a) * b
        key = jax.random.key(seed)
        ks = jax.random.split(key, 6)
        s = 0.02
        x = jax.random.normal(ks[0], (B, T, C), jnp.float32)
        w_shared_in = jax.random.normal(ks[1], (C, 2 * H), jnp.float32) * s
        w_shared_out = jax.random.normal(ks[2], (H, C), jnp.float32) * s
        w1_shared = jax.random.normal(ks[3], (C, 2 * H), jnp.float32) * s
        w2 = jax.random.normal(ks[4], (E, H, C), jnp.float32) * s
        w_gate = jax.random.normal(ks[5], (C, E), jnp.float32) * s
        gate_bias = jnp.zeros((E,), jnp.float32)
        return {'x': x, 'w_shared_in': w_shared_in, 'w_shared_out': w_shared_out, 'w1_shared': w1_shared, 'w2': w2, 'w_gate': w_gate, 'gate_bias': gate_bias}
    _L0_ffn_in = _L0_ffn_setup()

    def _L1_attn_setup():
        import jax, jax.numpy as jnp
        import numpy as np
        D_MODEL = 128
        D_STATE = 16
        D_CONV = 4
        EXPAND = 2
        D_INNER = EXPAND * D_MODEL
        DT_RANK = D_MODEL // 16
        BSZ = 2
        SEQ = 128

        def _silu(x):
            return x * jax.nn.sigmoid(x)

        def _mamba(x, in_proj, conv_w, conv_b, x_proj, dt_w, dt_b, A_log, Dp, out_proj):
            Bb, Ll, _ = x.shape
            xz = jnp.einsum('bld,ed->ble', x, in_proj)
            xi, z = jnp.split(xz, 2, axis=-1)
            xp = jnp.pad(xi, ((0, 0), (D_CONV - 1, 0), (0, 0)))
            xc = conv_b + sum((conv_w[:, k] * xp[:, k:k + Ll, :] for k in range(D_CONV)))
            xc = _silu(xc)
            dbl = jnp.einsum('ble,fe->blf', xc, x_proj)
            dt, Bm, Cm = jnp.split(dbl, [DT_RANK, DT_RANK + D_STATE], axis=-1)
            delta = jax.nn.softplus(jnp.einsum('blr,er->ble', dt, dt_w) + dt_b)
            A = -jnp.exp(A_log)
            dA = jnp.exp(delta[..., None] * A)
            dBu = (delta * xc)[..., None] * Bm[:, :, None, :]

            def step(h, t):
                dA_t, dBu_t, C_t = t
                h = dA_t * h + dBu_t
                return (h, jnp.einsum('ben,bn->be', h, C_t))
            h0 = jnp.zeros((Bb, D_INNER, D_STATE), x.dtype)
            _, ys = jax.lax.scan(step, h0, (dA.transpose(1, 0, 2, 3), dBu.transpose(1, 0, 2, 3), Cm.transpose(1, 0, 2)))
            y = ys.transpose(1, 0, 2) + xc * Dp
            y = y * _silu(z)
            return jnp.einsum('ble,de->bld', y, out_proj)
        key = jax.random.key(seed)
        ks = jax.random.split(key, 4)

        def nrm(k, shape, s=0.02):
            return s * jax.random.normal(k, shape, dtype=jnp.float32)

        def mamba_params(kb):
            k = jax.random.split(kb, 6)
            return dict(in_proj=nrm(k[0], (2 * D_INNER, D_MODEL)), conv_w=nrm(k[1], (D_INNER, D_CONV), 0.2), conv_b=jnp.zeros((D_INNER,), jnp.float32), x_proj=nrm(k[2], (DT_RANK + 2 * D_STATE, D_INNER)), dt_w=nrm(k[3], (D_INNER, DT_RANK), 0.1), dt_b=nrm(k[4], (D_INNER,), 0.5) - 4.0, A_log=jnp.log(jnp.broadcast_to(jnp.arange(1, D_STATE + 1, dtype=jnp.float32), (D_INNER, D_STATE))), D=jnp.ones((D_INNER,), jnp.float32), out_proj=nrm(k[5], (D_MODEL, D_INNER)))
        inp = {'x': jax.random.normal(ks[2], (BSZ, SEQ, D_MODEL), dtype=jnp.float32)}
        for name, p in (('fwd', mamba_params(ks[0])), ('bwd', mamba_params(ks[1]))):
            for kk, v in p.items():
                inp[f'{name}_{kk}'] = v
        inp['merge_w'] = nrm(ks[3], (D_MODEL, 2 * D_MODEL))
        return inp
    _L1_attn_in = _L1_attn_setup()

    def _L1_ffn_setup():
        import jax, jax.numpy as jnp
        import numpy as np
        B, L, H, E, FF, C = (4, 256, 128, 8, 512, 2)
        key = jax.random.key(seed)
        ks = jax.random.split(key, 6)
        s = 0.02
        return {'x': jax.random.normal(ks[0], (B, L, H), dtype=jnp.float32), 'Wg': jax.random.normal(ks[1], (H, E), dtype=jnp.float32) * s, 'W1': jax.random.normal(ks[2], (E, H, FF), dtype=jnp.float32) * s, 'b1': jnp.zeros((E, FF), dtype=jnp.float32), 'W2': jax.random.normal(ks[3], (E, FF, H), dtype=jnp.float32) * s, 'b2': jnp.zeros((E, H), dtype=jnp.float32)}
    _L1_ffn_in = _L1_ffn_setup()

    def _L2_attn_setup():
        import jax, jax.numpy as jnp
        import numpy as np
        N_EMBD = 128
        BLOCK_SIZE = 256
        ATTN_SPAN = 32
        LN_EPS = 1e-05

        def _band_mask(T, span, dtype):
            ones = jnp.ones((T, T), dtype=dtype)
            return jnp.tril(ones, 0) * (1.0 - jnp.tril(ones, -span))

        def _layer_norm(h, w, b):
            mu = jnp.mean(h, axis=-1, keepdims=True)
            var = jnp.var(h, axis=-1, keepdims=True)
            return (h - mu) * jax.lax.rsqrt(var + LN_EPS) * w + b
        key = jax.random.key(seed)
        k_x, k_w, k_b, k_lw = jax.random.split(key, 4)
        B, T, C = (4, BLOCK_SIZE, N_EMBD)
        x = jax.random.normal(k_x, (B, T, C), dtype=jnp.float32)
        lim = 1.0 / np.sqrt(C)
        W_qkv = jax.random.uniform(k_w, (C, 3 * C), minval=-lim, maxval=lim, dtype=jnp.float32)
        b_qkv = jax.random.uniform(k_b, (3 * C,), minval=-lim, maxval=lim, dtype=jnp.float32)
        ln_w = jnp.ones((C,), dtype=jnp.float32)
        ln_b = jnp.zeros((C,), dtype=jnp.float32)
        return {'x': x, 'W_qkv': W_qkv, 'b_qkv': b_qkv, 'ln_w': ln_w, 'ln_b': ln_b}
    _L2_attn_in = _L2_attn_setup()

    def _L2_ffn_setup():
        import jax, jax.numpy as jnp
        import numpy as np
        IN_DIM = 128
        OUT_DIM = 128
        NUM_EXPERTS = 8
        TOP_K = 2
        key = jax.random.key(seed)
        ks = jax.random.split(key, 5)
        s = 1.0 / np.sqrt(IN_DIM)
        x = jax.random.normal(ks[0], (4, 256, IN_DIM), dtype=jnp.float32)
        Wg = jax.random.uniform(ks[1], (IN_DIM, NUM_EXPERTS), jnp.float32, -s, s)
        bg = jnp.zeros((NUM_EXPERTS,), jnp.float32)
        We = jax.random.uniform(ks[2], (NUM_EXPERTS, OUT_DIM, IN_DIM), jnp.float32, -s, s)
        be = jax.random.uniform(ks[3], (NUM_EXPERTS, OUT_DIM), jnp.float32, -s, s)
        return {'x': x, 'Wg': Wg, 'bg': bg, 'We': We, 'be': be}
    _L2_ffn_in = _L2_ffn_setup()

    def _L3_attn_setup():
        import jax, jax.numpy as jnp
        import numpy as np
        D_MODEL = 128
        D_STATE = 16
        D_CONV = 8
        EXPAND = 1
        D_INNER = EXPAND * D_MODEL
        DT_RANK = (D_MODEL + 15) // 16
        FFN_HID = 4 * D_MODEL

        def _layernorm(x, g, b, eps=1e-05):
            mu = jnp.mean(x, axis=-1, keepdims=True)
            var = jnp.var(x, axis=-1, keepdims=True)
            return (x - mu) * jax.lax.rsqrt(var + eps) * g + b

        def _mamba(x, in_proj_w, conv_w, conv_b, x_proj_w, dt_proj_w, dt_proj_b, A_log, D_param, out_proj_w):
            B, T, _ = x.shape
            xz = jnp.einsum('btd,ed->bte', x, in_proj_w)
            xin, z = jnp.split(xz, 2, axis=-1)
            xp = jnp.pad(xin, ((0, 0), (D_CONV - 1, 0), (0, 0)))
            xc = sum((xp[:, k:k + T, :] * conv_w[:, k] for k in range(D_CONV))) + conv_b
            xc = jax.nn.silu(xc)
            dbl = jnp.einsum('btd,ed->bte', xc, x_proj_w)
            dt = dbl[..., :DT_RANK]
            Bmat = dbl[..., DT_RANK:DT_RANK + D_STATE]
            Cmat = dbl[..., DT_RANK + D_STATE:]
            delta = jax.nn.softplus(jnp.einsum('btr,dr->btd', dt, dt_proj_w) + dt_proj_b)
            A = -jnp.exp(A_log)
            dA = jnp.exp(delta[..., None] * A)
            dBx = delta[..., None] * Bmat[:, :, None, :] * xc[..., None]

            def step(h, inp):
                dA_t, dBx_t, C_t = inp
                h = h * dA_t + dBx_t
                y = jnp.einsum('bdn,bn->bd', h, C_t)
                return (h, y)
            h0 = jnp.zeros((B, D_INNER, D_STATE), x.dtype)
            _, ys = jax.lax.scan(step, h0, (dA.transpose(1, 0, 2, 3), dBx.transpose(1, 0, 2, 3), Cmat.transpose(1, 0, 2)))
            y = ys.transpose(1, 0, 2) + xc * D_param
            y = y * jax.nn.silu(z)
            return jnp.einsum('btd,ed->bte', y, out_proj_w)
        key = jax.random.key(seed)
        ks = jax.random.split(key, 16)
        s = lambda *shape: 0.02
        x = jax.random.normal(ks[0], (2, 512, D_MODEL), dtype=jnp.float32)
        in_proj_w = jax.random.normal(ks[1], (2 * D_INNER, D_MODEL), dtype=jnp.float32) * 0.02
        conv_w = jax.random.normal(ks[2], (D_INNER, D_CONV), dtype=jnp.float32) * 0.1
        conv_b = jnp.zeros((D_INNER,), jnp.float32)
        x_proj_w = jax.random.normal(ks[3], (DT_RANK + 2 * D_STATE, D_INNER), dtype=jnp.float32) * 0.02
        dt_proj_w = jax.random.normal(ks[4], (D_INNER, DT_RANK), dtype=jnp.float32) * 0.02
        dt_proj_b = jax.random.uniform(ks[5], (D_INNER,), jnp.float32, -4.0, -2.0)
        A_log = jnp.log(jnp.tile(jnp.arange(1, D_STATE + 1, dtype=jnp.float32)[None, :], (D_INNER, 1)))
        D_param = jnp.ones((D_INNER,), jnp.float32)
        out_proj_w = jax.random.normal(ks[6], (D_MODEL, D_INNER), dtype=jnp.float32) * 0.02
        ln1_g = jnp.ones((D_MODEL,), jnp.float32)
        ln1_b = jnp.zeros((D_MODEL,), jnp.float32)
        ln2_g = jnp.ones((D_MODEL,), jnp.float32)
        ln2_b = jnp.zeros((D_MODEL,), jnp.float32)
        w1 = jax.random.normal(ks[7], (FFN_HID, D_MODEL), dtype=jnp.float32) * 0.02
        b1 = jnp.zeros((FFN_HID,), jnp.float32)
        w2 = jax.random.normal(ks[8], (D_MODEL, FFN_HID), dtype=jnp.float32) * 0.02
        b2 = jnp.zeros((D_MODEL,), jnp.float32)
        return dict(x=x, in_proj_w=in_proj_w, conv_w=conv_w, conv_b=conv_b, x_proj_w=x_proj_w, dt_proj_w=dt_proj_w, dt_proj_b=dt_proj_b, A_log=A_log, D_param=D_param, out_proj_w=out_proj_w, ln1_g=ln1_g, ln1_b=ln1_b, ln2_g=ln2_g, ln2_b=ln2_b, w1=w1, b1=b1, w2=w2, b2=b2)
    _L3_attn_in = _L3_attn_setup()

    def _L3_ffn_setup():
        import jax, jax.numpy as jnp
        import numpy as np
        DIM = 128
        DEPTH = 2
        HEADS = 8
        DIM_HEAD = 64
        WINDOW = 64
        INNER = HEADS * DIM_HEAD
        HID = int(DIM * 4 * 2 / 3)
        B, N = (2, 1024)
        QK_SCALE = 8.0

        def shift_token(t):
            t1, t2 = jnp.split(t, 2, axis=-1)
            t2 = jnp.pad(t2, ((0, 0), (1, 0), (0, 0)))[:, :-1]
            return jnp.concatenate([t1, t2], axis=-1)

        def l2norm(t):
            return t / jnp.clip(jnp.linalg.norm(t, axis=-1, keepdims=True), 1e-12)

        def rotate_half(x):
            x1, x2 = jnp.split(x, 2, axis=-1)
            return jnp.concatenate([-x2, x1], axis=-1)

        def rotary_xpos(q, k):
            n = q.shape[-2]
            half_idx = jnp.arange(0, DIM_HEAD, 2, dtype=jnp.float32)
            inv_freq = 1.0 / 10000.0 ** (half_idx / DIM_HEAD)
            t = jnp.arange(n, dtype=jnp.float32)
            freqs = t[:, None] * inv_freq[None, :]
            freqs = jnp.concatenate([freqs, freqs], axis=-1)
            base = (half_idx + 0.4 * DIM_HEAD) / (1.4 * DIM_HEAD)
            power = (t - n // 2) / float(WINDOW // 2)
            scale = base[None, :] ** power[:, None]
            scale = jnp.concatenate([scale, scale], axis=-1)
            cos, sin = (jnp.cos(freqs), jnp.sin(freqs))
            q = q * cos * scale + rotate_half(q) * sin * scale
            k = k * cos / scale + rotate_half(k) * sin / scale
            return (q, k)

        def local_attention(q, k, v):
            b, h, n, d = q.shape
            w = n // WINDOW
            bq = q.reshape(b, h, w, WINDOW, d) * QK_SCALE
            bk = k.reshape(b, h, w, WINDOW, d)
            bv = v.reshape(b, h, w, WINDOW, d)

            def look_around(t):
                p = jnp.pad(t, ((0, 0), (0, 0), (1, 0), (0, 0), (0, 0)))
                return jnp.concatenate([p[:, :, :w], p[:, :, 1:]], axis=3)
            bk, bv = (look_around(bk), look_around(bv))
            bt = jnp.arange(n).reshape(w, WINDOW)
            btp = jnp.pad(bt, ((1, 0), (0, 0)), constant_values=-1)
            btk = jnp.concatenate([btp[:w], btp[1:]], axis=1)
            sim = jnp.einsum('bhwid,bhwjd->bhwij', bq, bk)
            i = bt[:, :, None]
            j = btk[:, None, :]
            mask = (i < j) | (i > j + WINDOW) | (j == -1)
            sim = jnp.where(mask, -jnp.finfo(sim.dtype).max, sim)
            attn = jax.nn.softmax(sim, axis=-1)
            out = jnp.einsum('bhwij,bhwjd->bhwid', attn, bv)
            return out.reshape(b, h, n, d)

        def _layer(x, wqkv, qs, ksc, wo, lg, lb, w1, b1, w2, b2):
            b, n, _ = x.shape
            h = shift_token(x)
            qkv = h @ wqkv
            q, k, v = jnp.split(qkv, 3, axis=-1)
            to_heads = lambda t: t.reshape(b, n, HEADS, DIM_HEAD).transpose(0, 2, 1, 3)
            q, k, v = (to_heads(q), to_heads(k), to_heads(v))
            q = l2norm(q) * qs
            k = l2norm(k) * ksc
            q, k = rotary_xpos(q, k)
            o = local_attention(q, k, v)
            o = o.transpose(0, 2, 1, 3).reshape(b, n, INNER)
            x = x + o @ wo
            h = shift_token(x)
            mu = h.mean(-1, keepdims=True)
            var = h.var(-1, keepdims=True)
            h = (h - mu) / jnp.sqrt(var + 1e-05) * lg + lb
            h = h @ w1 + b1
            a, g = jnp.split(h, 2, axis=-1)
            h = a * jax.nn.gelu(g, approximate=False)
            x = x + h @ w2 + b2
            return x
        key = jax.random.key(seed)
        ks = jax.random.split(key, 6)
        return {'x': jax.random.normal(ks[0], (B, N, DIM), jnp.float32), 'wqkv': jax.random.normal(ks[1], (DEPTH, DIM, 3 * INNER), jnp.float32) * 0.02, 'q_scale': jnp.ones((DEPTH, DIM_HEAD), jnp.float32), 'k_scale': jnp.ones((DEPTH, DIM_HEAD), jnp.float32), 'wo': jax.random.normal(ks[2], (DEPTH, INNER, DIM), jnp.float32) * 0.02, 'ln_g': jnp.ones((DEPTH, DIM), jnp.float32), 'ln_b': jnp.zeros((DEPTH, DIM), jnp.float32), 'w1': jax.random.normal(ks[3], (DEPTH, DIM, 2 * HID), jnp.float32) * 0.02, 'b1': jnp.zeros((DEPTH, 2 * HID), jnp.float32), 'w2': jax.random.normal(ks[4], (DEPTH, HID, DIM), jnp.float32) * 0.02, 'b2': jnp.zeros((DEPTH, DIM), jnp.float32)}
    _L3_ffn_in = _L3_ffn_setup()
    _d = {'L0_attn_x': _L0_attn_in['x'], 'L0_attn_Wq': _L0_attn_in['Wq'], 'L0_attn_bq': _L0_attn_in['bq'], 'L0_attn_Wk': _L0_attn_in['Wk'], 'L0_attn_bk': _L0_attn_in['bk'], 'L0_attn_Wv': _L0_attn_in['Wv'], 'L0_attn_bv': _L0_attn_in['bv'], 'L0_attn_Wo': _L0_attn_in['Wo'], 'L0_attn_bo': _L0_attn_in['bo'], 'L0_attn_head_mask': _L0_attn_in['head_mask'], 'L0_ffn_w_shared_in': _L0_ffn_in['w_shared_in'], 'L0_ffn_w_shared_out': _L0_ffn_in['w_shared_out'], 'L0_ffn_w1_shared': _L0_ffn_in['w1_shared'], 'L0_ffn_w2': _L0_ffn_in['w2'], 'L0_ffn_w_gate': _L0_ffn_in['w_gate'], 'L0_ffn_gate_bias': _L0_ffn_in['gate_bias'], 'L1_attn_fwd_in_proj': _L1_attn_in['fwd_in_proj'], 'L1_attn_fwd_conv_w': _L1_attn_in['fwd_conv_w'], 'L1_attn_fwd_conv_b': _L1_attn_in['fwd_conv_b'], 'L1_attn_fwd_x_proj': _L1_attn_in['fwd_x_proj'], 'L1_attn_fwd_dt_w': _L1_attn_in['fwd_dt_w'], 'L1_attn_fwd_dt_b': _L1_attn_in['fwd_dt_b'], 'L1_attn_fwd_A_log': _L1_attn_in['fwd_A_log'], 'L1_attn_fwd_D': _L1_attn_in['fwd_D'], 'L1_attn_fwd_out_proj': _L1_attn_in['fwd_out_proj'], 'L1_attn_bwd_in_proj': _L1_attn_in['bwd_in_proj'], 'L1_attn_bwd_conv_w': _L1_attn_in['bwd_conv_w'], 'L1_attn_bwd_conv_b': _L1_attn_in['bwd_conv_b'], 'L1_attn_bwd_x_proj': _L1_attn_in['bwd_x_proj'], 'L1_attn_bwd_dt_w': _L1_attn_in['bwd_dt_w'], 'L1_attn_bwd_dt_b': _L1_attn_in['bwd_dt_b'], 'L1_attn_bwd_A_log': _L1_attn_in['bwd_A_log'], 'L1_attn_bwd_D': _L1_attn_in['bwd_D'], 'L1_attn_bwd_out_proj': _L1_attn_in['bwd_out_proj'], 'L1_attn_merge_w': _L1_attn_in['merge_w'], 'L1_ffn_Wg': _L1_ffn_in['Wg'], 'L1_ffn_W1': _L1_ffn_in['W1'], 'L1_ffn_b1': _L1_ffn_in['b1'], 'L1_ffn_W2': _L1_ffn_in['W2'], 'L1_ffn_b2': _L1_ffn_in['b2'], 'L2_attn_W_qkv': _L2_attn_in['W_qkv'], 'L2_attn_b_qkv': _L2_attn_in['b_qkv'], 'L2_attn_ln_w': _L2_attn_in['ln_w'], 'L2_attn_ln_b': _L2_attn_in['ln_b'], 'L2_ffn_Wg': _L2_ffn_in['Wg'], 'L2_ffn_bg': _L2_ffn_in['bg'], 'L2_ffn_We': _L2_ffn_in['We'], 'L2_ffn_be': _L2_ffn_in['be'], 'L3_attn_in_proj_w': _L3_attn_in['in_proj_w'], 'L3_attn_conv_w': _L3_attn_in['conv_w'], 'L3_attn_conv_b': _L3_attn_in['conv_b'], 'L3_attn_x_proj_w': _L3_attn_in['x_proj_w'], 'L3_attn_dt_proj_w': _L3_attn_in['dt_proj_w'], 'L3_attn_dt_proj_b': _L3_attn_in['dt_proj_b'], 'L3_attn_A_log': _L3_attn_in['A_log'], 'L3_attn_D_param': _L3_attn_in['D_param'], 'L3_attn_out_proj_w': _L3_attn_in['out_proj_w'], 'L3_attn_ln1_g': _L3_attn_in['ln1_g'], 'L3_attn_ln1_b': _L3_attn_in['ln1_b'], 'L3_attn_ln2_g': _L3_attn_in['ln2_g'], 'L3_attn_ln2_b': _L3_attn_in['ln2_b'], 'L3_attn_w1': _L3_attn_in['w1'], 'L3_attn_b1': _L3_attn_in['b1'], 'L3_attn_w2': _L3_attn_in['w2'], 'L3_attn_b2': _L3_attn_in['b2'], 'L3_ffn_wqkv': _L3_ffn_in['wqkv'], 'L3_ffn_q_scale': _L3_ffn_in['q_scale'], 'L3_ffn_k_scale': _L3_ffn_in['k_scale'], 'L3_ffn_wo': _L3_ffn_in['wo'], 'L3_ffn_ln_g': _L3_ffn_in['ln_g'], 'L3_ffn_ln_b': _L3_ffn_in['ln_b'], 'L3_ffn_w1': _L3_ffn_in['w1'], 'L3_ffn_b1': _L3_ffn_in['b1'], 'L3_ffn_w2': _L3_ffn_in['w2'], 'L3_ffn_b2': _L3_ffn_in['b2']}
    _x0 = _d['L0_attn_x']
    _d['L0_attn_x'] = jax.random.normal(jax.random.fold_in(jax.random.key(seed), 1), (8, 512, 128), dtype=_x0.dtype)
    del _x0
    return _d

def reference(L0_attn_x, L0_attn_Wq, L0_attn_bq, L0_attn_Wk, L0_attn_bk, L0_attn_Wv, L0_attn_bv, L0_attn_Wo, L0_attn_bo, L0_attn_head_mask, L0_ffn_w_shared_in, L0_ffn_w_shared_out, L0_ffn_w1_shared, L0_ffn_w2, L0_ffn_w_gate, L0_ffn_gate_bias, L1_attn_fwd_in_proj, L1_attn_fwd_conv_w, L1_attn_fwd_conv_b, L1_attn_fwd_x_proj, L1_attn_fwd_dt_w, L1_attn_fwd_dt_b, L1_attn_fwd_A_log, L1_attn_fwd_D, L1_attn_fwd_out_proj, L1_attn_bwd_in_proj, L1_attn_bwd_conv_w, L1_attn_bwd_conv_b, L1_attn_bwd_x_proj, L1_attn_bwd_dt_w, L1_attn_bwd_dt_b, L1_attn_bwd_A_log, L1_attn_bwd_D, L1_attn_bwd_out_proj, L1_attn_merge_w, L1_ffn_Wg, L1_ffn_W1, L1_ffn_b1, L1_ffn_W2, L1_ffn_b2, L2_attn_W_qkv, L2_attn_b_qkv, L2_attn_ln_w, L2_attn_ln_b, L2_ffn_Wg, L2_ffn_bg, L2_ffn_We, L2_ffn_be, L3_attn_in_proj_w, L3_attn_conv_w, L3_attn_conv_b, L3_attn_x_proj_w, L3_attn_dt_proj_w, L3_attn_dt_proj_b, L3_attn_A_log, L3_attn_D_param, L3_attn_out_proj_w, L3_attn_ln1_g, L3_attn_ln1_b, L3_attn_ln2_g, L3_attn_ln2_b, L3_attn_w1, L3_attn_b1, L3_attn_w2, L3_attn_b2, L3_ffn_wqkv, L3_ffn_q_scale, L3_ffn_k_scale, L3_ffn_wo, L3_ffn_ln_g, L3_ffn_ln_b, L3_ffn_w1, L3_ffn_b1, L3_ffn_w2, L3_ffn_b2):

    def _L0_attn_ref(x, Wq, bq, Wk, bk, Wv, bv, Wo, bo, head_mask):
        import jax, jax.numpy as jnp
        import numpy as np
        HIDDEN = 128
        HEADS = 16
        HEAD_DIM = HIDDEN // HEADS
        B, S = (4, 256)
        b, s, _ = x.shape
        q = (x @ Wq.T + bq).reshape(b, s, HEADS, HEAD_DIM)
        k = (x @ Wk.T + bk).reshape(b, s, HEADS, HEAD_DIM)
        v = (x @ Wv.T + bv).reshape(b, s, HEADS, HEAD_DIM)
        attn = jnp.einsum('bqhd,bkhd->bhqk', q, k) / np.sqrt(HEAD_DIM).astype(np.float32)
        attn = jax.nn.softmax(attn, axis=-1)
        attn = attn * head_mask[None, :, None, None]
        out = jnp.einsum('bhqk,bkhd->bqhd', attn, v).reshape(b, s, HIDDEN)
        return out @ Wo.T + bo

    def _L0_ffn_ref(x, w_shared_in, w_shared_out, w1_shared, w2, w_gate, gate_bias):
        import jax, jax.numpy as jnp
        import numpy as np
        B, T, C, H, E, K = (4, 128, 128, 128, 8, 2)

        def _swiglu(x):
            a, b = jnp.split(x, 2, axis=-1)
            return jax.nn.silu(a) * b
        Bx, Tx, Cx = x.shape
        S = Bx * Tx
        fx = x.reshape(S, Cx)
        shared_out = _swiglu(fx @ w_shared_in) @ w_shared_out
        logits = fx @ w_gate + gate_bias
        probs = jax.nn.softmax(logits, axis=-1)
        top_val, top_idx = jax.lax.top_k(probs, K)
        wdense = jnp.zeros((S, E), probs.dtype).at[jnp.arange(S)[:, None], top_idx].add(top_val)
        hid = _swiglu(fx @ w1_shared)
        routed_out = jnp.zeros_like(shared_out)
        for e in range(E):
            routed_out = routed_out + wdense[:, e:e + 1] * (hid @ w2[e])
        return (shared_out + routed_out).reshape(Bx, Tx, Cx)

    def _L1_attn_ref(x, fwd_in_proj, fwd_conv_w, fwd_conv_b, fwd_x_proj, fwd_dt_w, fwd_dt_b, fwd_A_log, fwd_D, fwd_out_proj, bwd_in_proj, bwd_conv_w, bwd_conv_b, bwd_x_proj, bwd_dt_w, bwd_dt_b, bwd_A_log, bwd_D, bwd_out_proj, merge_w):
        import jax, jax.numpy as jnp
        import numpy as np
        D_MODEL = 128
        D_STATE = 16
        D_CONV = 4
        EXPAND = 2
        D_INNER = EXPAND * D_MODEL
        DT_RANK = D_MODEL // 16
        BSZ = 2
        SEQ = 128

        def _silu(x):
            return x * jax.nn.sigmoid(x)

        def _mamba(x, in_proj, conv_w, conv_b, x_proj, dt_w, dt_b, A_log, Dp, out_proj):
            Bb, Ll, _ = x.shape
            xz = jnp.einsum('bld,ed->ble', x, in_proj)
            xi, z = jnp.split(xz, 2, axis=-1)
            xp = jnp.pad(xi, ((0, 0), (D_CONV - 1, 0), (0, 0)))
            xc = conv_b + sum((conv_w[:, k] * xp[:, k:k + Ll, :] for k in range(D_CONV)))
            xc = _silu(xc)
            dbl = jnp.einsum('ble,fe->blf', xc, x_proj)
            dt, Bm, Cm = jnp.split(dbl, [DT_RANK, DT_RANK + D_STATE], axis=-1)
            delta = jax.nn.softplus(jnp.einsum('blr,er->ble', dt, dt_w) + dt_b)
            A = -jnp.exp(A_log)
            dA = jnp.exp(delta[..., None] * A)
            dBu = (delta * xc)[..., None] * Bm[:, :, None, :]

            def step(h, t):
                dA_t, dBu_t, C_t = t
                h = dA_t * h + dBu_t
                return (h, jnp.einsum('ben,bn->be', h, C_t))
            h0 = jnp.zeros((Bb, D_INNER, D_STATE), x.dtype)
            _, ys = jax.lax.scan(step, h0, (dA.transpose(1, 0, 2, 3), dBu.transpose(1, 0, 2, 3), Cm.transpose(1, 0, 2)))
            y = ys.transpose(1, 0, 2) + xc * Dp
            y = y * _silu(z)
            return jnp.einsum('ble,de->bld', y, out_proj)
        f = _mamba(x, fwd_in_proj, fwd_conv_w, fwd_conv_b, fwd_x_proj, fwd_dt_w, fwd_dt_b, fwd_A_log, fwd_D, fwd_out_proj)
        b = _mamba(jnp.flip(x, 1), bwd_in_proj, bwd_conv_w, bwd_conv_b, bwd_x_proj, bwd_dt_w, bwd_dt_b, bwd_A_log, bwd_D, bwd_out_proj)
        b = jnp.flip(b, 1)
        return jnp.einsum('blf,df->bld', jnp.concatenate([f, b], axis=-1), merge_w)

    def _L1_ffn_ref(x, Wg, W1, b1, W2, b2):
        import jax, jax.numpy as jnp
        import numpy as np
        B, L, H, E, FF, C = (4, 256, 128, 8, 512, 2)
        b, l, h = x.shape
        e = Wg.shape[1]
        n = b * l
        k = min(max(int(n * C / e), 1), n)
        xt = x.reshape(n, h)
        S = jax.nn.sigmoid(xt @ Wg).T
        G, I = jax.lax.top_k(S, k)
        ex = xt[I]
        hid = jax.nn.gelu(jnp.einsum('ekh,ehf->ekf', ex, W1) + b1[:, None, :], approximate=False)
        out = (jnp.einsum('ekf,efh->ekh', hid, W2) + b2[:, None, :]) * G[..., None]
        new_x = jnp.zeros_like(xt).at[I.reshape(-1)].add(out.reshape(-1, h))
        return new_x.reshape(b, l, h)

    def _L2_attn_ref(x, W_qkv, b_qkv, ln_w, ln_b):
        import jax, jax.numpy as jnp
        import numpy as np
        N_EMBD = 128
        BLOCK_SIZE = 256
        ATTN_SPAN = 32
        LN_EPS = 1e-05

        def _band_mask(T, span, dtype):
            ones = jnp.ones((T, T), dtype=dtype)
            return jnp.tril(ones, 0) * (1.0 - jnp.tril(ones, -span))

        def _layer_norm(h, w, b):
            mu = jnp.mean(h, axis=-1, keepdims=True)
            var = jnp.var(h, axis=-1, keepdims=True)
            return (h - mu) * jax.lax.rsqrt(var + LN_EPS) * w + b
        B, T, C = x.shape
        qkv = x @ W_qkv + b_qkv
        q, k, v = jnp.split(qkv, 3, axis=-1)
        scale = np.sqrt(C * ATTN_SPAN).astype(np.float32)
        scores = jnp.einsum('bid,bjd->bij', q, k) / scale
        scores = scores * _band_mask(T, ATTN_SPAN, x.dtype)[None, :, :]
        out = jnp.einsum('bij,bjd->bid', scores, v)
        return _layer_norm(out, ln_w, ln_b)

    def _L2_ffn_ref(x, Wg, bg, We, be):
        import jax, jax.numpy as jnp
        import numpy as np
        IN_DIM = 128
        OUT_DIM = 128
        NUM_EXPERTS = 8
        TOP_K = 2
        gate = jax.nn.softmax(x @ Wg + bg, axis=-1)
        topk_vals, topk_idx = jax.lax.top_k(gate, TOP_K)
        onehot = jax.nn.one_hot(topk_idx, NUM_EXPERTS, dtype=gate.dtype)
        gate_sparse = jnp.einsum('bsk,bske->bse', topk_vals, onehot)
        gate_sparse = gate_sparse / jnp.sum(gate_sparse, axis=-1, keepdims=True)
        y = jnp.einsum('bsi,eoi->bseo', x, We) + be[None, None, :, :].transpose(0, 1, 2, 3)
        out = jnp.einsum('bseo,bse->bso', y, gate_sparse)
        return out

    def _L3_attn_ref(x, in_proj_w, conv_w, conv_b, x_proj_w, dt_proj_w, dt_proj_b, A_log, D_param, out_proj_w, ln1_g, ln1_b, ln2_g, ln2_b, w1, b1, w2, b2):
        import jax, jax.numpy as jnp
        import numpy as np
        D_MODEL = 128
        D_STATE = 16
        D_CONV = 8
        EXPAND = 1
        D_INNER = EXPAND * D_MODEL
        DT_RANK = (D_MODEL + 15) // 16
        FFN_HID = 4 * D_MODEL

        def _layernorm(x, g, b, eps=1e-05):
            mu = jnp.mean(x, axis=-1, keepdims=True)
            var = jnp.var(x, axis=-1, keepdims=True)
            return (x - mu) * jax.lax.rsqrt(var + eps) * g + b

        def _mamba(x, in_proj_w, conv_w, conv_b, x_proj_w, dt_proj_w, dt_proj_b, A_log, D_param, out_proj_w):
            B, T, _ = x.shape
            xz = jnp.einsum('btd,ed->bte', x, in_proj_w)
            xin, z = jnp.split(xz, 2, axis=-1)
            xp = jnp.pad(xin, ((0, 0), (D_CONV - 1, 0), (0, 0)))
            xc = sum((xp[:, k:k + T, :] * conv_w[:, k] for k in range(D_CONV))) + conv_b
            xc = jax.nn.silu(xc)
            dbl = jnp.einsum('btd,ed->bte', xc, x_proj_w)
            dt = dbl[..., :DT_RANK]
            Bmat = dbl[..., DT_RANK:DT_RANK + D_STATE]
            Cmat = dbl[..., DT_RANK + D_STATE:]
            delta = jax.nn.softplus(jnp.einsum('btr,dr->btd', dt, dt_proj_w) + dt_proj_b)
            A = -jnp.exp(A_log)
            dA = jnp.exp(delta[..., None] * A)
            dBx = delta[..., None] * Bmat[:, :, None, :] * xc[..., None]

            def step(h, inp):
                dA_t, dBx_t, C_t = inp
                h = h * dA_t + dBx_t
                y = jnp.einsum('bdn,bn->bd', h, C_t)
                return (h, y)
            h0 = jnp.zeros((B, D_INNER, D_STATE), x.dtype)
            _, ys = jax.lax.scan(step, h0, (dA.transpose(1, 0, 2, 3), dBx.transpose(1, 0, 2, 3), Cmat.transpose(1, 0, 2)))
            y = ys.transpose(1, 0, 2) + xc * D_param
            y = y * jax.nn.silu(z)
            return jnp.einsum('btd,ed->bte', y, out_proj_w)
        x = x + _mamba(_layernorm(x, ln1_g, ln1_b), in_proj_w, conv_w, conv_b, x_proj_w, dt_proj_w, dt_proj_b, A_log, D_param, out_proj_w)
        h = _layernorm(x, ln2_g, ln2_b)
        h = jax.nn.relu(jnp.einsum('btd,hd->bth', h, w1) + b1)
        x = x + jnp.einsum('bth,dh->btd', h, w2) + b2
        return x

    def _L3_ffn_ref(x, wqkv, q_scale, k_scale, wo, ln_g, ln_b, w1, b1, w2, b2):
        import jax, jax.numpy as jnp
        import numpy as np
        DIM = 128
        DEPTH = 2
        HEADS = 8
        DIM_HEAD = 64
        WINDOW = 64
        INNER = HEADS * DIM_HEAD
        HID = int(DIM * 4 * 2 / 3)
        B, N = (2, 1024)
        QK_SCALE = 8.0

        def shift_token(t):
            t1, t2 = jnp.split(t, 2, axis=-1)
            t2 = jnp.pad(t2, ((0, 0), (1, 0), (0, 0)))[:, :-1]
            return jnp.concatenate([t1, t2], axis=-1)

        def l2norm(t):
            return t / jnp.clip(jnp.linalg.norm(t, axis=-1, keepdims=True), 1e-12)

        def rotate_half(x):
            x1, x2 = jnp.split(x, 2, axis=-1)
            return jnp.concatenate([-x2, x1], axis=-1)

        def rotary_xpos(q, k):
            n = q.shape[-2]
            half_idx = jnp.arange(0, DIM_HEAD, 2, dtype=jnp.float32)
            inv_freq = 1.0 / 10000.0 ** (half_idx / DIM_HEAD)
            t = jnp.arange(n, dtype=jnp.float32)
            freqs = t[:, None] * inv_freq[None, :]
            freqs = jnp.concatenate([freqs, freqs], axis=-1)
            base = (half_idx + 0.4 * DIM_HEAD) / (1.4 * DIM_HEAD)
            power = (t - n // 2) / float(WINDOW // 2)
            scale = base[None, :] ** power[:, None]
            scale = jnp.concatenate([scale, scale], axis=-1)
            cos, sin = (jnp.cos(freqs), jnp.sin(freqs))
            q = q * cos * scale + rotate_half(q) * sin * scale
            k = k * cos / scale + rotate_half(k) * sin / scale
            return (q, k)

        def local_attention(q, k, v):
            b, h, n, d = q.shape
            w = n // WINDOW
            bq = q.reshape(b, h, w, WINDOW, d) * QK_SCALE
            bk = k.reshape(b, h, w, WINDOW, d)
            bv = v.reshape(b, h, w, WINDOW, d)

            def look_around(t):
                p = jnp.pad(t, ((0, 0), (0, 0), (1, 0), (0, 0), (0, 0)))
                return jnp.concatenate([p[:, :, :w], p[:, :, 1:]], axis=3)
            bk, bv = (look_around(bk), look_around(bv))
            bt = jnp.arange(n).reshape(w, WINDOW)
            btp = jnp.pad(bt, ((1, 0), (0, 0)), constant_values=-1)
            btk = jnp.concatenate([btp[:w], btp[1:]], axis=1)
            sim = jnp.einsum('bhwid,bhwjd->bhwij', bq, bk)
            i = bt[:, :, None]
            j = btk[:, None, :]
            mask = (i < j) | (i > j + WINDOW) | (j == -1)
            sim = jnp.where(mask, -jnp.finfo(sim.dtype).max, sim)
            attn = jax.nn.softmax(sim, axis=-1)
            out = jnp.einsum('bhwij,bhwjd->bhwid', attn, bv)
            return out.reshape(b, h, n, d)

        def _layer(x, wqkv, qs, ksc, wo, lg, lb, w1, b1, w2, b2):
            b, n, _ = x.shape
            h = shift_token(x)
            qkv = h @ wqkv
            q, k, v = jnp.split(qkv, 3, axis=-1)
            to_heads = lambda t: t.reshape(b, n, HEADS, DIM_HEAD).transpose(0, 2, 1, 3)
            q, k, v = (to_heads(q), to_heads(k), to_heads(v))
            q = l2norm(q) * qs
            k = l2norm(k) * ksc
            q, k = rotary_xpos(q, k)
            o = local_attention(q, k, v)
            o = o.transpose(0, 2, 1, 3).reshape(b, n, INNER)
            x = x + o @ wo
            h = shift_token(x)
            mu = h.mean(-1, keepdims=True)
            var = h.var(-1, keepdims=True)
            h = (h - mu) / jnp.sqrt(var + 1e-05) * lg + lb
            h = h @ w1 + b1
            a, g = jnp.split(h, 2, axis=-1)
            h = a * jax.nn.gelu(g, approximate=False)
            x = x + h @ w2 + b2
            return x
        for l in range(DEPTH):
            x = _layer(x, wqkv[l], q_scale[l], k_scale[l], wo[l], ln_g[l], ln_b[l], w1[l], b1[l], w2[l], b2[l])
        return x
    x = L0_attn_x
    xn = _layernorm(x, axis=-1)
    s = _L0_attn_ref(xn, L0_attn_Wq, L0_attn_bq, L0_attn_Wk, L0_attn_bk, L0_attn_Wv, L0_attn_bv, L0_attn_Wo, L0_attn_bo, L0_attn_head_mask)
    g = _silu(_L0_ffn_ref(xn, L0_ffn_w_shared_in, L0_ffn_w_shared_out, L0_ffn_w1_shared, L0_ffn_w2, L0_ffn_w_gate, L0_ffn_gate_bias))
    x = x + s * g
    xn = _layernorm(x, axis=-1)
    s = _L1_attn_ref(xn, L1_attn_fwd_in_proj, L1_attn_fwd_conv_w, L1_attn_fwd_conv_b, L1_attn_fwd_x_proj, L1_attn_fwd_dt_w, L1_attn_fwd_dt_b, L1_attn_fwd_A_log, L1_attn_fwd_D, L1_attn_fwd_out_proj, L1_attn_bwd_in_proj, L1_attn_bwd_conv_w, L1_attn_bwd_conv_b, L1_attn_bwd_x_proj, L1_attn_bwd_dt_w, L1_attn_bwd_dt_b, L1_attn_bwd_A_log, L1_attn_bwd_D, L1_attn_bwd_out_proj, L1_attn_merge_w)
    g = _silu(_L1_ffn_ref(xn, L1_ffn_Wg, L1_ffn_W1, L1_ffn_b1, L1_ffn_W2, L1_ffn_b2))
    x = x + s * g
    xn = _layernorm(x, axis=-1)
    s = _L2_attn_ref(xn, L2_attn_W_qkv, L2_attn_b_qkv, L2_attn_ln_w, L2_attn_ln_b)
    g = _silu(_L2_ffn_ref(xn, L2_ffn_Wg, L2_ffn_bg, L2_ffn_We, L2_ffn_be))
    x = x + s * g
    xn = _layernorm(x, axis=-1)
    s = _L3_attn_ref(xn, L3_attn_in_proj_w, L3_attn_conv_w, L3_attn_conv_b, L3_attn_x_proj_w, L3_attn_dt_proj_w, L3_attn_dt_proj_b, L3_attn_A_log, L3_attn_D_param, L3_attn_out_proj_w, L3_attn_ln1_g, L3_attn_ln1_b, L3_attn_ln2_g, L3_attn_ln2_b, L3_attn_w1, L3_attn_b1, L3_attn_w2, L3_attn_b2)
    g = _silu(_L3_ffn_ref(xn, L3_ffn_wqkv, L3_ffn_q_scale, L3_ffn_k_scale, L3_ffn_wo, L3_ffn_ln_g, L3_ffn_ln_b, L3_ffn_w1, L3_ffn_b1, L3_ffn_w2, L3_ffn_b2))
    x = x + s * g
    return x

_drawn_inputs = setup_inputs


def setup_inputs(seed=0):
    import zlib

    import numpy as np

    out = dict(_drawn_inputs(seed))
    spreads = {'L0_attn_bq': (0.0, 0.1),
     'L0_attn_bk': (0.0, 0.1),
     'L0_attn_bv': (0.0, 0.1),
     'L0_attn_bo': (0.0, 0.1),
     'L0_ffn_gate_bias': (0.0, 0.1),
     'L1_attn_fwd_conv_b': (0.0, 0.1),
     'L1_attn_fwd_D': (1.0, 0.2),
     'L1_attn_bwd_conv_b': (0.0, 0.1),
     'L1_attn_bwd_D': (1.0, 0.2),
     'L1_ffn_b1': (0.0, 0.1),
     'L1_ffn_b2': (0.0, 0.1),
     'L2_attn_ln_w': (1.0, 0.2),
     'L2_attn_ln_b': (0.0, 0.1),
     'L2_ffn_bg': (0.0, 0.1),
     'L3_attn_conv_b': (0.0, 0.1),
     'L3_attn_D_param': (1.0, 0.2),
     'L3_attn_ln1_g': (1.0, 0.2),
     'L3_attn_ln1_b': (0.0, 0.1),
     'L3_attn_ln2_g': (1.0, 0.2),
     'L3_attn_ln2_b': (0.0, 0.1),
     'L3_attn_b1': (0.0, 0.1),
     'L3_attn_b2': (0.0, 0.1),
     'L3_ffn_q_scale': (1.0, 0.2),
     'L3_ffn_k_scale': (1.0, 0.2),
     'L3_ffn_ln_g': (1.0, 0.2),
     'L3_ffn_ln_b': (0.0, 0.1),
     'L3_ffn_b1': (0.0, 0.1),
     'L3_ffn_b2': (0.0, 0.1)}
    factors = {}
    for name, (base, spread) in spreads.items():
        noise = np.random.default_rng([zlib.crc32(name.encode()), seed]).standard_normal(out[name].shape)
        drawn = base * np.exp(spread * noise) if base else spread * noise
        out[name] = jnp.asarray(drawn.astype(out[name].dtype))
    for name, factor in factors.items():
        out[name] = (out[name] * factor).astype(out[name].dtype)
    return out
```

```python
from contextlib import ExitStack

import concourse.bass as bass
import concourse.mybir as mybir
import numpy as np

F32 = mybir.dt.float32
BF16 = mybir.dt.bfloat16
I32 = mybir.dt.int32
ALU = mybir.AluOpType
ACT = mybir.ActivationFunctionType
AX = mybir.AxisListType

P = 128
SEQS, SEQ = 8, 512
TOKENS = SEQS * SEQ
BLOCKS = SEQ // P
EXPERTS = 8
LN_EPS = 1e-5
SILU, GELU = ACT.Silu, ACT.Gelu


class Engine:

    def __init__(self, queue, sem, serial=False):
        self.queue, self.sem, self.count, self.reached, self.serial = queue, sem, 0, {}, serial

    def wait(self, *marks):
        for mark in marks:
            if mark is None:
                continue
            if isinstance(mark, list):
                self.wait(*mark)
                continue
            sem, value = mark
            if self.reached.get(id(sem), 0) < value:
                self.queue.wait_ge(sem, value)
                self.reached[id(sem)] = value

    def do(self, after, build):
        self.wait(*after)
        if self.serial and self.count:
            self.wait(self.last())
        build(self.queue).then_inc(self.sem, 1)
        self.count += 1
        return self.sem, self.count

    def last(self):
        return self.sem, self.count


class Transfers:

    def __init__(self, sem):
        self.sem, self.count = sem, 0

    def start(self, engine, out, in_, after=()):
        engine.wait(*after)
        engine.queue.dma_start(out, in_).then_inc(self.sem, 16)
        self.count += 16
        return self.sem, self.count


def weave(*runs):
    runs = list(runs)
    while runs:
        for run in list(runs):
            if next(run, "over") == "over":
                runs.remove(run)


def in_flight(make, count, width, lead=1):
    active, started, turn = [], 0, 0
    while active or started < count:
        if started < count and len(active) < width and (not active or turn >= lead):
            active.append(make(started, started % width))
            started, turn = started + 1, 0
        for run in list(active):
            if next(run, "over") == "over":
                active.remove(run)
        turn += 1
        yield


class Chip:

    def __init__(self, nc, ctx):
        self.nc, self.ctx, self.prefix = nc, ctx, ""
        self.names = {}
        self.pe = Engine(nc.tensor, self.sem("pe_steps"))
        self.act = Engine(nc.scalar, self.sem("act_steps"))
        self.dve = Engine(nc.vector, self.sem("dve_steps"))
        self.pool = Engine(nc.gpsimd, self.sem("pool_steps"), serial=True)
        self.sync = Engine(nc.sync, self.sem("sync_steps"))
        self.psum = ctx.enter_context(nc.psum_tensor("psum", [P, 8, SEQ], F32))
        self.emptied = [None] * 8
        self.steps = {}

    def sem(self, name):
        return self.ctx.enter_context(self.nc.semaphore(self.prefix + name))

    def buffer(self, ctx, name, shape, dtype=F32):
        name = self.prefix + name
        self.names[name] = count = self.names.get(name, 0) + 1
        return ctx.enter_context(self.nc.sbuf_tensor(f"{name}_{count}" if count > 1 else name, shape, dtype))

    def product(self, out, pairs, after, stop=True, start=True):
        self.pe.wait(*after)
        for i, (lhs_t, rhs) in enumerate(pairs[:-1]):
            self.pe.queue.matmul(out, lhs_t, rhs, start=start and i == 0, stop=False)
        lhs_t, rhs = pairs[-1]
        return self.pe.do([], lambda e: e.matmul(out, lhs_t, rhs, start=start and len(pairs) == 1, stop=stop))

    def barrier(self):
        engines = [self.pe, self.act, self.dve, self.pool]
        marks = [e.last() for e in engines if e.count]
        for e in engines + [self.sync]:
            e.wait(*marks)
        self.emptied = [None] * 8
        self.steps = {}


class Weights:

    def __init__(self, c, name, dram, place):
        self.c, self.name, self.dram, self.place = c, name, dram, place

    def load(self, ctx):
        tile = self.c.buffer(ctx, self.name, list(self.dram.shape))
        ready = Transfers(self.c.sem(self.name + "_loaded")).start(self.c.sync, tile[:, :], self.dram)
        return {name: tile[0:rows, at:at + cols] for name, (at, rows, cols) in self.place.items()}, ready


def constants(c):
    pool, buf = c.pool, lambda n, s, d=F32: c.buffer(c.ctx, n, s, d)
    c.ident = buf("ident", [P, P])
    c.ident16 = buf("ident16", [P, P], BF16)
    c.mean_of = buf("mean_of", [P, P])
    c.eps = buf("eps", [P, 1])
    zero = pool.do([], lambda e: e.memset(c.ident[:, :], 0.0))
    one = pool.do([zero], lambda e: e.affine_select(
        out=c.ident[:, :], in_=c.ident[:, :], compare_op=ALU.not_equal, fill=1.0, base=0,
        pattern=[[-1, P]], channel_multiplier=1))
    pool.do([one], lambda e: e.tensor_copy(c.ident16[:, :], c.ident[:, :]))
    pool.do([], lambda e: e.memset(c.mean_of[:, :], 1.0 / P))
    c.constants_ready = pool.do([], lambda e: e.memset(c.eps[:, :], LN_EPS))


def norm_buffers(c, ctx, slots):
    return [{"written": f"norm_written{s}", "centred": c.buffer(ctx, f"norm_centred{s}", [P, SEQ]),
             "square": c.buffer(ctx, f"norm_square{s}", [P, SEQ]),
             "scale": c.buffer(ctx, f"norm_scale{s}", [P, 2, BLOCKS])} for s in range(slots)]


def normalise(c, src, out, after, bank_a, bank_b, w, gain=None, bias=None, out_free=()):
    a, b = c.psum[:, bank_a, :], c.psum[:, bank_b, 0:BLOCKS]
    centred, square, scale = w["centred"], w["square"], w["scale"]
    mean = c.product(a, [(c.mean_of[:, :], src)], [c.constants_ready, c.emptied[bank_a], after])
    yield
    less = c.dve.do([mean, c.steps.get(w["written"])], lambda e: e.tensor_tensor(centred[:, :], src, a, ALU.subtract))
    yield
    squared = c.act.do([less], lambda e: e.activation(square[:, :], centred[:, :], ACT.Square))
    yield
    c.pe.wait(squared, c.emptied[bank_b])
    for j in range(BLOCKS):
        var = c.product(b[:, j:j + 1], [(square[:, j * P:(j + 1) * P], c.mean_of[:, 0:1])], [])
    yield
    root = c.act.do([var], lambda e: e.activation(scale[:, 0, :], b, ACT.Sqrt, bias=c.eps[:, :]))
    c.emptied[bank_b] = root
    yield
    recip = c.dve.do([root], lambda e: e.reciprocal(scale[:, 1, :], scale[:, 0, :]))
    yield
    c.pe.wait(recip, less)
    for j in range(BLOCKS):
        spread = c.product(a[:, j * P:(j + 1) * P],
                           [(scale[:, 1, j:j + 1].broadcast_to([P, P]), c.ident[:, :])], [])
    yield
    if gain is None:
        done = c.dve.do([spread, *out_free], lambda e: e.tensor_tensor(out, centred[:, :], a, ALU.mult))
        c.emptied[bank_a] = c.steps[w["written"]] = done
    else:
        scaled = c.dve.do([spread], lambda e: e.scalar_tensor_tensor(
            centred[:, :], centred[:, :], gain, a, ALU.mult, ALU.mult))
        c.emptied[bank_a] = scaled
        yield
        done = c.act.do([scaled, *out_free], lambda e: e.activation(out, centred[:, :], ACT.Identity, bias=bias))
        c.steps[w["written"]] = done
    w["done"] = done
    yield


def normalise_all(c, ctx, src, out, src_marks):
    marks = [None] * SEQS
    w = norm_buffers(c, ctx, 3)

    def tile(b, slot):
        yield from normalise(c, src[:, b, :], out[:, b, :], src_marks[b], 2 * slot, 2 * slot + 1, w[slot])
        marks[b] = w[slot]["done"]

    weave(in_flight(tile, SEQS, 3, lead=3))
    return marks


def top_two(c, prob, work, after):
    dve, n = c.dve, prob.shape[1]
    left, hit, first, mask = (work[:, i, :, :] for i in (0, 1, 2, 4))
    peak = work[:, 3, :, 0:1]
    wide = peak.broadcast_to([P, n, EXPERTS])
    rank = c.rank[:, :].rearrange("p (o e) -> p o e", o=1).broadcast_to([P, n, EXPERTS])
    m = dve.do(after, lambda e: e.tensor_copy(left, prob))
    for turn in range(2):
        m = dve.do([m], lambda e: e.tensor_reduce(peak, left, AX.X, ALU.max))
        m = dve.do([m], lambda e: e.tensor_tensor(hit, left, wide, ALU.is_equal))
        m = dve.do([m], lambda e: e.tensor_tensor(hit, hit, rank, ALU.mult))
        m = dve.do([m], lambda e: e.tensor_reduce(peak, hit, AX.X, ALU.max))
        m = dve.do([m], lambda e: e.tensor_tensor(first, hit, wide, ALU.is_equal))
        if turn == 0:
            m = dve.do([m], lambda e: e.tensor_copy(mask, first))
            m = dve.do([m], lambda e: e.scalar_tensor_tensor(left, first, -2.0, left, ALU.mult, ALU.add))
        else:
            m = dve.do([m], lambda e: e.tensor_tensor(mask, mask, first, ALU.add))
    return m


def split3(c, engine, parts, rest, after):
    m = engine.do(after, lambda e: e.tensor_copy(parts[0], rest))
    m = engine.do([m], lambda e: e.tensor_tensor(rest, rest, parts[0], ALU.subtract))
    m = engine.do([m], lambda e: e.tensor_copy(parts[1], rest))
    return engine.do([m], lambda e: e.tensor_tensor(parts[2], rest, parts[1], ALU.subtract))


def route_top_two(c, ctx, xn, xn_marks, gate, gate_bias, weights_ready, renormalise, whole_rows=False):
    n = TOKENS // P
    buf = lambda name, s, d=F32: c.buffer(ctx, name, s, d)
    prob, work = buf("prob", [P, n, EXPERTS]), buf("route_work", [P, 5, n, EXPERTS])
    total, inverse = buf("route_total", [P, n]), buf("route_inverse", [P, n])
    parts = buf("route_parts", [P, n, 3, EXPERTS], BF16)
    spread = buf("route_rows", [3 * EXPERTS, TOKENS], BF16)
    if whole_rows:
        whole, whole_marks = buf("route_whole_rows", [EXPERTS, TOKENS]), []
    logits = c.psum[:, 6, 0:n * EXPERTS].rearrange("p (n e) -> p n e", e=EXPERTS)
    dve, act = c.dve, c.act
    c.pe.wait(c.emptied[6], weights_ready)
    for j in range(n):
        b, k = divmod(j, BLOCKS)
        m = c.product(logits[:, j, :], [(xn[:, b, k * P:(k + 1) * P], gate)], [xn_marks[b]])
    wide = lambda t: t[:, :].rearrange("p (n o) -> p n o", o=1).broadcast_to([P, n, EXPERTS])
    bias = gate_bias.rearrange("p (o e) -> p o e", o=1).broadcast_to([P, n, EXPERTS])
    m = dve.do([m], lambda e: e.tensor_tensor(prob[:, :, :], logits, bias, ALU.add))
    c.emptied[6] = m
    m = dve.do([m], lambda e: e.tensor_reduce(total[:, :], prob[:, :, :], AX.X, ALU.max))
    m = dve.do([m], lambda e: e.tensor_tensor(prob[:, :, :], prob[:, :, :], wide(total), ALU.subtract))
    m = act.do([m], lambda e: e.activation(prob[:, :, :], prob[:, :, :], ACT.Exp))
    m = dve.do([m], lambda e: e.tensor_reduce(total[:, :], prob[:, :, :], AX.X, ALU.add))
    m = dve.do([m], lambda e: e.reciprocal(inverse[:, :], total[:, :]))
    m = dve.do([m], lambda e: e.tensor_tensor(prob[:, :, :], prob[:, :, :], wide(inverse), ALU.mult))
    m = top_two(c, prob[:, :, :], work[:, :, :, :], [m, c.constants_ready])
    m = dve.do([m], lambda e: e.tensor_tensor(prob[:, :, :], prob[:, :, :], work[:, 4, :, :], ALU.mult))
    if renormalise:
        m = dve.do([m], lambda e: e.tensor_reduce(total[:, :], prob[:, :, :], AX.X, ALU.add))
        m = dve.do([m], lambda e: e.reciprocal(inverse[:, :], total[:, :]))
        m = dve.do([m], lambda e: e.tensor_tensor(prob[:, :, :], prob[:, :, :], wide(inverse), ALU.mult))
    if whole_rows:
        for b in range(SEQS):
            c.pe.wait(m, c.emptied[4 + b % 2])
            for k in range(BLOCKS):
                turned = c.pe.do([], lambda e: e.transpose(
                    c.psum[0:EXPERTS, 4 + b % 2, k * P:(k + 1) * P], prob[:, b * BLOCKS + k, :], c.ident[:, :]))
            kept = act.do([turned], lambda e: e.activation(
                whole[:, b * SEQ:(b + 1) * SEQ], c.psum[0:EXPERTS, 4 + b % 2, :], ACT.Copy))
            c.emptied[4 + b % 2] = kept
            whole_marks.append(kept)
        m = kept
    m = split3(c, dve, [parts[:, :, i, :] for i in range(3)], prob[:, :, :], [m])
    marks = []
    for b in range(SEQS):
        rows = c.psum[0:3 * EXPERTS, 6 + b % 2, 0:SEQ // 2].bitcast(BF16)
        c.pe.wait(m, c.emptied[6 + b % 2])
        for k in range(BLOCKS):
            turned = c.pe.do([], lambda e: e.transpose(
                rows[:, k * P:(k + 1) * P], parts[:, b * BLOCKS + k, :, :].rearrange("p i e -> p (i e)"),
                c.ident16[:, :]))
        kept = act.do([turned], lambda e: e.activation(spread[:, b * SEQ:(b + 1) * SEQ], rows, ACT.Copy))
        c.emptied[6 + b % 2] = kept
        marks.append(kept)
    return (spread, marks, whole, whole_marks) if whole_rows else (spread, marks)


def update(c, ctx_buf, x, b, attn, attn_ready, gate_psum, gate_ready, bank, slot):
    gated = ctx_buf
    m = c.act.do([gate_ready, c.steps.get(f"gated_added{slot}")], lambda e: e.activation(gated[:, :], gate_psum, SILU))
    c.emptied[bank] = m
    m = c.pool.do([m, attn_ready], lambda e: e.tensor_tensor(gated[:, :], gated[:, :], attn, ALU.mult))
    m = c.pool.do([m], lambda e: e.tensor_tensor(x[:, b, :], x[:, b, :], gated[:, :], ALU.add))
    c.steps[f"gated_added{slot}"] = m
    return m


STATES = 16
BC_ROWS = 2 * STATES
DT_AT = 3 * BC_ROWS
GROUP = 4


class Mamba:

    def __init__(self, c, ctx, w, w_ready, halves, taps):
        self.c, self.w, self.w_ready, self.halves, self.taps = c, w, w_ready, halves, taps
        buf = lambda name, s, d=F32: c.buffer(ctx, name, s, d)
        pad = taps - 1
        self.x_in = [buf(f"mamba_in{h}", [P, pad + SEQ]) for h in range(halves)]
        self.conv = [buf(f"mamba_conv{h}", [P, SEQ]) for h in range(halves)]
        self.work = [buf(f"mamba_work{h}", [P, 2, SEQ]) for h in range(halves)]
        self.proj = buf("mamba_proj", [P, SEQ])
        per_slot = lambda name, d=F32: [[buf(f"mamba_{name}{s}{h}", [P, SEQ], d) for h in range(halves)] for s in range(2)]
        self.x, self.z, self.delta, self.u = per_slot("x"), per_slot("z"), per_slot("delta"), per_slot("u")
        self.bc = [buf(f"mamba_bc{s}", [3 * BC_ROWS, SEQ], BF16) for s in range(2)]
        self.decay = [buf(f"mamba_decay{i}", [P, GROUP, SEQ]) for i in range(2)]
        self.state = [buf(f"mamba_state{i}", [P, GROUP, SEQ]) for i in range(3)]
        self.c_wide = [buf(f"mamba_c{i}", [P, GROUP, SEQ]) for i in range(2)]
        self.pick = buf("mamba_pick", [3 * BC_ROWS, BC_ROWS], BF16)
        self.decay_scanned, self.state_summed, self.c_multiplied = [None] * 2, [None] * 3, [None] * 2
        self.unit_projected = [None] * 2
        self.turns = 0
        self.unit = {}
        set_up = [c.pool.do([w_ready], lambda e: e.tensor_copy(self.pick[:, :], w["pick_state"]))]
        set_up += [c.pool.do([], lambda e: e.memset(d[:, :, 0:1], 0.0)) for d in self.decay]
        set_up += [c.pool.do([], lambda e: e.memset(x[:, 0:pad], 0.0)) for x in self.x_in]
        self.set_up = set_up[-1]

    def decay_rates(self, name):
        a = self.w[name + "a_log"]
        m = self.c.act.do([self.w_ready], lambda e: e.activation(a, a, ACT.Exp))
        self.rates_ready = self.c.act.do([m], lambda e: e.activation(a, a, ACT.Copy, scale=-1.0))

    def front(self, name, slot, src, src_ready):
        c, w, halves, pad = self.c, self.w, range(self.halves), self.taps - 1
        inner = self.halves * P
        wait, free = [src_ready, self.w_ready, self.set_up], self.unit_projected[slot]
        bank = lambda n: c.psum[:, n, :]
        conv_done = []
        for h in halves:
            m = c.product(bank(6), [(w[name + "w_in"][:, h * P:(h + 1) * P], src)], [*wait, c.emptied[6]])
            m = c.act.do([m, c.steps.get(f"conv_made{h}")], lambda e: e.activation(self.x_in[h][:, pad:pad + SEQ], bank(6), ACT.Copy))
            c.emptied[6] = m
            yield
            taps = w[name + "conv_w"][:, h * self.taps:(h + 1) * self.taps]
            m = c.dve.do([m, c.steps.get(f"conv_activated{h}")], lambda e: e.tensor_scalar(
                self.conv[h][:, :], self.x_in[h][:, 0:SEQ], taps[:, 0:1], None, ALU.mult))
            for k in range(1, self.taps):
                m = c.dve.do([m], lambda e: e.scalar_tensor_tensor(
                    self.conv[h][:, :], self.x_in[h][:, k:k + SEQ], taps[:, k:k + 1], self.conv[h][:, :], ALU.mult, ALU.add))
            c.steps[f"conv_made{h}"] = m
            conv_done.append(m)
            yield
        for h in halves:
            m = c.product(bank(6), [(w[name + "w_in"][:, inner + h * P:inner + (h + 1) * P], src)], [*wait, c.emptied[6]])
            c.emptied[6] = c.act.do([m, free], lambda e: e.activation(self.z[slot][h][:, :], bank(6), SILU))
        for h in halves:
            m = c.act.do([conv_done[h], free], lambda e: e.activation(
                self.x[slot][h][:, :], self.conv[h][:, :], SILU, bias=w[name + "conv_b"][:, h:h + 1]))
            c.steps[f"conv_activated{h}"] = m
        yield
        rows = DT_AT + 8
        m = c.product(c.psum[0:rows, 6, :], [(w[name + "x_proj"][:, h * rows:(h + 1) * rows], self.x[slot][h][:, :])
                                             for h in halves], [m, c.emptied[6]])
        proj, bc = self.proj, self.bc[slot]
        m = kept = c.act.do([m, c.steps.get("proj_used")], lambda e: e.activation(proj[0:rows, :], c.psum[0:rows, 6, :], ACT.Copy))
        c.emptied[6] = m
        yield
        m = c.pool.do([m, free], lambda e: e.tensor_copy(bc[:, :], proj[0:DT_AT, :]))
        for at in (BC_ROWS, 2 * BC_ROWS):
            part = slice(at, at + BC_ROWS)
            m = c.pool.do([m], lambda e: e.tensor_tensor(proj[part, :], proj[part, :], bc[part, :], ALU.subtract))
            m = c.pool.do([m], lambda e: e.tensor_copy(bc[part, :], proj[part, :]))
        bc_ready = c.pool.do([m], lambda e: e.tensor_tensor(bc[part, :], proj[part, :], bc[part, :], ALU.subtract))
        yield
        for h in halves:
            bias, work = w[name + "dt_b"][:, h:h + 1], self.work[h]
            raw = c.product(bank(6), [(w[name + "dt_w"][DT_AT:rows, h * P:(h + 1) * P], proj[DT_AT:rows, :])],
                            [kept, c.emptied[6]])
            a = c.act.do([raw, c.steps.get(f"softplus_added{h}")], lambda e: e.activation(work[:, 0, :], bank(6), ACT.Abs, bias=bias))
            b = c.dve.do([a, free], lambda e: e.tensor_scalar(self.delta[slot][h][:, :], bank(6), bias, 0.0, ALU.add, ALU.max))
            c.emptied[6] = b
            a = c.act.do([a], lambda e: e.activation(work[:, 1, :], work[:, 0, :], ACT.Exp, scale=-1.0))
            a = c.act.do([a], lambda e: e.activation(work[:, 0, :], work[:, 1, :], ACT.Ln, bias=1.0))
            yield
            m = c.pool.do([a, b], lambda e: e.tensor_tensor(self.delta[slot][h][:, :], self.delta[slot][h][:, :], work[:, 0, :], ALU.add))
            c.steps[f"softplus_added{h}"] = m
            m = c.pool.do([m], lambda e: e.tensor_tensor(self.u[slot][h][:, :], self.delta[slot][h][:, :], self.x[slot][h][:, :], ALU.mult))
            yield
        c.steps["proj_used"] = [raw, bc_ready]
        self.unit[slot] = [m, bc_ready]

    def scan(self, name, slot):
        c, w, halves = self.c, self.w, range(self.halves)
        ready = self.unit[slot]
        bc = self.bc[slot]
        pick = lambda n: self.pick[:, n:n + 1].broadcast_to([3 * BC_ROWS, P])
        pending = []
        for group in range(STATES // GROUP):
            turn = self.turns
            self.turns += 1
            states = [self.state[(turn * self.halves + h) % 3] for h in halves]
            free = [self.state_summed[(turn * self.halves + h) % 3] for h in halves]
            decayed = []
            for h in halves:
                i = (turn * self.halves + h) % 2
                for n in range(GROUP):
                    at = h * STATES + group * GROUP + n
                    m = c.act.do([ready, self.rates_ready, self.set_up, self.decay_scanned[i]], lambda e: e.activation(
                        self.decay[i][:, n, 1:SEQ], self.delta[slot][h][:, 1:SEQ], ACT.Exp, scale=w[name + "a_log"][:, at:at + 1]))
                decayed.append((i, m))
                if h == 0:
                    yield
            filled = [None, None]
            for pair in range(GROUP // 2):
                for n in range(2):
                    m = c.product(c.psum[:, n, :], [(pick(group * GROUP + 2 * pair + n), bc[:, :])], [ready, c.emptied[n]])
                for h in halves:
                    u = self.u[slot][h][:, :].rearrange("p (o t) -> p o t", o=1).broadcast_to([P, 2, SEQ])
                    filled[h] = c.dve.do([m, free[h]], lambda e: e.tensor_tensor(
                        states[h][:, 2 * pair:2 * pair + 2, :], c.psum[:, 0:2, :], u, ALU.mult))
                c.emptied[0] = c.emptied[1] = filled[self.halves - 1]
                yield
                for n in range(2):
                    m = c.product(c.psum[:, 2 + n, :], [(pick(STATES + group * GROUP + 2 * pair + n), bc[:, :])],
                                  [c.emptied[2 + n]])
                wide = self.c_wide[turn % 2]
                spread = c.act.do([m, self.c_multiplied[turn % 2]], lambda e: e.activation(
                    wide[:, 2 * pair:2 * pair + 2, :], c.psum[:, 2:4, :], ACT.Copy))
                c.emptied[2] = c.emptied[3] = spread
                yield
            for h, s, m in pending:
                self.add_states(h, s, m, group - 1)
            pending = []
            for h in halves:
                i, m = decayed[h]
                flat = lambda t: t[:, :, :].rearrange("p n t -> p (n t)")
                m = c.dve.do([m, filled[h]], lambda e: e.tensor_tensor_scan(
                    flat(states[h]), flat(self.decay[i]), flat(states[h]), 0.0, ALU.mult, ALU.add))
                self.decay_scanned[i] = m
                m = c.pool.do([m, spread], lambda e: e.tensor_tensor(
                    states[h][:, :, :], states[h][:, :, :], wide[:, :, :], ALU.mult))
                pending.append((h, (turn * self.halves + h) % 3, m))
                yield
            self.c_multiplied[turn % 2] = m
            if self.halves == 2 and group < STATES // GROUP:
                h, s, m = pending.pop(0)
                self.add_states(h, s, m, group)
        for h, s, m in pending:
            self.add_states(h, s, m, group)
        yield

    def add_states(self, h, s, ready, group):
        c = self.c
        m = c.product(c.psum[:, 4 + h, :], [(c.ident[:, :], self.state[s][:, n, :]) for n in range(GROUP)],
                      [ready, c.emptied[4 + h] if group == 0 else None],
                      start=group == 0, stop=group == STATES // GROUP - 1)
        self.state_summed[s] = m
        self.summed = m

    def back(self, name, slot, out, free, reverse):
        c, w = self.c, self.w
        for h in range(self.halves):
            y = self.u[slot][h]
            m = c.dve.do([self.summed], lambda e: e.scalar_tensor_tensor(
                y[:, :], self.x[slot][h][:, :], w[name + "skip"][:, h:h + 1], c.psum[:, 4 + h, :], ALU.mult, ALU.add))
            c.emptied[4 + h] = m
            gated = c.pool.do([m], lambda e: e.tensor_tensor(y[:, :], y[:, :], self.z[slot][h][:, :], ALU.mult))
            yield
        m = c.product(c.psum[:, 7, :], [(w[name + "w_out"][:, h * P:(h + 1) * P], self.u[slot][h][:, :])
                                        for h in range(self.halves)], [gated, c.emptied[7]])
        self.unit_projected[slot] = m
        bank = c.psum[:, 7, ::-1] if reverse else c.psum[:, 7, :]
        self.out_ready = c.act.do([m, free], lambda e: e.activation(out, bank, ACT.Copy))
        c.emptied[7] = self.out_ready
        yield


HEADS0, DIM0 = 16, 8
PAIRS0 = HEADS0 // 2
QUADS0 = HEADS0 // 4
TERMS = 6
KEY_PART = (0, 0, 1, 0, 2, 1)
QUERY_PART = (0, 1, 0, 2, 0, 1)
ROWS0 = TERMS * DIM0
MAX_ROWS = 3


class Attention0:

    def __init__(self, c, ctx, xn, xn_marks, w, w_ready, out):
        self.c, self.xn, self.xn_marks, self.w, self.w_ready, self.out = c, xn, xn_marks, w, w_ready, out
        buf = lambda name, s, d=F32: c.buffer(ctx, name, s, d)
        self.q_rows = [buf(f"q_rows{s}", [P, PAIRS0, SEQ], BF16) for s in range(2)]
        self.k_rows = [buf(f"k_rows{s}", [P, PAIRS0, SEQ], BF16) for s in range(2)]
        self.rest = [buf(f"qk_rest{i}", [P, SEQ]) for i in range(2)]
        self.parts = [buf(f"qk_parts{i}", [P, 3, SEQ], BF16) for i in range(2)]
        self.values = [buf(f"values{s}", [P, BLOCKS, HEADS0, 32]) for s in range(2)]
        self.peak = [buf(f"peak{s}", [P, BLOCKS, HEADS0]) for s in range(2)]
        self.less_peak = buf("less_peak", [HEADS0, SEQ])
        self.peak_parts = buf("peak_parts", [HEADS0, 3, SEQ], BF16)
        self.exps = [buf(f"exps{i}", [P, 2, SEQ]) for i in range(4)]
        self.heads = [buf(f"heads{g}", [P, SEQ]) for g in range(QUADS0)]
        self.sums = buf("sums", [HEADS0, SEQ])
        self.normed = [buf(f"normed{g}", [P, SEQ]) for g in range(QUADS0)]
        dram = lambda name, s: c.nc.dram_tensor(name, s, BF16, kind="Internal").ap()
        self.qk_dram = [[dram(f"qk_dram{i}{s}", [P, 3, SEQ]) for i in range(2)] for s in range(2)]
        self.peak_dram = [dram(f"peak_dram{s}", [HEADS0, 3, SEQ]) for s in range(2)]
        self.ones_dram = dram("ones_dram", [MAX_ROWS, PAIRS0 * SEQ])
        self.to_dram = [[Transfers(c.sem(f"qk_to_dram{i}{s}")) for i in range(2)] for s in range(2)]
        self.from_dram = [Transfers(c.sem(f"qk_from_dram{s}")) for s in range(2)]
        self.peak_out = [Transfers(c.sem(f"peak_out{s}")) for s in range(2)]
        self.peak_in = [Transfers(c.sem(f"peak_in{s}")) for s in range(2)]
        self.ready = [None] * SEQS
        self.values_weighedy = [None] * SEQS
        self.shifted = [None] * SEQS
        self.done = [None] * SEQS
        self.rows_scored = [None] * 2
        self.values_weighed = [None] * 2
        self.exps_weighed = [None] * 4
        self.units = 0
        self.setup()

    def setup(self):
        c = self.c
        self.set = []
        for s in range(2):
            m = c.pool.do([], lambda e: e.memset(self.values[s][:, :, :, :], 0.0))
            self.set.append(c.pool.do([m], lambda e: e.memset(self.values[s][:, :, :, DIM0:DIM0 + 1], 1.0)))
        ones = self.exps[0][0:MAX_ROWS, :, :].rearrange("p a t -> p (a t)").bitcast(BF16)[:, 0:2 * SEQ]
        m = c.pool.do([], lambda e: e.memset(ones, 1.0))
        t = Transfers(c.sem("ones_to_dram"))
        for i in range(PAIRS0 * SEQ // (2 * SEQ)):
            stored = t.start(c.sync, self.ones_dram[:, i * 2 * SEQ:(i + 1) * 2 * SEQ], ones, [m])
        t = Transfers(c.sem("ones_to_rows"))
        for s in range(2):
            for j in range(2):
                rows = self.k_rows[s][64 * j + ROWS0:64 * j + ROWS0 + MAX_ROWS, :, :]
                self.ones_ready = t.start(c.sync, rows.rearrange("p g t -> p (g t)"), self.ones_dram, [stored])
        self.exps_weighed[0] = stored

    def project(self, b):
        c, w, s, xn = self.c, self.w, b % 2, self.xn[:, b, :]
        bank = c.psum[:, 7, :]
        moved = []
        for i, name in enumerate(("wq", "wk")):
            bias = w["bq" if i == 0 else "bk"]
            m = c.product(bank, [(w[name], xn)], [self.w_ready, self.xn_marks[b], c.emptied[7]])
            rest, parts = self.rest[i], [self.parts[i][:, k, :] for k in range(3)]
            before = c.steps.get(f"parts_stored{i}")
            m = c.act.do([m, before], lambda e: e.activation(rest[:, :], bank, ACT.Identity, bias=bias))
            c.emptied[7] = m
            m = split3(c, c.pool, parts, rest[:, :], [m])
            yield
            m = self.to_dram[s][i].start(c.sync, self.qk_dram[s][i], self.parts[i][:, :, :], [m, self.ready[b - 2] if b > 1 else None])
            c.steps[f"parts_stored{i}"] = m
            moved.append(m)
            yield
        for i, (rows, term_part) in enumerate(((self.q_rows[s], QUERY_PART), (self.k_rows[s], KEY_PART))):
            src = self.qk_dram[s][i].rearrange("(g j d) k t -> j k d g t", j=2, d=DIM0)
            for j in range(2):
                for t in range(TERMS):
                    at = 64 * j + DIM0 * t
                    self.ready[b] = self.from_dram[s].start(
                        c.sync, rows[at:at + DIM0, :, :], src[j, term_part[t]], [moved[i], self.rows_scored[s]])
                yield
        for k in range(BLOCKS):
            v = c.psum[:, 7, k * P:(k + 1) * P]
            m = c.product(v, [(xn[:, k * P:(k + 1) * P], w["wv"])], [c.emptied[7]] if k == 0 else [])
        for k in range(BLOCKS):
            m2 = c.dve.do([m, self.values_weighed[s], self.set[s]], lambda e: e.tensor_tensor(
                self.values[s][:, k, :, 0:DIM0], bank[:, k * P:(k + 1) * P].rearrange("p (h d) -> p h d", d=DIM0),
                w["bv_rows"].rearrange("p (h d) -> p h d", d=DIM0), ALU.add))
        c.emptied[7] = self.values_weighedy[b] = m2
        yield

    def take_pair(self):
        self.units += 1
        return 2 * (self.units % 3)

    def maxima(self, b):
        c, s = self.c, b % 2
        q, k, peak = self.q_rows[s], self.k_rows[s], self.peak[s]
        for block in range(BLOCKS):
            for g in range(PAIRS0):
                at = self.take_pair()
                for j in range(2):
                    rows = slice(64 * j, 64 * j + ROWS0)
                    m = c.product(c.psum[:, at + j, :], [(q[rows, g, block * P:(block + 1) * P], k[rows, g, :])],
                                  [self.ready[b], c.emptied[at + j]])
                m = c.dve.do([m, self.shifted[b - 2] if b > 1 else None], lambda e: e.tensor_reduce(
                    peak[:, block, 2 * g:2 * g + 2], c.psum[:, at:at + 2, :], AX.X, ALU.max))
                c.emptied[at] = c.emptied[at + 1] = m
                yield
        c.pe.wait(m, c.emptied[7])
        for block in range(BLOCKS):
            m = c.pe.do([], lambda e: e.transpose(
                c.psum[0:HEADS0, 7, block * P:(block + 1) * P], peak[:, block, :], c.ident[:, :]))
        m = c.act.do([m, c.steps.get("peak_stored")], lambda e: e.activation(
            self.less_peak[:, :], c.psum[0:HEADS0, 7, :], ACT.Copy, scale=-1.0))
        c.emptied[7] = m
        m = split3(c, c.pool, [self.peak_parts[:, i, :] for i in range(3)], self.less_peak[:, :], [m])
        yield
        m = self.peak_out[s].start(c.sync, self.peak_dram[s], self.peak_parts[:, :, :],
                                   [m, self.shifted[b - 2] if b > 1 else None])
        c.steps["peak_stored"] = m
        src = self.peak_dram[s].rearrange("(g j) k t -> j k g t", j=2)
        for j in range(2):
            at = 64 * j + ROWS0
            self.shifted[b] = self.peak_in[s].start(c.sync, q[at:at + MAX_ROWS, :, :], src[j], [m, self.rows_scored[s]])
        yield

    def attend(self, b):
        c, w, s = self.c, self.w, b % 2
        q, k, values = self.q_rows[s], self.k_rows[s], self.values[s]
        rows = [slice(64 * j, 64 * j + ROWS0 + MAX_ROWS) for j in range(2)]
        turn = 0
        pending = None
        for quad in range(QUADS0):
            for block in range(BLOCKS):
                exps = []
                for half in range(2):
                    at, g = self.take_pair(), 2 * quad + half
                    for j in range(2):
                        m = c.product(c.psum[:, at + j, :], [(k[rows[j], g, block * P:(block + 1) * P], q[rows[j], g, :])],
                                      [self.ready[b], self.shifted[b], self.ones_ready, c.emptied[at + j]])
                    e_buf, n = self.exps[turn % 4], turn % 4
                    m = c.act.do([m, self.exps_weighed[n]], lambda e: e.activation(
                        e_buf[:, :, :], c.psum[:, at:at + 2, :], ACT.Exp, scale=1.0 / float(np.sqrt(np.float32(DIM0)))))
                    c.emptied[at] = c.emptied[at + 1] = m
                    exps.append((n, m))
                    turn += 1
                    yield
                if pending:
                    self.weigh(b, *pending)
                pending = (quad, block, exps)
        self.rows_scored[s] = c.pe.last()
        self.weigh(b, *pending)
        self.values_weighed[s] = c.pe.last()
        yield
        m = c.product(c.psum[0:HEADS0, 7, :], [(w["sum_rows"][:, g * HEADS0:(g + 1) * HEADS0], self.heads[g][:, :])
                                               for g in range(QUADS0)], [self.heads_kept, c.emptied[7]])
        m = c.dve.do([m, c.steps.get("sums_spread")], lambda e: e.reciprocal(self.sums[:, :], c.psum[0:HEADS0, 7, :]))
        c.emptied[7] = m
        yield
        for g in range(QUADS0):
            wide = c.product(c.psum[:, 7, :], [(w["head_rows"][0:HEADS0, g * P:(g + 1) * P], self.sums[:, :])],
                             [m, c.emptied[7]])
            n = c.dve.do([wide, c.steps.get("heads_projected")], lambda e: e.scalar_tensor_tensor(
                self.normed[g][:, :], self.heads[g][:, :], w["mask_rows"][:, g:g + 1], c.psum[:, 7, :], ALU.mult, ALU.mult))
            c.emptied[7] = n
            yield
        c.steps["sums_spread"] = wide
        c.steps["heads_divided"] = n
        m = c.product(c.psum[:, 7, :], [(w["wo_rows"][:, g * P:(g + 1) * P], self.normed[g][:, :])
                                        for g in range(QUADS0)], [n, c.emptied[7]])
        c.steps["heads_projected"] = m
        self.done[b] = c.act.do([m], lambda e: e.activation(self.out[:, b, :], c.psum[:, 7, :], ACT.Identity, bias=w["bo"]))
        c.emptied[7] = self.done[b]
        yield

    def weigh(self, b, quad, block, exps):
        c, values = self.c, self.values[b % 2]
        c.pe.wait(self.values_weighedy[b], exps[1][1])
        if block == 0:
            c.pe.wait(c.emptied[6])
        for half in range(2):
            for j in range(2):
                i, head = 2 * half + j, 4 * quad + 2 * half + j
                m = c.product(c.psum[32 * i:32 * i + 32, 6, :],
                              [(values[:, block, head, :], self.exps[exps[half][0]][:, j, :])], [],
                              start=block == 0, stop=block == BLOCKS - 1)
            self.exps_weighed[exps[half][0]] = m
        if block == BLOCKS - 1:
            self.heads_kept = c.dve.do([m, c.steps.get("heads_divided")], lambda e: e.tensor_copy(
                self.heads[quad][:, :], c.psum[:, 6, :]))
            c.emptied[6] = self.heads_kept

    def run(self):
        def project(b):
            if b < SEQS:
                yield from self.project(b)

        def maxima(b):
            if b < SEQS:
                yield from self.maxima(b)

        weave(project(0))
        weave(maxima(0), project(1))
        for b in range(SEQS):
            weave(self.attend(b), maxima(b + 1))
            weave(project(b + 2))


def swiglu(c, w_in, rhs, after, bank_a, bank_b, silu_buf, out, free):
    a, b = c.psum[:, bank_a, :], c.psum[:, bank_b, :]
    ma = c.product(a, [(w_in[:, 0:P], rhs)], [*after, c.emptied[bank_a]])
    mb = c.product(b, [(w_in[:, P:2 * P], rhs)], [c.emptied[bank_b]])
    yield
    m = c.act.do([ma, *free], lambda e: e.activation(silu_buf, a, SILU))
    c.emptied[bank_a] = m
    yield
    m = c.dve.do([m, mb, *free], lambda e: e.tensor_tensor(out, silu_buf, b, ALU.mult))
    c.emptied[bank_b] = m
    yield m


def ffn0(c, ctx, x, xn, xn_marks, attn, attn_marks, w, w_ready):
    rows, rows_scoredy = route_top_two(c, ctx, xn, xn_marks, w["w_gate"], w["gate_bias_rows"], w_ready, False)
    buf = lambda name, s=[P, SEQ]: [c.buffer(ctx, f"{name}{i}", s) for i in range(2)]
    silu, shared, hidden, gated, scaled = buf("silu"), buf("shared"), buf("hidden"), buf("gated"), buf("scaled", [P, 2, SEQ])
    marks = [None] * SEQS

    def tile(b, slot):
        base = 4 * slot
        rhs, total = xn[:, b, :], c.psum[:, base + 2, :]
        free = [c.steps.get(f"ffn_summed{slot}")]
        for name, out in (("w_shared_in", shared), ("w1_shared", hidden)):
            for m in swiglu(c, w[name], rhs, [w_ready], base, base + 1, silu[slot][:, :], out[slot][:, :], free):
                yield
            free.append(m)
            if name == "w_shared_in":
                shared_ready = m
        hidden_usedy = m
        c.product(total, [(w["w_shared_out"], shared[slot][:, :])], [shared_ready, c.emptied[base + 2]], stop=False)
        read = [None, None]
        for n in range(EXPERTS):
            wide_bank, half = base + n % 2, n % 2
            wide = c.psum[:, wide_bank, :]
            m = c.product(wide, [(c.pick[0:3 * EXPERTS, n:n + 1].broadcast_to([3 * EXPERTS, P]), rows[:, b * SEQ:(b + 1) * SEQ])],
                          [rows_scoredy[b], c.emptied[wide_bank]])
            m = c.dve.do([m, hidden_usedy, read[half], *free], lambda e: e.tensor_tensor(
                scaled[slot][:, half, :], hidden[slot][:, :], wide, ALU.mult))
            c.emptied[wide_bank] = m
            yield
            m = c.product(total, [(w["w2"][:, n * P:(n + 1) * P], scaled[slot][:, half, :])], [m],
                          start=False, stop=n == EXPERTS - 1)
            read[half] = m
        c.steps[f"ffn_summed{slot}"] = m
        yield
        marks[b] = update(c, gated[slot], x, b, attn[:, b, :], attn_marks[b], total, m, base + 2, slot)
        yield

    weave(in_flight(tile, SEQS, 2, lead=6))
    return marks


def layer0(c, x, xn, attn, x_marks, attn_weights, ffn_weights):
    with ExitStack() as layer_ctx:
        w, w_ready = attn_weights.load(layer_ctx)
        wf, wf_ready = ffn_weights.load(layer_ctx)
        with ExitStack() as ctx:
            xn_marks = normalise_all(c, ctx, x, xn, x_marks)
        c.barrier()
        with ExitStack() as ctx:
            attention = Attention0(c, ctx, xn, xn_marks, w, w_ready, attn)
            attention.run()
        c.barrier()
        with ExitStack() as ctx:
            return ffn0(c, ctx, x, xn, xn_marks, attn, attention.done, wf, wf_ready)


CHUNKS = P // EXPERTS
CHUNK = TOKENS // CHUNKS
HIDDEN1 = 512
HID_BLOCKS1 = HIDDEN1 // P
CAPACITY = TOKENS * 2 // EXPERTS


def attention1(c, ctx, xn, xn_marks, w, w_ready, out):
    mamba = Mamba(c, ctx, w, w_ready, 2, 4)
    for name in ("fwd_", "bwd_"):
        mamba.decay_rates(name)
    turned = c.buffer(ctx, "turned", [P, SEQ])
    both = [c.buffer(ctx, f"direction{i}", [P, SEQ]) for i in range(2)]
    done = [None] * SEQS
    merged = [None]

    def front(u):
        if u >= 2 * SEQS:
            return
        b, backwards = divmod(u, 2)
        src, ready = xn[:, b, :], xn_marks[b]
        if backwards:
            ready = c.act.do([ready, c.steps.get("turned_projected")], lambda e: e.activation(turned[:, :], xn[:, b, ::-1], ACT.Copy))
            src = turned[:, :]
        yield from mamba.front(("fwd_", "bwd_")[backwards], u % 2, src, ready)
        if backwards:
            c.steps["turned_projected"] = c.pe.last()

    def scan(u):
        b, backwards = divmod(u, 2)
        name = ("fwd_", "bwd_")[backwards]
        yield from mamba.scan(name, u % 2)
        yield from mamba.back(name, u % 2, both[backwards][:, :], merged[0], backwards)
        if backwards:
            m = c.product(c.psum[:, 7, :], [(w["merge"][:, i * P:(i + 1) * P], both[i][:, :]) for i in range(2)],
                          [mamba.out_ready, c.emptied[7]])
            merged[0] = m
            done[b] = c.emptied[7] = c.act.do([m], lambda e: e.activation(out[:, b, :], c.psum[:, 7, :], ACT.Copy))

    weave(front(0))
    for u in range(2 * SEQS):
        weave(scan(u), front(u + 1))
    return done


def choose_tokens(c, ctx, xn, xn_marks, w, w_ready):
    buf = lambda name, s, d=F32: c.buffer(ctx, name, s, d)
    score, hit, tie, rank = (buf(f"choose_{n}", [P, CHUNK]) for n in ("score", "hit", "tie", "rank"))
    col = buf("choose_columns", [P, 8])
    bits = buf("choose_bits", [P, 3], I32)
    level, trial, step = bits[:, 0:1], bits[:, 1:2], bits[:, 2:3]
    dve, bank = c.dve, c.psum[:, 7, 0:1]
    gate = w["gate_wide"]
    per_seq = SEQ // CHUNK
    m = c.product(c.psum[:, 6, 0:CHUNK], [
        (gate[:, (CHUNKS - 1 - k) * EXPERTS:(2 * CHUNKS - 1 - k) * EXPERTS],
         xn[:, k // per_seq, (k % per_seq) * CHUNK:(k % per_seq + 1) * CHUNK]) for k in range(CHUNKS)],
        [w_ready, xn_marks, c.emptied[6]])
    m = scored = c.emptied[6] = c.act.do([m], lambda e: e.activation(score[:, :], c.psum[:, 6, 0:CHUNK], ACT.Sigmoid))
    t = dve.do([], lambda e: e.memset(level, 0))
    for bit in range(29, -1, -1):
        m = dve.do([t], lambda e: e.tensor_scalar(trial, level, 1 << bit, None, ALU.bitwise_or))
        m = dve.do([m, scored], lambda e: e.tensor_scalar(
            hit[:, :], score[:, :], trial.bitcast(F32), 0.0, ALU.is_ge, ALU.add, accum_out=col[:, 0:1]))
        m = c.product(bank, [(w["same_expert"], col[:, 0:1])], [m, c.emptied[7]])
        m = dve.do([m], lambda e: e.tensor_scalar(step, bank, CAPACITY - 0.5, float(1 << bit), ALU.is_ge, ALU.mult))
        c.emptied[7] = m
        t = dve.do([m], lambda e: e.tensor_tensor(level, level, step, ALU.bitwise_or))
        yield
    least = level.bitcast(F32)
    m = dve.do([t], lambda e: e.tensor_scalar(hit[:, :], score[:, :], least, 0.0, ALU.is_gt, ALU.add, accum_out=col[:, 1:2]))
    m = dve.do([m], lambda e: e.tensor_scalar(tie[:, :], score[:, :], least, 0.0, ALU.is_equal, ALU.add, accum_out=col[:, 2:3]))
    m = c.product(bank, [(w["same_expert"], col[:, 1:2]), (w["before"], col[:, 2:3])], [m, c.emptied[7]])
    m = dve.do([m], lambda e: e.tensor_scalar(col[:, 3:4], bank, -1.0, float(CAPACITY), ALU.mult, ALU.add))
    c.emptied[7] = m
    m = dve.do([m], lambda e: e.memset(rank[:, :], 1.0))
    m = dve.do([m], lambda e: e.tensor_tensor_scan(rank[:, :], rank[:, :], tie[:, :], 0.0, ALU.mult, ALU.add))
    m = dve.do([m], lambda e: e.scalar_tensor_tensor(tie[:, :], rank[:, :], col[:, 3:4], tie[:, :], ALU.is_le, ALU.mult))
    m = dve.do([m], lambda e: e.tensor_tensor(hit[:, :], hit[:, :], tie[:, :], ALU.add))
    m = dve.do([m], lambda e: e.tensor_tensor(score[:, :], score[:, :], hit[:, :], ALU.mult))
    c.chosen = score, m
    yield


def ffn1(c, ctx, x, xn, xn_marks, attn, attn_marks, w, w_ready):
    chosen, chosen_ready = c.chosen
    buf = lambda name, n, s=[P, SEQ]: [c.buffer(ctx, f"{name}{i}", s) for i in range(n)]
    hidden, given, total = buf("hidden", 2, [P, HID_BLOCKS1, SEQ]), buf("given", 2), buf("total", 2)
    marks = [None] * SEQS
    hidden_used, given_added = [None] * 2, [None] * 2
    per_seq = SEQ // CHUNK
    for turn in range(SEQS * EXPERTS + 1):
        if turn < SEQS * EXPERTS:
            b, n, s = turn // EXPERTS, turn % EXPERTS, turn % 2
            made = []
            for f in range(HID_BLOCKS1):
                at = n * HIDDEN1 + f * P
                m = c.product(c.psum[:, f, :], [(w["w1"][:, at:at + P], xn[:, b, :])],
                              [xn_marks[b], w_ready, c.emptied[f]])
                bias = w["b1"][:, n * HID_BLOCKS1 + f:n * HID_BLOCKS1 + f + 1]
                m = c.act.do([m, hidden_used[s]], lambda e: e.activation(hidden[s][:, f, :], c.psum[:, f, :], GELU, bias=bias))
                c.emptied[f] = m
                made.append(m)
        if turn:
            b, n, s = (turn - 1) // EXPERTS, (turn - 1) % EXPERTS, (turn - 1) % 2
            out = c.psum[:, 4 + s, :]
            c.pe.wait(chosen_ready, c.emptied[6 + s])
            for k in range(per_seq):
                row = (b * per_seq + k) * EXPERTS + n
                wide = c.product(c.psum[:, 6 + s, k * CHUNK:(k + 1) * CHUNK],
                                 [(c.ident[:, row:row + 1].broadcast_to([P, P]), chosen[:, :])], [])
            m = c.product(out, [(w["w2"][:, (n * HID_BLOCKS1 + f) * P:(n * HID_BLOCKS1 + f + 1) * P], hidden[s][:, f, :])
                                for f in range(HID_BLOCKS1)], [before[-1], c.emptied[4 + s]])
            hidden_used[s] = m
            m = c.act.do([m, given_added[s]], lambda e: e.activation(given[s][:, :], out, ACT.Identity, bias=w["b2"][:, n:n + 1]))
            c.emptied[4 + s] = m
            m = c.dve.do([m, wide], lambda e: e.tensor_tensor(given[s][:, :], given[s][:, :], c.psum[:, 6 + s, :], ALU.mult))
            c.emptied[6 + s] = m
            acc = total[b % 2]
            if n == 0:
                m = c.pool.do([m, c.steps.get(f"total_added{b % 2}")], lambda e: e.tensor_copy(acc[:, :], given[s][:, :]))
            else:
                m = c.pool.do([m], lambda e: e.tensor_tensor(acc[:, :], acc[:, :], given[s][:, :], ALU.add))
            given_added[s] = m
            if n == EXPERTS - 1:
                marks[b] = update_from(c, x, b, attn[:, b, :], attn_marks[b], acc, m)
                c.steps[f"total_added{b % 2}"] = marks[b]
        before = made
    return marks


def update_from(c, x, b, attn, attn_ready, ffn, ffn_ready):
    m = c.act.do([ffn_ready], lambda e: e.activation(ffn[:, :], ffn[:, :], SILU))
    m = c.pool.do([m, attn_ready], lambda e: e.tensor_tensor(ffn[:, :], ffn[:, :], attn, ALU.mult))
    return c.pool.do([m], lambda e: e.tensor_tensor(x[:, b, :], x[:, b, :], ffn[:, :], ALU.add))


def layer1(c, x, xn, attn, x_marks, attn_weights, ffn_weights):
    with ExitStack() as layer_ctx:
        w, w_ready = attn_weights.load(layer_ctx)
        with ExitStack() as ctx:
            xn_marks = normalise_all(c, ctx, x, xn, x_marks)
        c.barrier()
        with ExitStack() as ctx:
            done = attention1(c, ctx, xn, xn_marks, w, w_ready, attn)
    c.barrier()
    with ExitStack() as ctx:
        w, w_ready = ffn_weights.load(ctx)
        weave(choose_tokens(c, ctx, xn, xn_marks, w, w_ready))
        return ffn1(c, ctx, x, xn, xn_marks, attn, done, w, w_ready)


SPAN2 = 32


def attention2(c, ctx, xn, xn_marks, w, w_ready, out):
    buf = lambda name, s=[P, SEQ]: [c.buffer(ctx, f"{name}{i}", s) for i in range(2)]
    q, k, v, own, last, raw = (buf(n) for n in ("q", "k", "v", "own", "last", "raw"))
    norm = norm_buffers(c, ctx, 2)
    done = [None] * SEQS
    scale = 1.0 / float(np.sqrt(P * SPAN2).astype(np.float32))
    blocks = lambda t: t.rearrange("p (b t) -> p b t", b=BLOCKS)

    def tile(b, s):
        x = xn[:, b, :]
        bank = [c.psum[:, 4 * s + i, :] for i in range(4)]
        free = lambda i: c.emptied[4 * s + i]
        wait = [xn_marks[b], w_ready]
        before = c.steps.get(f"bands_weighed{s}")
        made = []
        for i, (name, dst) in enumerate((("q", q), ("k", k))):
            m = c.product(bank[i], [(w["w_" + name], x)], [*wait, free(i)])
            made.append(c.act.do([m, before], lambda e: e.activation(dst[s][:, :], bank[i], ACT.Identity, bias=w["b_" + name])))
            c.emptied[4 * s + i] = made[-1]
        yield
        c.pe.wait(free(2))
        for t in range(BLOCKS):
            m = c.product(bank[2][:, t * P:(t + 1) * P], [(x[:, t * P:(t + 1) * P], w["w_v"])], [])
        bias = w["b_v_rows"].rearrange("p (o d) -> p o d", o=1).broadcast_to([P, BLOCKS, P])
        v_ready = c.dve.do([m, before], lambda e: e.tensor_tensor(blocks(v[s][:, :]), blocks(bank[2]), bias, ALU.add))
        c.emptied[4 * s + 2] = v_ready
        yield
        c.pe.wait(*made, free(0), free(1))
        for t in range(BLOCKS):
            here = slice(t * P, (t + 1) * P)
            m = c.product(bank[0][:, here], [(k[s][:, here], q[s][:, here])], [])
            if t:
                m = c.product(bank[1][:, here], [(k[s][:, (t - 1) * P:t * P], q[s][:, here])], [])
        for i, (dst, name, first) in enumerate(((own, "own_band", 0), (last, "last_band", 1))):
            n = BLOCKS - first
            band = w[name].rearrange("p (o t) -> p o t", o=1).broadcast_to([P, n, P])
            masked = c.dve.do([m, before], lambda e: e.scalar_tensor_tensor(
                blocks(dst[s][:, :])[:, first:, :], blocks(bank[i])[:, first:, :], scale, band, ALU.mult, ALU.mult))
            c.emptied[4 * s + i] = masked
        yield
        c.pe.wait(masked, v_ready, free(3))
        for t in range(BLOCKS):
            here = slice(t * P, (t + 1) * P)
            pairs = [(v[s][:, here], own[s][:, here])]
            if t:
                pairs.append((v[s][:, (t - 1) * P:t * P], last[s][:, here]))
            m = c.product(bank[3][:, here], pairs, [])
        c.steps[f"bands_weighed{s}"] = m
        m = c.act.do([m, c.steps.get(norm[s]["written"])], lambda e: e.activation(raw[s][:, :], bank[3], ACT.Copy))
        c.emptied[4 * s + 3] = m
        yield
        yield from normalise(c, raw[s][:, :], out[:, b, :], m, 4 * s, 4 * s + 1, norm[s], w["ln_w"], w["ln_b"])
        done[b] = norm[s]["done"]

    weave(in_flight(tile, SEQS, 2, lead=6))
    return done


def ffn2(c, ctx, x, xn, xn_marks, attn, attn_marks, w, w_ready):
    rows, rows_scoredy, whole, whole_ready = route_top_two(
        c, ctx, xn, xn_marks, w["w_gate"], w["gate_bias_rows"], w_ready, True, whole_rows=True)
    gated = [c.buffer(ctx, f"gated{i}", [P, SEQ]) for i in range(2)]
    scaled = [c.buffer(ctx, f"scaled{i}", [P, 2, SEQ]) for i in range(2)]
    marks = [None] * SEQS

    def tile(b, slot):
        base = 4 * slot
        total = c.psum[:, base + 2, :]
        here = slice(b * SEQ, (b + 1) * SEQ)
        c.product(total, [(w["be"][0:EXPERTS, :], whole[:, here])], [w_ready, whole_ready[b], c.emptied[base + 2]], stop=False)
        read = [c.steps.get(f"ffn_summed{slot}")] * 2
        for n in range(EXPERTS):
            at, half = base + n % 2, n % 2
            wide = c.psum[:, at, :]
            m = c.product(wide, [(c.pick[0:3 * EXPERTS, n:n + 1].broadcast_to([3 * EXPERTS, P]), rows[:, here])],
                          [rows_scoredy[b], c.emptied[at]])
            m = c.dve.do([m, read[half]], lambda e: e.tensor_tensor(scaled[slot][:, half, :], xn[:, b, :], wide, ALU.mult))
            c.emptied[at] = m
            yield
            read[half] = m = c.product(total, [(w["we"][:, n * P:(n + 1) * P], scaled[slot][:, half, :])], [m],
                                       start=False, stop=n == EXPERTS - 1)
        c.steps[f"ffn_summed{slot}"] = m
        yield
        marks[b] = update(c, gated[slot], x, b, attn[:, b, :], attn_marks[b], total, m, base + 2, slot)
        yield

    weave(in_flight(tile, SEQS, 2, lead=4))
    return marks


def layer2(c, x, xn, attn, x_marks, attn_weights, ffn_weights):
    with ExitStack() as layer_ctx:
        w, w_ready = attn_weights.load(layer_ctx)
        wf, wf_ready = ffn_weights.load(layer_ctx)
        with ExitStack() as ctx:
            xn_marks = normalise_all(c, ctx, x, xn, x_marks)
        c.barrier()
        with ExitStack() as ctx:
            done = attention2(c, ctx, xn, xn_marks, w, w_ready, attn)
        c.barrier()
        with ExitStack() as ctx:
            return ffn2(c, ctx, x, xn, xn_marks, attn, done, wf, wf_ready)


HIDDEN3 = 512
HEADS3, DIM3, WINDOW = 8, 64, 64
PAIRS3 = HEADS3 // 2
KEYS3 = P + WINDOW
DEPTH = 2
QK_SCALE = 8.0
GLU3 = 341
GLU_ROWS = (P, P, GLU3 - 2 * P)
MASKED = -1e30


def attention3(c, ctx, xn, xn_marks, w, w_ready, out):
    normed = c.buffer(ctx, "normed", [P, SEQS, SEQ])
    normed_ready, mamba_done, done = [None] * SEQS, [None] * SEQS, [None] * SEQS

    def opening(b, slot):
        yield from normalise(c, xn[:, b, :], normed[:, b, :], xn_marks[b], 2 * slot, 2 * slot + 1, norm[slot],
                             w["ln1_g"], w["ln1_b"])
        normed_ready[b] = norm[slot]["done"]

    with ExitStack() as inner:
        norm = norm_buffers(c, inner, 3)
        c.pe.wait(w_ready)
        c.dve.wait(w_ready)
        c.act.wait(w_ready)
        weave(in_flight(opening, SEQS, 3, lead=3))
    c.barrier()
    with ExitStack() as inner:
        mamba = Mamba(c, inner, w, w_ready, 1, 8)
        mamba.decay_rates("")

        def front(b):
            if b < SEQS:
                yield from mamba.front("", b % 2, normed[:, b, :], normed_ready[b])

        def scan(b):
            yield from mamba.scan("", b % 2)
            yield from mamba.back("", b % 2, out[:, b, :], None, False)
            mamba_done[b] = c.pool.do([mamba.out_ready], lambda e: e.tensor_tensor(
                out[:, b, :], out[:, b, :], xn[:, b, :], ALU.add))
            yield

        weave(front(0))
        for b in range(SEQS):
            weave(scan(b), front(b + 1))
    c.barrier()
    with ExitStack() as inner:
        c.prefix += "mlp_"
        norm = norm_buffers(c, inner, 2)
        hidden = [c.buffer(inner, f"hidden{s}", [P, HIDDEN3 // P, SEQ]) for s in range(2)]
        more = [c.buffer(inner, f"more{s}", [P, SEQ]) for s in range(2)]

        def mlp(b, s):
            h = normed[:, b, :]
            yield from normalise(c, out[:, b, :], h, mamba_done[b], 4 * s, 4 * s + 1, norm[s], w["ln2_g"], w["ln2_b"])
            m = norm[s]["done"]
            made, free = [], c.steps.get(f"mlp_biased{s}")
            for f in range(HIDDEN3 // P):
                at = 4 * s + f % 3
                m2 = c.product(c.psum[:, at, :], [(w["w1"][:, f * P:(f + 1) * P], h)], [m, c.emptied[at]])
                m2 = c.act.do([m2, free], lambda e: e.activation(hidden[s][:, f, :], c.psum[:, at, :], ACT.Relu, bias=w["b1"][:, f:f + 1]))
                c.emptied[at] = m2
                made.append(m2)
                yield
            total = c.psum[:, 4 * s + 3, :]
            m = c.product(total, [(w["w2"][:, f * P:(f + 1) * P], hidden[s][:, f, :]) for f in range(HIDDEN3 // P)],
                          [made, c.emptied[4 * s + 3]])
            yield
            m = c.act.do([m, c.steps.get(f"mlp_added{s}")], lambda e: e.activation(more[s][:, :], total, ACT.Identity, bias=w["b2"]))
            c.steps[f"mlp_biased{s}"] = c.emptied[4 * s + 3] = m
            m = c.pool.do([m], lambda e: e.tensor_tensor(out[:, b, :], out[:, b, :], more[s][:, :], ALU.add))
            c.steps[f"mlp_added{s}"] = done[b] = m
            yield

        weave(in_flight(mlp, SEQS, 2, lead=7))
    return done


class Ffn3:

    def __init__(self, c, ctx, x, y, y_marks, attn, attn_marks, w, w_ready):
        self.c, self.x, self.y, self.marks, self.attn, self.attn_marks = c, x, y, list(y_marks), attn, attn_marks
        self.w, self.w_ready = w, w_ready
        buf = lambda name, s, d=F32: c.buffer(ctx, name, s, d)
        two = range(2)
        self.h = [buf(f"shifted{s}", [P, SEQ]) for s in two]
        self.q = [buf(f"q{s}", [P, PAIRS3, SEQ]) for s in two]
        self.k = [buf(f"k{s}", [P, PAIRS3, SEQ]) for s in two]
        self.v = [buf(f"v{s}", [P, BLOCKS + 1, HEADS3 * DIM3]) for s in two]
        self.o = [buf(f"o{s}", [P, PAIRS3, SEQ]) for s in two]
        self.scale = [buf(f"qk_scale{s}", [P, 3, BLOCKS, 2 * HEADS3]) for s in two]
        self.k_parts = [buf(f"k_parts{s}", [P, BLOCKS, 3, HEADS3], BF16) for s in two]
        self.k_rows = [buf(f"k_rows{s}", [3 * HEADS3, SEQ], BF16) for s in two]
        self.square = [buf(f"square{i}", [P, SEQ]) for i in two]
        self.turned = [buf(f"turned{i}", [P, SEQ]) for i in two]
        self.p = [buf(f"p{i}", [P, 4, KEYS3]) for i in two]
        self.p_t = [buf(f"p_t{i}", [P, 2, 4 * P]) for i in two]
        self.stats = [buf(f"stats{i}", [P, 4, 4]) for i in two]
        self.norm = norm_buffers(c, ctx, 2)
        self.mask = buf("mask16", [P, 2 * 2 * KEYS3], BF16)
        self.pick_head = buf("pick_head16", [3 * HEADS3, PAIRS3 * P], BF16)
        c.pool.do([w_ready], lambda e: e.tensor_copy(self.mask[:, :], w["masks"]))
        c.pool.do([w_ready], lambda e: e.tensor_copy(self.pick_head[:, :], w["pick_head"]))
        for s in two:
            self.set_up = c.pool.do([], lambda e: e.memset(self.v[s][0:WINDOW, 0, :], 0.0))
        self.bank = self.small = 0

    def one(self):
        self.bank = (self.bank + 1) % 6
        return self.bank

    def pair(self):
        self.bank = (self.bank // 2 * 2 + 3) % 6
        return self.bank - 1

    def shift(self, b, s):
        c, y, h, half = self.c, self.y, self.h[s], P // 2
        free = [self.marks[b], self.set_up, c.steps.get(f"shifted_used{s}")]
        c.pool.do(free, lambda e: e.tensor_copy(h[0:half, :], y[0:half, b, :]))
        c.pool.do([], lambda e: e.memset(h[half:P, 0:1], 0.0))
        return c.pool.do([], lambda e: e.tensor_copy(h[half:P, 1:SEQ], y[half:P, b, 0:SEQ - 1]))

    def queries_keys(self, b, s, d, ready):
        c, w, h = self.c, self.w, self.h[s][:, :]
        own = 6 + s
        sums = c.psum[:, own, 0:BLOCKS * 2 * HEADS3].rearrange("p (b n) -> p b n", b=BLOCKS)
        rotated = []
        turn = 0
        for i in range(PAIRS3):
            for which, dst in (("q", self.q), ("k", self.k)):
                n, at = turn % 2, self.pair()
                turn += 1
                a, a2 = c.psum[:, at, :], c.psum[:, at + 1, :]
                cols = slice(i * P, (i + 1) * P)
                m = c.product(a, [(w[f"w{which}{d}"][:, cols], h)], [ready, self.w_ready, c.emptied[at]])
                m2 = c.product(a2, [(w[f"w{which}_turned{d}"][:, cols], h)], [c.emptied[at + 1]])
                sq = c.act.do([m, c.steps.get(f"square_used{n}")], lambda e: e.activation(self.square[n][:, :], a, ACT.Square))
                out = dst[s][:, i, :]
                m = c.dve.do([m, sq, c.steps.get(f"keys_values_used{s}")], lambda e: e.scalar_tensor_tensor(
                    out, a, w[f"{which}_scale{d}"], w[f"{which}_cos"], ALU.mult, ALU.mult))
                c.emptied[at] = m
                m2 = c.dve.do([m2, c.steps.get(f"turned_added{n}")], lambda e: e.scalar_tensor_tensor(
                    self.turned[n][:, :], a2, w[f"{which}_scale_turned{d}"], w[f"{which}_sin"], ALU.mult, ALU.mult))
                c.emptied[at + 1] = m2
                m = c.pool.do([m, m2], lambda e: e.tensor_tensor(out, out, self.turned[n][:, :], ALU.add))
                c.steps[f"turned_added{n}"] = m
                rotated.append(m)
                yield
                c.pe.wait(sq, c.emptied[own])
                first = (HEADS3 if which == "k" else 0) + 2 * i
                for t in range(BLOCKS):
                    m = c.product(sums[:, t, first:first + 2], [(self.square[n][:, t * P:(t + 1) * P], w["two_heads"])], [])
                c.steps[f"square_used{n}"] = m
        scale = self.scale[s]
        m = c.act.do([m, c.steps.get(f"exps_made{s}")], lambda e: e.activation(scale[:, 0, :, :], sums, ACT.Sqrt))
        c.emptied[own] = m
        m = c.dve.do([m], lambda e: e.tensor_scalar(scale[:, 1, :, :], scale[:, 0, :, :], 1e-12, None, ALU.max))
        m = c.dve.do([m], lambda e: e.reciprocal(scale[:, 2, :, :], scale[:, 1, :, :]))
        yield
        parts = self.k_parts[s]
        k_scale = scale[:, 2, :, HEADS3:2 * HEADS3]
        m = split3(c, c.dve, [parts[:, :, i, :] for i in range(3)], k_scale, [m])
        m = c.dve.do([m], lambda e: e.tensor_scalar(scale[:, 2, :, 0:HEADS3], scale[:, 2, :, 0:HEADS3], QK_SCALE, None, ALU.mult))
        at = self.one()
        rows = c.psum[0:3 * HEADS3, at, 0:SEQ // 2].bitcast(BF16)
        c.pe.wait(m, c.emptied[at])
        for t in range(BLOCKS):
            m = c.pe.do([], lambda e: e.transpose(rows[:, t * P:(t + 1) * P], parts[:, t, :, :].rearrange("p i n -> p (i n)"), c.ident16[:, :]))
        m = c.act.do([m, c.steps.get(f"keys_spread{s}")], lambda e: e.activation(self.k_rows[s][:, :], rows, ACT.Copy))
        c.emptied[at] = m
        yield
        for i in range(PAIRS3):
            at = self.one()
            wide = c.product(c.psum[:, at, :], [(self.pick_head[:, i * P:(i + 1) * P], self.k_rows[s][:, :])], [m, self.set_up, c.emptied[at]])
            k = self.k[s][:, i, :]
            ready = c.dve.do([wide, rotated], lambda e: e.tensor_tensor(k, k, c.psum[:, at, :], ALU.mult))
            c.emptied[at] = ready
        c.steps[f"keys_spread{s}"] = wide
        self.qk_ready = ready
        yield

    def values(self, b, s, d, ready):
        c, w, h = self.c, self.w, self.h[s]
        for t in range(BLOCKS + 1):
            at = self.one()
            first, rows = t * P - WINDOW, slice(0, P)
            tokens = slice(max(first, 0), min(first + P, SEQ))
            if t == 0:
                rows = slice(WINDOW, P)
            elif t == BLOCKS:
                rows = slice(0, WINDOW)
            m = c.product(c.psum[rows, at, :], [(h[:, tokens], w[f"wv{d}"])], [ready, self.w_ready, c.emptied[at]])
            m = c.act.do([m, c.steps.get(f"keys_values_used{s}")], lambda e: e.activation(self.v[s][rows, t, :], c.psum[rows, at, :], ACT.Copy))
            c.emptied[at] = m
            if t % 2:
                yield
        self.v_ready = m
        c.steps[f"shifted_used{s}"] = c.pe.last()
        yield

    def attend(self, b, s):
        c, w, q, k, v, scale = self.c, self.w, self.q[s], self.k[s], self.v[s], self.scale[s]
        qk_ready, v_ready = self.qk_ready, self.v_ready
        own = 6 + s
        for t in range(BLOCKS):
            here = slice(t * P, (t + 1) * P)
            keys = slice(max(t * P - WINDOW, 0), (t + 1) * P)
            gap = KEYS3 - (keys.stop - keys.start)
            mask = self.mask[:, (t == 0) * 2 * KEYS3:((t == 0) + 1) * 2 * KEYS3]
            for quad in range(2):
                n = self.small = (self.small + 1) % 2
                at = self.pair()
                for j in range(2):
                    c.pe.wait(qk_ready, c.emptied[at + j])
                    c.pe.queue.matmul(c.psum[:, at + j, 0:2 * KEYS3], c.ident16[:, :], mask, start=True, stop=False)
                    for i in range(2):
                        rows, pair = slice(64 * j, 64 * j + DIM3), 2 * quad + i
                        m = c.product(c.psum[:, at + j, i * KEYS3 + gap:(i + 1) * KEYS3],
                                      [(q[rows, pair, here], k[rows, pair, keys])], [], start=False, stop=i == 1)
                scores = c.psum[:, at:at + 2, 0:2 * KEYS3].rearrange("p j (i n) -> p j i n", i=2)
                stats, p = self.stats[n], self.p[n]
                factor = scale[:, 2, t, 4 * quad:4 * quad + 4].rearrange("p (i j) -> p j i", j=2)
                by_bank = lambda row: stats[:, row, :].rearrange("p (j i) -> p j i", j=2)
                m = c.dve.do([m, c.steps.get(f"p_normed{n}")], lambda e: e.tensor_reduce(
                    by_bank(0), scores, AX.X, ALU.max))
                m = c.dve.do([m], lambda e: e.scalar_tensor_tensor(by_bank(1), by_bank(0), -1.0, factor, ALU.mult, ALU.mult))
                for n4 in range(4):
                    j, i = divmod(n4, 2)
                    m2 = c.act.do([m, c.steps.get(f"p_transposed{n}")], lambda e: e.activation(
                        p[:, n4, :], scores[:, j, i, :], ACT.Exp, bias=stats[:, 1, n4:n4 + 1],
                        scale=factor[:, j, i:i + 1], accum_out=stats[:, 2, n4:n4 + 1]))
                c.emptied[at] = c.emptied[at + 1] = m2
                c.steps[f"exps_made{s}"] = m2
                m = c.dve.do([m2], lambda e: e.reciprocal(stats[:, 3, :], stats[:, 2, :]))
                wide = stats[:, 3, :].rearrange("p (n o) -> p n o", o=1).broadcast_to([P, 4, KEYS3])
                m = c.pool.do([m], lambda e: e.tensor_tensor(p[:, :, :], p[:, :, :], wide, ALU.mult))
                c.steps[f"p_normed{n}"] = m
                yield
                at = self.pair()
                c.pe.wait(m, c.emptied[at], c.emptied[at + 1])
                for i in range(4):
                    m = c.pe.do([], lambda e: e.transpose(c.psum[:, at, i * P:(i + 1) * P], p[:, i, 0:P], c.ident[:, :]))
                for i in range(4):
                    m2 = c.pe.do([], lambda e: e.transpose(c.psum[0:WINDOW, at + 1, i * P:(i + 1) * P], p[:, i, P:KEYS3], c.ident[:, :]))
                c.steps[f"p_transposed{n}"] = m2
                p_t = self.p_t[n]
                a = c.dve.do([m, c.steps.get(f"p_weighed{n}")], lambda e: e.tensor_copy(p_t[:, 0, :], c.psum[:, at, :]))
                z = c.act.do([m2, c.steps.get(f"p_weighed{n}")], lambda e: e.activation(p_t[0:WINDOW, 1, :], c.psum[0:WINDOW, at + 1, :], ACT.Copy))
                c.emptied[at], c.emptied[at + 1] = a, z
                yield
                c.pe.wait(a, z, v_ready)
                if quad == 0:
                    c.pe.wait(c.emptied[own])
                for i in range(4):
                    j, pair = i // 2, 2 * quad + i % 2
                    head, rows = 2 * pair + j, slice(64 * j, 64 * j + DIM3)
                    dims, turned = slice(head * DIM3, (head + 1) * DIM3), slice(i * P, (i + 1) * P)
                    m = c.product(c.psum[rows, own, pair * P:(pair + 1) * P],
                                  [(v[:, t, dims], p_t[:, 0, turned]), (v[0:WINDOW, t + 1, dims], p_t[0:WINDOW, 1, turned])], [])
                c.steps[f"p_weighed{n}"] = m
                yield
            m = c.act.do([m, c.steps.get(f"heads_projected{s}")], lambda e: e.activation(
                self.o[s][:, :, here], c.psum[:, own, :].rearrange("p (i t) -> p i t", i=PAIRS3), ACT.Copy))
            c.emptied[own] = m
        c.steps[f"keys_values_used{s}"] = c.pe.last()
        self.o_ready = m

    def attention_out(self, b, s, d):
        c, w = self.c, self.w
        at = self.one()
        m = c.product(c.psum[:, at, :], [(w[f"wo{d}"][:, i * P:(i + 1) * P], self.o[s][:, i, :]) for i in range(PAIRS3)],
                      [self.o_ready, c.emptied[at]])
        c.steps[f"heads_projected{s}"] = m
        m = c.dve.do([m], lambda e: e.tensor_tensor(self.y[:, b, :], self.y[:, b, :], c.psum[:, at, :], ALU.add))
        c.emptied[at] = self.marks[b] = m
        yield

    def gated_mlp(self, b, s, d):
        c, w, h, hidden = self.c, self.w, self.h[s], self.q[s]
        ready = self.shift(b, s)
        a1, a2 = self.pair(), 6 + s
        yield from normalise(c, h[:, :], h[:, :], ready, a2, a2, self.norm[s], w[f"ln_g{d}"], w[f"ln_b{d}"])
        ready = self.norm[s]["done"]
        for i, rows in enumerate(GLU_ROWS):
            at, n = self.pair(), i % 2
            cols = slice(i * P, i * P + rows)
            ma = c.product(c.psum[0:rows, at, :], [(w[f"w1_a{d}"][:, cols], h[:, :])], [ready, c.emptied[at]])
            mg = c.product(c.psum[0:rows, at + 1, :], [(w[f"w1_g{d}"][:, cols], h[:, :])], [c.emptied[at + 1]])
            gate = self.square[n]
            mg = c.act.do([mg, c.steps.get(f"square_used{n}")], lambda e: e.activation(
                gate[0:rows, :], c.psum[0:rows, at + 1, :], GELU, bias=w[f"b1_g{d}"][0:rows, i:i + 1]))
            c.emptied[at + 1] = mg
            m = c.dve.do([ma, mg, c.steps.get(f"keys_values_used{s}")], lambda e: e.scalar_tensor_tensor(
                hidden[0:rows, i, :], c.psum[0:rows, at, :], w[f"b1_a{d}"][0:rows, i:i + 1], gate[0:rows, :], ALU.add, ALU.mult))
            c.emptied[at] = c.steps[f"square_used{n}"] = m
            yield
        c.steps[f"shifted_used{s}"] = ma
        at = self.one()
        m = c.product(c.psum[:, at, :], [(w[f"w2{d}"][0:rows, i * P:(i + 1) * P], hidden[0:rows, i, :]) for i, rows in enumerate(GLU_ROWS)],
                      [m, c.emptied[at]])
        c.steps[f"keys_values_used{s}"] = m
        m = c.dve.do([m], lambda e: e.scalar_tensor_tensor(
            self.y[:, b, :], c.psum[:, at, :], w[f"b2{d}"], self.y[:, b, :], ALU.add, ALU.add))
        c.emptied[at] = self.marks[b] = m
        yield

    def tile(self, b, s):
        c = self.c
        for d in range(DEPTH):
            ready = self.shift(b, s)
            yield from self.queries_keys(b, s, d, ready)
            yield from self.values(b, s, d, ready)
            yield from self.attend(b, s)
            yield from self.attention_out(b, s, d)
            yield from self.gated_mlp(b, s, d)
        gated = self.square[s]
        m = c.act.do([self.marks[b], c.steps.get(f"square_used{s}")], lambda e: e.activation(gated[:, :], self.y[:, b, :], SILU))
        m = c.pool.do([m, self.attn_marks[b]], lambda e: e.tensor_tensor(gated[:, :], gated[:, :], self.attn[:, b, :], ALU.mult))
        m = c.pool.do([m], lambda e: e.tensor_tensor(self.x[:, b, :], self.x[:, b, :], gated[:, :], ALU.add))
        c.steps[f"square_used{s}"] = self.marks[b] = m
        yield


def layer3(c, x, xn, attn, x_marks, attn_weights, ffn_weights):
    with ExitStack() as layer_ctx:
        w, w_ready = attn_weights.load(layer_ctx)
        with ExitStack() as ctx:
            xn_marks = normalise_all(c, ctx, x, xn, x_marks)
        c.barrier()
        c.prefix = "layer3_attn_"
        with ExitStack() as ctx:
            done = attention3(c, ctx, xn, xn_marks, w, w_ready, attn)
    c.barrier()
    c.prefix = "layer3_ffn_"
    with ExitStack() as ctx:
        w, w_ready = ffn_weights.load(ctx)
        run = Ffn3(c, ctx, x, xn, xn_marks, attn, done, w, w_ready)
        weave(in_flight(run.tile, SEQS, 2, lead=40))
        return run.marks


def columns(a):
    return np.ascontiguousarray(np.moveaxis(a, 0, 1)).reshape(a.shape[1], -1)


def layer0_pieces(i):
    head_pad = lambda a: np.pad(a.reshape(QUADS0, 4, DIM0, -1), ((0, 0), (0, 0), (0, 32 - DIM0), (0, 0)))
    sum_rows = np.zeros((P, QUADS0, HEADS0), np.float32)
    head_rows = np.zeros((HEADS0, QUADS0, P), np.float32)
    for head in range(HEADS0):
        g, j = divmod(head, 4)
        sum_rows[32 * j + DIM0, g, head] = 1.0
        head_rows[head, g, 32 * j:32 * j + 32] = 1.0
    return {
        "wq": i["L0_attn_Wq"].T, "wk": i["L0_attn_Wk"].T, "wv": i["L0_attn_Wv"].T,
        "bq": i["L0_attn_bq"][:, None], "bk": i["L0_attn_bk"][:, None], "bo": i["L0_attn_bo"][:, None],
        "bv_rows": np.broadcast_to(i["L0_attn_bv"], (P, P)),
        "wo_rows": columns(head_pad(i["L0_attn_Wo"].T).reshape(QUADS0, P, P)),
        "mask_rows": np.repeat(i["L0_attn_head_mask"].reshape(QUADS0, 4), 32, axis=1).T,
        "sum_rows": sum_rows.reshape(P, -1), "head_rows": head_rows.reshape(HEADS0, -1),
    }, {
        "w_shared_in": i["L0_ffn_w_shared_in"], "w_shared_out": i["L0_ffn_w_shared_out"],
        "w1_shared": i["L0_ffn_w1_shared"], "w2": columns(i["L0_ffn_w2"]),
        "w_gate": i["L0_ffn_w_gate"], "gate_bias_rows": np.broadcast_to(i["L0_ffn_gate_bias"], (P, EXPERTS)),
    }




def mamba_pieces(i, at, name, names):
    w_in, conv_w, conv_b, x_proj, dt_w, dt_b, a_log, skip, w_out = (i[at + n] for n in names)
    rank = x_proj.shape[0] - BC_ROWS
    halves = w_out.shape[1] // P
    proj = np.concatenate([x_proj[rank:]] * 3 + [x_proj[:rank]], axis=0)
    vector = lambda a: columns(a.reshape(halves, P, -1))
    dt_rows = np.zeros((P, dt_w.shape[0]), np.float32)
    dt_rows[DT_AT:DT_AT + rank] = dt_w.T
    pieces = {"w_in": w_in.T, "conv_w": vector(conv_w), "conv_b": vector(conv_b), "x_proj": vector(proj.T),
              "dt_w": dt_rows, "dt_b": vector(dt_b), "a_log": vector(a_log), "skip": vector(skip),
              "w_out": vector(w_out.T)}
    return {name + n: a for n, a in pieces.items()}


def layer1_pieces(i):
    names = ("in_proj", "conv_w", "conv_b", "x_proj", "dt_w", "dt_b", "A_log", "D", "out_proj")
    pick_state = np.zeros((3 * BC_ROWS, BC_ROWS), np.float32)
    pick_state[np.arange(3 * BC_ROWS), np.arange(3 * BC_ROWS) % BC_ROWS] = 1.0
    row = np.arange(P)
    same = (row[:, None] % EXPERTS == row[None, :] % EXPERTS)
    return {
        **mamba_pieces(i, "L1_attn_fwd_", "fwd_", names), **mamba_pieces(i, "L1_attn_bwd_", "bwd_", names),
        "pick_state": pick_state,
        "merge": columns(i["L1_attn_merge_w"].T.reshape(2, P, P)),
    }, {
        "gate_wide": np.pad(i["L1_ffn_Wg"], ((0, 0), (EXPERTS * (CHUNKS - 1),) * 2)),
        "same_expert": same.astype(np.float32),
        "before": (same & (row[:, None] < row[None, :])).astype(np.float32),
        "w1": columns(i["L1_ffn_W1"]), "b1": columns(i["L1_ffn_b1"].reshape(-1, P, 1)),
        "w2": columns(i["L1_ffn_W2"].reshape(-1, P, P)), "b2": columns(i["L1_ffn_b2"][:, :, None]),
    }


def layer2_pieces(i):
    w, b = i["L2_attn_W_qkv"], i["L2_attn_b_qkv"]
    key, query = np.arange(P)[:, None], np.arange(P)[None, :]
    return {
        "w_q": w[:, 0:P], "w_k": w[:, P:2 * P], "w_v": w[:, 2 * P:3 * P],
        "b_q": b[0:P, None], "b_k": b[P:2 * P, None], "b_v_rows": np.broadcast_to(b[2 * P:3 * P], (P, P)),
        "own_band": ((query >= key) & (query - key < SPAN2)).astype(np.float32),
        "last_band": (query + P - key < SPAN2).astype(np.float32),
        "ln_w": i["L2_attn_ln_w"][:, None], "ln_b": i["L2_attn_ln_b"][:, None],
    }, {
        "w_gate": i["L2_ffn_Wg"], "gate_bias_rows": np.broadcast_to(i["L2_ffn_bg"], (P, EXPERTS)),
        "we": columns(np.swapaxes(i["L2_ffn_We"], 1, 2)), "be": i["L2_ffn_be"],
    }


def rotary_tables():
    half = np.arange(0, DIM3, 2, dtype=np.float32)
    inverse = (np.float32(1.0) / np.float32(10000.0) ** (half / np.float32(DIM3))).astype(np.float32)
    t = np.arange(SEQ, dtype=np.float32)
    turn = t[:, None] * inverse[None, :]
    base = (half + np.float32(0.4 * DIM3)) / np.float32(1.4 * DIM3)
    scale = base[None, :] ** ((t - SEQ // 2) / np.float32(WINDOW // 2))[:, None]
    cos, sin, scale = (np.concatenate([a, a], axis=1).T for a in (np.cos(turn), np.sin(turn), scale))
    sin = sin * np.where(np.arange(DIM3) < DIM3 // 2, -1.0, 1.0)[:, None]
    two = lambda a: np.concatenate([a, a], axis=0).astype(np.float32)
    return {"q_cos": two(cos * scale), "q_sin": two(sin * scale), "k_cos": two(cos / scale), "k_sin": two(sin / scale)}


def layer3_pieces(i):
    names = ("in_proj_w", "conv_w", "conv_b", "x_proj_w", "dt_proj_w", "dt_proj_b", "A_log", "D_param", "out_proj_w")
    pick_state = np.zeros((3 * BC_ROWS, BC_ROWS), np.float32)
    pick_state[np.arange(3 * BC_ROWS), np.arange(3 * BC_ROWS) % BC_ROWS] = 1.0
    attn = {**mamba_pieces(i, "L3_attn_", "", names), "pick_state": pick_state}
    for name in ("ln1_g", "ln1_b", "ln2_g", "ln2_b", "b2"):
        attn[name] = i["L3_attn_" + name][:, None]
    attn["w1"], attn["b1"] = i["L3_attn_w1"].T, i["L3_attn_b1"].reshape(-1, P).T
    attn["w2"] = columns(i["L3_attn_w2"].T.reshape(-1, P, P))

    turned = (np.arange(HEADS3)[:, None] * DIM3 + (np.arange(DIM3) + DIM3 // 2) % DIM3).reshape(-1)
    query, key = np.arange(P)[:, None], np.arange(KEYS3)[None, :] - WINDOW
    seen = (key <= query) & (key >= query - WINDOW)
    masks = [np.where(s, 0.0, MASKED).astype(np.float32) for s in (seen, seen & (key >= 0))]
    pick_head = np.zeros((3, HEADS3, PAIRS3, P), np.float32)
    for head in range(HEADS3):
        pick_head[:, head, head // 2, DIM3 * (head % 2):DIM3 * (head % 2 + 1)] = 1.0
    ffn = {**rotary_tables(), "masks": np.concatenate([m for m in masks for _ in range(2)], axis=1),
           "pick_head": pick_head.reshape(3 * HEADS3, -1),
           "two_heads": (np.arange(P)[:, None] // DIM3 == np.arange(2)[None, :]).astype(np.float32)}
    inner = HEADS3 * DIM3
    vector = lambda a: np.concatenate([a, a])[:, None]
    thirds = lambda a: np.pad(a, (0, 3 * P - GLU3)).reshape(3, P).T
    for d in range(DEPTH):
        qkv = i["L3_ffn_wqkv"][d]
        for n, which in enumerate("qk"):
            part, scale = qkv[:, n * inner:(n + 1) * inner], i[f"L3_ffn_{which}_scale"][d]
            ffn[f"w{which}{d}"], ffn[f"w{which}_turned{d}"] = part, part[:, turned]
            ffn[f"{which}_scale{d}"] = vector(scale)
            ffn[f"{which}_scale_turned{d}"] = vector(scale[turned[:DIM3]])
        ffn[f"wv{d}"] = qkv[:, 2 * inner:]
        ffn[f"wo{d}"] = columns(i["L3_ffn_wo"][d].reshape(PAIRS3, P, P))
        ffn[f"ln_g{d}"], ffn[f"ln_b{d}"] = i["L3_ffn_ln_g"][d][:, None], i["L3_ffn_ln_b"][d][:, None]
        w1, b1 = i["L3_ffn_w1"][d], i["L3_ffn_b1"][d]
        ffn[f"w1_a{d}"], ffn[f"w1_g{d}"] = w1[:, :GLU3], w1[:, GLU3:]
        ffn[f"b1_a{d}"], ffn[f"b1_g{d}"] = thirds(b1[:GLU3]), thirds(b1[GLU3:])
        ffn[f"w2{d}"] = columns(np.pad(i["L3_ffn_w2"][d], ((0, 3 * P - GLU3), (0, 0))).reshape(3, P, P))
        ffn[f"b2{d}"] = i["L3_ffn_b2"][d][:, None]
    return attn, ffn


PIECES = [layer0_pieces, layer1_pieces, layer2_pieces, layer3_pieces]
LAYERS = [layer0, layer1, layer2, layer3]


def program(nc, x_dram, weight_drams, out_dram, places):
    with ExitStack() as ctx:
        c = Chip(nc, ctx)
        buf = lambda name, s, d=F32: c.buffer(ctx, name, s, d)
        x, xn, attn = buf("x", [P, SEQS, SEQ]), buf("xn", [P, SEQS, SEQ]), buf("attn", [P, SEQS, SEQ])
        c.rank, c.pick = buf("rank", [P, EXPERTS]), buf("pick", [P, EXPERTS], BF16)
        x_marks = []
        loads = [Transfers(c.sem(f"x_loaded{b}")) for b in range(SEQS)]
        for b in range(SEQS):
            x_marks.append(loads[b].start(c.sync, x[:, b, :], x_dram[:, b * SEQ:(b + 1) * SEQ]))
        constants(c)
        for n in range(EXPERTS):
            c.pool.do([], lambda e: e.memset(c.rank[:, n:n + 1], float(EXPERTS - n)))
        parts = c.ident[:, 0:3 * EXPERTS].rearrange("p (i e) -> p i e", e=EXPERTS)
        m = c.pool.do([c.constants_ready], lambda e: e.tensor_tensor(c.pick[:, :], parts[:, 0, :], parts[:, 1, :], ALU.add))
        c.constants_ready = c.pool.do([m], lambda e: e.tensor_tensor(c.pick[:, :], c.pick[:, :], parts[:, 2, :], ALU.add))
        for n, (layer, dram, place) in enumerate(zip(LAYERS, weight_drams, places)):
            c.prefix = f"layer{n}_"
            x_marks = layer(c, x, xn, attn, x_marks, *[Weights(c, f"weights{i}", *p) for i, p in enumerate(zip(dram, place))])
            c.barrier()
        stores = Transfers(c.sem("out_stored"))
        for b in range(SEQS):
            stored = stores.start(c.sync, out_dram[:, b * SEQ:(b + 1) * SEQ], x[:, b, :], [x_marks[b]])
        c.sync.wait(stored)


def kernel(**inputs):
    import concourse.bacc as bacc
    from concourse.bass_utils import run_bass_kernel_spmd

    inputs = {name: np.asarray(a) for name, a in inputs.items()}
    x = inputs["L0_attn_x"]
    arrays = {"x_dram": np.ascontiguousarray(x.reshape(TOKENS, P).T)}
    nc = bacc.Bacc("TRN2", target_bir_lowering=False, num_devices=1)
    x_dram = nc.dram_tensor("x_dram", (P, TOKENS), F32, kind="ExternalInput").ap()
    places, drams = [], []
    for n, layer_pieces in enumerate(PIECES):
        places.append([])
        drams.append([])
        for part, pieces in enumerate(layer_pieces(inputs)):
            place, at = {}, 0
            packed = np.zeros((P, sum(a.shape[1] for a in pieces.values())), np.float32)
            for name, a in pieces.items():
                place[name] = (at, a.shape[0], a.shape[1])
                packed[0:a.shape[0], at:at + a.shape[1]] = a
                at += a.shape[1]
            name = f"weights{n}_{part}_dram"
            arrays[name] = packed
            places[-1].append(place)
            drams[-1].append(nc.dram_tensor(name, packed.shape, F32, kind="ExternalInput").ap())
    out_dram = nc.dram_tensor("out_dram", (P, TOKENS), F32, kind="ExternalOutput").ap()
    program(nc, x_dram, drams, out_dram, places)
    result = run_bass_kernel_spmd(nc, [arrays], core_ids=[0])
    return np.ascontiguousarray(result.results[0]["out_dram"].T).reshape(x.shape)
```

```python
from contextlib import ExitStack

import concourse.bass as bass
import concourse.mybir as mybir
import numpy as np

F32 = mybir.dt.float32
BF16 = mybir.dt.bfloat16
I32 = mybir.dt.int32
ALU = mybir.AluOpType
ACT = mybir.ActivationFunctionType
AX = mybir.AxisListType

P = 128
SEQS, SEQ = 8, 512
TOKENS = SEQS * SEQ
BLOCKS = SEQ // P
EXPERTS = 8
LN_EPS = 1e-5
SILU, GELU = ACT.Silu, ACT.Gelu


class Engine:

    def __init__(self, queue, sem, serial=False):
        self.queue, self.sem, self.count, self.reached, self.serial = queue, sem, 0, {}, serial

    def wait(self, *marks):
        for mark in marks:
            if mark is None:
                continue
            if isinstance(mark, list):
                self.wait(*mark)
                continue
            sem, value = mark
            if self.reached.get(id(sem), 0) < value:
                self.queue.wait_ge(sem, value)
                self.reached[id(sem)] = value

    def do(self, after, build):
        self.wait(*after)
        if self.serial and self.count:
            self.wait(self.last())
        build(self.queue).then_inc(self.sem, 1)
        self.count += 1
        return self.sem, self.count

    def last(self):
        return self.sem, self.count


class Transfers:

    def __init__(self, sem):
        self.sem, self.count = sem, 0

    def start(self, engine, out, in_, after=()):
        engine.wait(*after)
        engine.queue.dma_start(out, in_).then_inc(self.sem, 16)
        self.count += 16
        return self.sem, self.count


def weave(*runs):
    runs = list(runs)
    while runs:
        for run in list(runs):
            if next(run, "over") == "over":
                runs.remove(run)


def behind(run, other, every):
    for turn, _ in enumerate(run):
        if turn % every == 0:
            next(other, "over")
        yield


def in_flight(make, count, width, lead=1):
    active, started, turn = [], 0, 0
    while active or started < count:
        if started < count and len(active) < width and (not active or turn >= lead):
            active.append(make(started, started % width))
            started, turn = started + 1, 0
        for run in list(active):
            if next(run, "over") == "over":
                active.remove(run)
        turn += 1
        yield


class Chip:

    def __init__(self, nc, ctx):
        self.nc, self.ctx, self.prefix = nc, ctx, ""
        self.names = {}
        self.brief_turn = False
        self.pe = Engine(nc.tensor, self.sem("pe_steps"))
        self.act = Engine(nc.scalar, self.sem("act_steps"))
        self.dve = Engine(nc.vector, self.sem("dve_steps"))
        self.pool = Engine(nc.gpsimd, self.sem("pool_steps"), serial=True)
        self.sync = Engine(nc.sync, self.sem("sync_steps"))
        self.psum = ctx.enter_context(nc.psum_tensor("psum", [P, 8, SEQ], F32))
        self.emptied = [None] * 8
        self.steps = {}

    def sem(self, name):
        return self.ctx.enter_context(self.nc.semaphore(self.prefix + name))

    def buffer(self, ctx, name, shape, dtype=F32):
        name = self.prefix + name
        self.names[name] = count = self.names.get(name, 0) + 1
        return ctx.enter_context(self.nc.sbuf_tensor(f"{name}_{count}" if count > 1 else name, shape, dtype))

    def product(self, out, pairs, after, stop=True, start=True):
        self.pe.wait(*after)
        for i, (lhs_t, rhs) in enumerate(pairs[:-1]):
            self.pe.queue.matmul(out, lhs_t, rhs, start=start and i == 0, stop=False)
        lhs_t, rhs = pairs[-1]
        return self.pe.do([], lambda e: e.matmul(out, lhs_t, rhs, start=start and len(pairs) == 1, stop=stop))

    def brief(self):
        self.brief_turn = not self.brief_turn
        at = 6 if self.brief_turn else 3
        return at, self.psum[:, at, :]

    def barrier(self):
        engines = [self.pe, self.act, self.dve, self.pool]
        marks = [e.last() for e in engines if e.count]
        for e in engines + [self.sync]:
            e.wait(*marks)
        self.emptied = [None] * 8
        self.steps = {}


class Weights:

    def __init__(self, c, name, dram, place):
        self.c, self.name, self.dram, self.place = c, name, dram, place

    def load(self, ctx):
        tile = self.c.buffer(ctx, self.name, list(self.dram.shape))
        ready = Transfers(self.c.sem(self.name + "_loaded")).start(self.c.sync, tile[:, :], self.dram)
        return {name: tile[0:rows, at:at + cols] for name, (at, rows, cols) in self.place.items()}, ready


def constants(c):
    pool, buf = c.pool, lambda n, s, d=F32: c.buffer(c.ctx, n, s, d)
    c.ident = buf("ident", [P, P])
    c.ident16 = buf("ident16", [P, P], BF16)
    c.mean_of = buf("mean_of", [P, P])
    c.eps = buf("eps", [P, 1])
    zero = pool.do([], lambda e: e.memset(c.ident[:, :], 0.0))
    one = pool.do([zero], lambda e: e.affine_select(
        out=c.ident[:, :], in_=c.ident[:, :], compare_op=ALU.not_equal, fill=1.0, base=0,
        pattern=[[-1, P]], channel_multiplier=1))
    pool.do([one], lambda e: e.tensor_copy(c.ident16[:, :], c.ident[:, :]))
    pool.do([], lambda e: e.memset(c.mean_of[:, :], 1.0 / P))
    c.constants_ready = pool.do([], lambda e: e.memset(c.eps[:, :], LN_EPS))


def norm_buffers(c, ctx, slots):
    return [{"written": f"norm_written{s}", "centred": c.buffer(ctx, f"norm_centred{s}", [P, SEQ]),
             "square": c.buffer(ctx, f"norm_square{s}", [P, SEQ]),
             "scale": c.buffer(ctx, f"norm_scale{s}", [P, 2, BLOCKS])} for s in range(slots)]


def normalise(c, src, out, after, bank_a, bank_b, w, gain=None, bias=None, out_free=()):
    a, b = c.psum[:, bank_a, :], c.psum[:, bank_b, 0:BLOCKS]
    centred, square, scale = w["centred"], w["square"], w["scale"]
    mean = c.product(a, [(c.mean_of[:, :], src)], [c.constants_ready, c.emptied[bank_a], after])
    yield
    less = c.dve.do([mean, c.steps.get(w["written"])], lambda e: e.tensor_tensor(centred[:, :], src, a, ALU.subtract))
    yield
    squared = c.act.do([less], lambda e: e.activation(square[:, :], centred[:, :], ACT.Square))
    yield
    c.pe.wait(squared, c.emptied[bank_b])
    for j in range(BLOCKS):
        var = c.product(b[:, j:j + 1], [(square[:, j * P:(j + 1) * P], c.mean_of[:, 0:1])], [])
    yield
    root = c.act.do([var], lambda e: e.activation(scale[:, 0, :], b, ACT.Sqrt, bias=c.eps[:, :]))
    c.emptied[bank_b] = root
    yield
    recip = c.dve.do([root], lambda e: e.reciprocal(scale[:, 1, :], scale[:, 0, :]))
    yield
    c.pe.wait(recip, less)
    for j in range(BLOCKS):
        spread = c.product(a[:, j * P:(j + 1) * P],
                           [(scale[:, 1, j:j + 1].broadcast_to([P, P]), c.ident[:, :])], [])
    yield
    if gain is None:
        done = c.dve.do([spread, *out_free], lambda e: e.tensor_tensor(out, centred[:, :], a, ALU.mult))
        c.emptied[bank_a] = c.steps[w["written"]] = done
    else:
        scaled = c.dve.do([spread], lambda e: e.scalar_tensor_tensor(
            centred[:, :], centred[:, :], gain, a, ALU.mult, ALU.mult))
        c.emptied[bank_a] = scaled
        yield
        done = c.act.do([scaled, *out_free], lambda e: e.activation(out, centred[:, :], ACT.Identity, bias=bias))
        c.steps[w["written"]] = done
    w["done"] = done
    yield


def normalise_all(c, ctx, src, out, src_marks):
    marks = [None] * SEQS
    w = norm_buffers(c, ctx, 3)

    def tile(b, slot):
        yield from normalise(c, src[:, b, :], out[:, b, :], src_marks[b], 2 * slot, 2 * slot + 1, w[slot])
        marks[b] = w[slot]["done"]

    weave(in_flight(tile, SEQS, 3, lead=3))
    return marks


def top_two(c, prob, work, after):
    dve, n = c.dve, prob.shape[1]
    left, hit, first, mask = (work[:, i, :, :] for i in (0, 1, 2, 4))
    peak = work[:, 3, :, 0:1]
    wide = peak.broadcast_to([P, n, EXPERTS])
    rank = c.rank[:, :].rearrange("p (o e) -> p o e", o=1).broadcast_to([P, n, EXPERTS])
    m = dve.do(after, lambda e: e.tensor_copy(left, prob))
    for turn in range(2):
        m = dve.do([m], lambda e: e.tensor_reduce(peak, left, AX.X, ALU.max))
        m = dve.do([m], lambda e: e.tensor_tensor(hit, left, wide, ALU.is_equal))
        m = dve.do([m], lambda e: e.tensor_tensor(hit, hit, rank, ALU.mult))
        m = dve.do([m], lambda e: e.tensor_reduce(peak, hit, AX.X, ALU.max))
        m = dve.do([m], lambda e: e.tensor_tensor(first, hit, wide, ALU.is_equal))
        if turn == 0:
            m = dve.do([m], lambda e: e.tensor_copy(mask, first))
            m = dve.do([m], lambda e: e.scalar_tensor_tensor(left, first, -2.0, left, ALU.mult, ALU.add))
        else:
            m = dve.do([m], lambda e: e.tensor_tensor(mask, mask, first, ALU.add))
    return m


def split3(c, engine, parts, rest, after):
    m = engine.do(after, lambda e: e.tensor_copy(parts[0], rest))
    m = engine.do([m], lambda e: e.tensor_tensor(rest, rest, parts[0], ALU.subtract))
    m = engine.do([m], lambda e: e.tensor_copy(parts[1], rest))
    return engine.do([m], lambda e: e.tensor_tensor(parts[2], rest, parts[1], ALU.subtract))


def route_top_two(c, ctx, xn, xn_marks, gate, gate_bias, weights_ready, renormalise, whole_rows=False):
    n = TOKENS // P
    buf = lambda name, s, d=F32: c.buffer(ctx, name, s, d)
    prob, work = buf("prob", [P, n, EXPERTS]), buf("route_work", [P, 5, n, EXPERTS])
    total, inverse = buf("route_total", [P, n]), buf("route_inverse", [P, n])
    parts = buf("route_parts", [P, n, 3, EXPERTS], BF16)
    spread = buf("route_rows", [3 * EXPERTS, TOKENS], BF16)
    if whole_rows:
        whole, whole_marks = buf("route_whole_rows", [EXPERTS, TOKENS]), []
    logits = c.psum[:, 6, 0:n * EXPERTS].rearrange("p (n e) -> p n e", e=EXPERTS)
    dve, act = c.dve, c.act
    c.pe.wait(c.emptied[6], weights_ready)
    for j in range(n):
        b, k = divmod(j, BLOCKS)
        m = c.product(logits[:, j, :], [(xn[:, b, k * P:(k + 1) * P], gate)], [xn_marks[b]])
    wide = lambda t: t[:, :].rearrange("p (n o) -> p n o", o=1).broadcast_to([P, n, EXPERTS])
    bias = gate_bias.rearrange("p (o e) -> p o e", o=1).broadcast_to([P, n, EXPERTS])
    m = dve.do([m], lambda e: e.tensor_tensor(prob[:, :, :], logits, bias, ALU.add))
    c.emptied[6] = m
    m = dve.do([m], lambda e: e.tensor_reduce(total[:, :], prob[:, :, :], AX.X, ALU.max))
    m = dve.do([m], lambda e: e.tensor_tensor(prob[:, :, :], prob[:, :, :], wide(total), ALU.subtract))
    m = act.do([m], lambda e: e.activation(prob[:, :, :], prob[:, :, :], ACT.Exp))
    m = dve.do([m], lambda e: e.tensor_reduce(total[:, :], prob[:, :, :], AX.X, ALU.add))
    m = dve.do([m], lambda e: e.reciprocal(inverse[:, :], total[:, :]))
    m = dve.do([m], lambda e: e.tensor_tensor(prob[:, :, :], prob[:, :, :], wide(inverse), ALU.mult))
    m = top_two(c, prob[:, :, :], work[:, :, :, :], [m, c.constants_ready])
    m = dve.do([m], lambda e: e.tensor_tensor(prob[:, :, :], prob[:, :, :], work[:, 4, :, :], ALU.mult))
    if renormalise:
        m = dve.do([m], lambda e: e.tensor_reduce(total[:, :], prob[:, :, :], AX.X, ALU.add))
        m = dve.do([m], lambda e: e.reciprocal(inverse[:, :], total[:, :]))
        m = dve.do([m], lambda e: e.tensor_tensor(prob[:, :, :], prob[:, :, :], wide(inverse), ALU.mult))
    if whole_rows:
        for b in range(SEQS):
            c.pe.wait(m, c.emptied[4 + b % 2])
            for k in range(BLOCKS):
                turned = c.pe.do([], lambda e: e.transpose(
                    c.psum[0:EXPERTS, 4 + b % 2, k * P:(k + 1) * P], prob[:, b * BLOCKS + k, :], c.ident[:, :]))
            kept = act.do([turned], lambda e: e.activation(
                whole[:, b * SEQ:(b + 1) * SEQ], c.psum[0:EXPERTS, 4 + b % 2, :], ACT.Copy))
            c.emptied[4 + b % 2] = kept
            whole_marks.append(kept)
        m = kept
    m = split3(c, dve, [parts[:, :, i, :] for i in range(3)], prob[:, :, :], [m])
    marks = []
    for b in range(SEQS):
        rows = c.psum[0:3 * EXPERTS, 6 + b % 2, 0:SEQ // 2].bitcast(BF16)
        c.pe.wait(m, c.emptied[6 + b % 2])
        for k in range(BLOCKS):
            turned = c.pe.do([], lambda e: e.transpose(
                rows[:, k * P:(k + 1) * P], parts[:, b * BLOCKS + k, :, :].rearrange("p i e -> p (i e)"),
                c.ident16[:, :]))
        kept = act.do([turned], lambda e: e.activation(spread[:, b * SEQ:(b + 1) * SEQ], rows, ACT.Copy))
        c.emptied[6 + b % 2] = kept
        marks.append(kept)
    return (spread, marks, whole, whole_marks) if whole_rows else (spread, marks)


def update(c, ctx_buf, x, b, attn, attn_ready, gate_psum, gate_ready, bank, slot):
    gated = ctx_buf
    m = c.act.do([gate_ready, c.steps.get(f"gated_added{slot}")], lambda e: e.activation(gated[:, :], gate_psum, SILU))
    c.emptied[bank] = m
    m = c.pool.do([m, attn_ready], lambda e: e.tensor_tensor(gated[:, :], gated[:, :], attn, ALU.mult))
    m = c.pool.do([m], lambda e: e.tensor_tensor(x[:, b, :], x[:, b, :], gated[:, :], ALU.add))
    c.steps[f"gated_added{slot}"] = m
    return m


STATES = 16
BC_ROWS = 2 * STATES
DT_AT = 3 * BC_ROWS
AHEAD = 2
BEHIND = 2
FRONT_STEPS = 5


class Mamba:

    STATE_BUFFERS, DECAY_BUFFERS, C_BUFFERS = 12, 8, 4

    def __init__(self, c, ctx, w, w_ready, halves, taps):
        self.c, self.w, self.w_ready, self.halves, self.taps = c, w, w_ready, halves, taps
        buf = lambda name, s, d=F32: c.buffer(ctx, name, s, d)
        pad = taps - 1
        self.x_in = [buf(f"mamba_in{h}", [P, pad + SEQ]) for h in range(halves)]
        self.work = buf("mamba_work", [P, 2, SEQ])
        self.proj = buf("mamba_proj", [P, SEQ])
        per_slot = lambda name: [[buf(f"mamba_{name}{s}{h}", [P, SEQ]) for h in range(halves)] for s in range(2)]
        self.x, self.z, self.delta, self.u = per_slot("x"), per_slot("z"), per_slot("delta"), per_slot("u")
        self.bc = [buf(f"mamba_bc{s}", [3 * BC_ROWS, SEQ], BF16) for s in range(2)]
        self.decay = [buf(f"mamba_decay{i}", [P, SEQ]) for i in range(self.DECAY_BUFFERS)]
        self.state = [buf(f"mamba_state{i}", [P, SEQ]) for i in range(self.STATE_BUFFERS)]
        self.c_wide = [buf(f"mamba_c{i}", [P, SEQ]) for i in range(self.C_BUFFERS)]
        self.pick = buf("mamba_pick", [3 * BC_ROWS, BC_ROWS], BF16)
        self.decay_scanned = [None] * self.DECAY_BUFFERS
        self.state_summed = [None] * self.STATE_BUFFERS
        self.c_multiplied = [None] * self.C_BUFFERS
        self.unit_projected = [None] * 2
        self.spreads = 0
        self.unit, self.last_exp = {}, {}
        set_up = [c.pool.do([w_ready], lambda e: e.tensor_copy(self.pick[:, :], w["pick_state"]))]
        set_up += [c.pool.do([], lambda e: e.memset(d[:, 0:1], 0.0)) for d in self.decay]
        set_up += [c.pool.do([], lambda e: e.memset(x[:, 0:pad], 0.0)) for x in self.x_in]
        self.set_up = set_up[-1]

    def decay_rates(self, name):
        a = self.w[name + "a_log"]
        m = self.c.act.do([self.w_ready], lambda e: e.activation(a, a, ACT.Exp))
        self.rates_ready = self.c.act.do([m], lambda e: e.activation(a, a, ACT.Copy, scale=-1.0))

    def front(self, name, slot, src, src_ready):
        c, w, halves, pad = self.c, self.w, range(self.halves), self.taps - 1
        inner = self.halves * P
        wait, free = [src_ready, self.w_ready, self.set_up], self.unit_projected[slot]
        conv_done = []
        for h in halves:
            at, bank = c.brief()
            m = c.product(bank, [(w[name + "w_in"][:, h * P:(h + 1) * P], src)], [*wait, c.emptied[at]])
            m = c.act.do([m, c.steps.get(f"conv_made{h}")], lambda e: e.activation(self.x_in[h][:, pad:pad + SEQ], bank, ACT.Copy))
            c.emptied[at] = m
            yield
            x = self.x[slot][h]
            taps = w[name + "conv_w"][:, h * self.taps:(h + 1) * self.taps]
            m = c.dve.do([m, free], lambda e: e.tensor_scalar(x[:, :], self.x_in[h][:, 0:SEQ], taps[:, 0:1], None, ALU.mult))
            for k in range(1, self.taps):
                m = c.dve.do([m], lambda e: e.scalar_tensor_tensor(
                    x[:, :], self.x_in[h][:, k:k + SEQ], taps[:, k:k + 1], x[:, :], ALU.mult, ALU.add))
                if k % 2:
                    yield
            c.steps[f"conv_made{h}"] = m
            conv_done.append(m)
        banks = [c.brief() for h in halves]
        for h in halves:
            at, bank = banks[h]
            m = c.product(bank, [(w[name + "w_in"][:, inner + h * P:inner + (h + 1) * P], src)], [*wait, c.emptied[at]])
            c.emptied[at] = c.act.do([m, free], lambda e: e.activation(self.z[slot][h][:, :], bank, SILU))
        for h in halves:
            x = self.x[slot][h]
            m = c.act.do([conv_done[h]], lambda e: e.activation(x[:, :], x[:, :], SILU, bias=w[name + "conv_b"][:, h:h + 1]))
        yield
        rows = DT_AT + 8
        at, bank = c.brief()
        proj, bc = self.proj, self.bc[slot]
        m = c.product(bank[0:rows, :], [(w[name + "x_proj"][:, h * rows:(h + 1) * rows], self.x[slot][h][:, :])
                                        for h in halves], [m, c.emptied[at]])
        kept = c.act.do([m, c.steps.get("proj_used")], lambda e: e.activation(proj[0:rows, :], bank[0:rows, :], ACT.Copy))
        m = c.act.do([m, free], lambda e: e.activation(bc[:, :], bank[0:DT_AT, :], ACT.Copy))
        c.emptied[at] = m
        yield
        for first in (BC_ROWS, 2 * BC_ROWS):
            part = slice(first, first + BC_ROWS)
            m = c.dve.do([m, kept], lambda e: e.tensor_tensor(proj[part, :], proj[part, :], bc[part, :], ALU.subtract))
            m = c.dve.do([m], lambda e: e.tensor_copy(bc[part, :], proj[part, :]))
        bc_ready = c.dve.do([m], lambda e: e.tensor_tensor(bc[part, :], proj[part, :], bc[part, :], ALU.subtract))
        yield
        for h in halves:
            at, bank = c.brief()
            bias, work, delta = w[name + "dt_b"][:, h:h + 1], self.work, self.delta[slot][h]
            raw = c.product(bank, [(w[name + "dt_w"][DT_AT:rows, h * P:(h + 1) * P], proj[DT_AT:rows, :])],
                            [kept, c.emptied[at]])
            a = c.act.do([raw, c.steps.get("softplus_added")], lambda e: e.activation(work[:, 0, :], bank, ACT.Abs, bias=bias))
            b = c.dve.do([a, free], lambda e: e.tensor_scalar(delta[:, :], bank, bias, 0.0, ALU.add, ALU.max))
            c.emptied[at] = b
            a = c.act.do([a], lambda e: e.activation(work[:, 1, :], work[:, 0, :], ACT.Exp, scale=-1.0))
            a = c.act.do([a], lambda e: e.activation(work[:, 0, :], work[:, 1, :], ACT.Ln, bias=1.0))
            yield
            m = c.dve.do([a, b], lambda e: e.tensor_tensor(delta[:, :], delta[:, :], work[:, 0, :], ALU.add))
            c.steps["softplus_added"] = m
            m = c.pool.do([m], lambda e: e.tensor_tensor(self.u[slot][h][:, :], delta[:, :], self.x[slot][h][:, :], ALU.mult))
            yield
        c.steps["proj_used"] = [raw, bc_ready]
        self.unit[slot] = [m, bc_ready]

    def spread(self, slot, row):
        c, at = self.c, self.spreads % 3
        self.spreads += 1
        m = c.product(c.psum[:, at, :], [(self.pick[:, row:row + 1].broadcast_to([3 * BC_ROWS, P]), self.bc[slot][:, :])],
                      [self.unit[slot], c.emptied[at]])
        return at, c.psum[:, at, :], m

    def run(self, names, front, finish):
        ready = {}
        yield from front(0)
        ahead = front(1)
        for turn in range(len(names) * STATES + AHEAD + BEHIND):
            unit, n = divmod(turn, STATES)
            if n == 0 and 0 < unit < len(names):
                yield from ahead
            for step, _ in enumerate(self.turn(turn, names, ready), turn * 6):
                if n >= AHEAD + BEHIND and step % FRONT_STEPS == 0:
                    next(ahead, "over")
                yield
            if n == AHEAD + BEHIND - 1 and unit:
                yield from finish(unit - 1)
                ahead = front(unit + 1)

    def turn(self, turn, names, ready):
        if turn < len(names) * STATES:
            yield from self.operands(names, turn, ready)
        if AHEAD <= turn < len(names) * STATES + AHEAD:
            yield from self.scan_state(turn - AHEAD, ready)
        if turn >= AHEAD + BEHIND:
            yield from self.sum_state(turn - AHEAD - BEHIND, ready)

    def operands(self, names, turn, ready):
        c, w, halves = self.c, self.w, range(self.halves)
        unit, n = divmod(turn, STATES)
        slot, rates = unit % 2, w[names[unit] + "a_log"]
        states = [(turn * self.halves + h) % self.STATE_BUFFERS for h in halves]
        decays = [(turn * self.halves + h) % self.DECAY_BUFFERS for h in halves]
        wide = turn % self.C_BUFFERS
        decayed, filled = [], []
        for h in halves:
            decayed.append(c.act.do([self.unit[slot], self.rates_ready, self.set_up, self.decay_scanned[decays[h]]], lambda e: e.activation(
                self.decay[decays[h]][:, 1:SEQ], self.delta[slot][h][:, 1:SEQ], ACT.Exp, scale=rates[:, h * STATES + n:h * STATES + n + 1])))
        yield
        at, b_wide, m = self.spread(slot, n)
        for h in halves:
            filled.append(c.dve.do([m, self.state_summed[states[h]]], lambda e: e.tensor_tensor(
                self.state[states[h]][:, :], b_wide, self.u[slot][h][:, :], ALU.mult)))
        c.emptied[at] = filled[-1]
        at, c_wide, m = self.spread(slot, STATES + n)
        copied = c.act.do([m, self.c_multiplied[wide]], lambda e: e.activation(self.c_wide[wide][:, :], c_wide, ACT.Copy))
        c.emptied[at] = copied
        yield
        ready[turn] = states, decays, wide, decayed, filled, copied

    def scan_state(self, turn, ready):
        c = self.c
        states, decays, wide, decayed, filled, copied = ready[turn]
        multiplied = []
        for h in range(self.halves):
            state, decay = self.state[states[h]][:, :], self.decay[decays[h]][:, :]
            m = c.dve.do([decayed[h], filled[h]], lambda e: e.tensor_tensor_scan(
                state, decay, state, 0.0, ALU.mult, ALU.add))
            self.decay_scanned[decays[h]] = m
            m = c.pool.do([m, copied], lambda e: e.tensor_tensor(state, state, self.c_wide[wide][:, :], ALU.mult))
            multiplied.append(m)
            yield
        self.c_multiplied[wide] = m
        ready[turn] = states, multiplied

    def sum_state(self, turn, ready):
        c, n = self.c, turn % STATES
        states, multiplied = ready.pop(turn)
        for h in range(self.halves):
            m = c.product(c.psum[:, 4 + h, :], [(c.ident[:, :], self.state[states[h]][:, :])],
                          [multiplied[h], c.emptied[4 + h] if n == 0 else None], start=n == 0, stop=n == STATES - 1)
            self.state_summed[states[h]] = self.summed = m
            yield

    def back(self, name, slot, out, free, reverse):
        c, w = self.c, self.w
        for h in range(self.halves):
            y = self.u[slot][h]
            m = c.dve.do([self.summed], lambda e: e.scalar_tensor_tensor(
                y[:, :], self.x[slot][h][:, :], w[name + "skip"][:, h:h + 1], c.psum[:, 4 + h, :], ALU.mult, ALU.add))
            c.emptied[4 + h] = m
            gated = c.pool.do([m], lambda e: e.tensor_tensor(y[:, :], y[:, :], self.z[slot][h][:, :], ALU.mult))
            yield
        at, bank = c.brief()
        m = c.product(bank, [(w[name + "w_out"][:, h * P:(h + 1) * P], self.u[slot][h][:, :])
                             for h in range(self.halves)], [gated, c.emptied[at]])
        self.unit_projected[slot] = m
        src = bank[:, ::-1] if reverse else bank
        self.out_ready = c.act.do([m, free], lambda e: e.activation(out, src, ACT.Copy))
        c.emptied[at] = self.out_ready
        yield


HEADS0, DIM0 = 16, 8
PAIRS0 = HEADS0 // 2
QUADS0 = HEADS0 // 4
TERMS = 6
KEY_PART = (0, 0, 1, 0, 2, 1)
QUERY_PART = (0, 1, 0, 2, 0, 1)
ROWS0 = TERMS * DIM0
SLOTS0 = 3
MAX_ROWS = 3


class Attention0:

    def __init__(self, c, ctx, xn, xn_marks, w, w_ready, out):
        self.c, self.xn, self.xn_marks, self.w, self.w_ready, self.out = c, xn, xn_marks, w, w_ready, out
        buf = lambda name, s, d=F32: c.buffer(ctx, name, s, d)
        self.q_rows = [buf(f"q_rows{s}", [P, PAIRS0, SEQ], BF16) for s in range(SLOTS0)]
        self.k_rows = [buf(f"k_rows{s}", [P, PAIRS0, SEQ], BF16) for s in range(SLOTS0)]
        self.rest = [buf(f"qk_rest{i}", [P, SEQ]) for i in range(2)]
        self.parts = [buf(f"qk_parts{i}", [P, 3, SEQ], BF16) for i in range(2)]
        self.values = [buf(f"values{s}", [P, BLOCKS, HEADS0, 32]) for s in range(SLOTS0)]
        self.peak = [buf(f"peak{s}", [P, BLOCKS, HEADS0]) for s in range(SLOTS0)]
        self.less_peak = buf("less_peak", [HEADS0, SEQ])
        self.peak_parts = buf("peak_parts", [HEADS0, 3, SEQ], BF16)
        self.exps = [buf(f"exps{i}", [P, 2, SEQ]) for i in range(4)]
        self.heads = [buf(f"heads{g}", [P, SEQ]) for g in range(QUADS0)]
        self.sums = buf("sums", [HEADS0, SEQ])
        self.normed = [buf(f"normed{g}", [P, SEQ]) for g in range(QUADS0)]
        dram = lambda name, s: c.nc.dram_tensor(name, s, BF16, kind="Internal").ap()
        self.qk_dram = [[dram(f"qk_dram{i}{s}", [P, 3, SEQ]) for i in range(2)] for s in range(SLOTS0)]
        self.peak_dram = [dram(f"peak_dram{s}", [HEADS0, 3, SEQ]) for s in range(SLOTS0)]
        self.ones_dram = dram("ones_dram", [MAX_ROWS, PAIRS0 * SEQ])
        self.to_dram = [[Transfers(c.sem(f"qk_to_dram{i}{s}")) for i in range(2)] for s in range(SLOTS0)]
        self.from_dram = [Transfers(c.sem(f"qk_from_dram{s}")) for s in range(SLOTS0)]
        self.peak_out = [Transfers(c.sem(f"peak_out{s}")) for s in range(SLOTS0)]
        self.peak_in = [Transfers(c.sem(f"peak_in{s}")) for s in range(SLOTS0)]
        self.ready = [None] * SEQS
        self.values_filled = [None] * SEQS
        self.shifted = [None] * SEQS
        self.done = [None] * SEQS
        self.rows_scored = [None] * SLOTS0
        self.values_weighed = [None] * SLOTS0
        self.exps_weighed = [None] * 4
        self.units = 0
        self.setup()

    def setup(self):
        c = self.c
        self.set = []
        for s in range(SLOTS0):
            m = c.pool.do([], lambda e: e.memset(self.values[s][:, :, :, :], 0.0))
            self.set.append(c.pool.do([m], lambda e: e.memset(self.values[s][:, :, :, DIM0:DIM0 + 1], 1.0)))
        ones = self.exps[0][0:MAX_ROWS, :, :].rearrange("p a t -> p (a t)").bitcast(BF16)[:, 0:2 * SEQ]
        m = c.pool.do([], lambda e: e.memset(ones, 1.0))
        t = Transfers(c.sem("ones_to_dram"))
        for i in range(PAIRS0 * SEQ // (2 * SEQ)):
            stored = t.start(c.sync, self.ones_dram[:, i * 2 * SEQ:(i + 1) * 2 * SEQ], ones, [m])
        t = Transfers(c.sem("ones_to_rows"))
        for s in range(SLOTS0):
            for j in range(2):
                rows = self.k_rows[s][64 * j + ROWS0:64 * j + ROWS0 + MAX_ROWS, :, :]
                self.ones_ready = t.start(c.sync, rows.rearrange("p g t -> p (g t)"), self.ones_dram, [stored])
        self.exps_weighed[0] = stored

    def project(self, b):
        c, w, s, xn = self.c, self.w, b % SLOTS0, self.xn[:, b, :]
        bank = c.psum[:, 7, :]
        moved = []
        for i, name in enumerate(("wq", "wk")):
            bias = w["bq" if i == 0 else "bk"]
            m = c.product(bank, [(w[name], xn)], [self.w_ready, self.xn_marks[b], c.emptied[7]])
            rest, parts = self.rest[i], [self.parts[i][:, k, :] for k in range(3)]
            before = c.steps.get(f"parts_stored{i}")
            m = c.act.do([m, before], lambda e: e.activation(rest[:, :], bank, ACT.Identity, bias=bias))
            c.emptied[7] = m
            m = split3(c, c.pool, parts, rest[:, :], [m])
            yield
            m = self.to_dram[s][i].start(c.sync, self.qk_dram[s][i], self.parts[i][:, :, :], [m, self.ready[b - SLOTS0] if b >= SLOTS0 else None])
            c.steps[f"parts_stored{i}"] = m
            moved.append(m)
            yield
        for i, (rows, term_part) in enumerate(((self.q_rows[s], QUERY_PART), (self.k_rows[s], KEY_PART))):
            src = self.qk_dram[s][i].rearrange("(g j d) k t -> j k d g t", j=2, d=DIM0)
            for j in range(2):
                for t in range(TERMS):
                    at = 64 * j + DIM0 * t
                    self.ready[b] = self.from_dram[s].start(
                        c.sync, rows[at:at + DIM0, :, :], src[j, term_part[t]], [moved[i], self.rows_scored[s]])
                yield
        for k in range(BLOCKS):
            v = c.psum[:, 7, k * P:(k + 1) * P]
            m = c.product(v, [(xn[:, k * P:(k + 1) * P], w["wv"])], [c.emptied[7]] if k == 0 else [])
        for k in range(BLOCKS):
            m2 = c.dve.do([m, self.values_weighed[s], self.set[s]], lambda e: e.tensor_tensor(
                self.values[s][:, k, :, 0:DIM0], bank[:, k * P:(k + 1) * P].rearrange("p (h d) -> p h d", d=DIM0),
                w["bv_rows"].rearrange("p (h d) -> p h d", d=DIM0), ALU.add))
        c.emptied[7] = self.values_filled[b] = m2
        yield

    def take_pair(self):
        self.units += 1
        return 2 * (self.units % 3)

    def maxima(self, b):
        c, s = self.c, b % SLOTS0
        q, k, peak = self.q_rows[s], self.k_rows[s], self.peak[s]
        for block in range(BLOCKS):
            for g in range(PAIRS0):
                at = self.take_pair()
                for j in range(2):
                    rows = slice(64 * j, 64 * j + ROWS0)
                    m = c.product(c.psum[:, at + j, :], [(q[rows, g, block * P:(block + 1) * P], k[rows, g, :])],
                                  [self.ready[b], c.emptied[at + j]])
                m = c.dve.do([m, self.shifted[b - SLOTS0] if b >= SLOTS0 else None], lambda e: e.tensor_reduce(
                    peak[:, block, 2 * g:2 * g + 2], c.psum[:, at:at + 2, :], AX.X, ALU.max))
                c.emptied[at] = c.emptied[at + 1] = m
                yield
        c.pe.wait(m, c.emptied[7])
        for block in range(BLOCKS):
            m = c.pe.do([], lambda e: e.transpose(
                c.psum[0:HEADS0, 7, block * P:(block + 1) * P], peak[:, block, :], c.ident[:, :]))
        m = c.act.do([m, c.steps.get("peak_stored")], lambda e: e.activation(
            self.less_peak[:, :], c.psum[0:HEADS0, 7, :], ACT.Copy, scale=-1.0))
        c.emptied[7] = m
        m = split3(c, c.pool, [self.peak_parts[:, i, :] for i in range(3)], self.less_peak[:, :], [m])
        yield
        m = self.peak_out[s].start(c.sync, self.peak_dram[s], self.peak_parts[:, :, :],
                                   [m, self.shifted[b - SLOTS0] if b >= SLOTS0 else None])
        c.steps["peak_stored"] = m
        src = self.peak_dram[s].rearrange("(g j) k t -> j k g t", j=2)
        for j in range(2):
            at = 64 * j + ROWS0
            self.shifted[b] = self.peak_in[s].start(c.sync, q[at:at + MAX_ROWS, :, :], src[j], [m, self.rows_scored[s]])
        yield

    def attend(self, b):
        c, s = self.c, b % SLOTS0
        q, k, values = self.q_rows[s], self.k_rows[s], self.values[s]
        rows = [slice(64 * j, 64 * j + ROWS0 + MAX_ROWS) for j in range(2)]
        turn = 0
        pending = None
        for quad in range(QUADS0):
            for block in range(BLOCKS):
                exps = []
                for half in range(2):
                    at, g = self.take_pair(), 2 * quad + half
                    for j in range(2):
                        m = c.product(c.psum[:, at + j, :], [(k[rows[j], g, block * P:(block + 1) * P], q[rows[j], g, :])],
                                      [self.ready[b], self.shifted[b], self.ones_ready, c.emptied[at + j]])
                    e_buf, n = self.exps[turn % 4], turn % 4
                    m = c.act.do([m, self.exps_weighed[n]], lambda e: e.activation(
                        e_buf[:, :, :], c.psum[:, at:at + 2, :], ACT.Exp, scale=1.0 / float(np.sqrt(np.float32(DIM0)))))
                    c.emptied[at] = c.emptied[at + 1] = m
                    exps.append((n, m))
                    turn += 1
                    yield
                if pending:
                    self.weigh(b, *pending)
                pending = (quad, block, exps)
        self.rows_scored[s] = c.pe.last()
        self.weigh(b, *pending)
        self.values_weighed[s] = c.pe.last()
        yield

    def divide(self, b):
        c, w = self.c, self.w
        m = c.product(c.psum[0:HEADS0, 7, :], [(w["sum_rows"][:, g * HEADS0:(g + 1) * HEADS0], self.heads[g][:, :])
                                               for g in range(QUADS0)], [self.heads_kept, c.emptied[7]])
        m = c.dve.do([m, c.steps.get("sums_spread")], lambda e: e.reciprocal(self.sums[:, :], c.psum[0:HEADS0, 7, :]))
        c.emptied[7] = m
        yield
        for g in range(QUADS0):
            wide = c.product(c.psum[:, 7, :], [(w["head_rows"][0:HEADS0, g * P:(g + 1) * P], self.sums[:, :])],
                             [m, c.emptied[7]])
            n = c.dve.do([wide, c.steps.get("heads_projected")], lambda e: e.scalar_tensor_tensor(
                self.normed[g][:, :], self.heads[g][:, :], w["mask_rows"][:, g:g + 1], c.psum[:, 7, :], ALU.mult, ALU.mult))
            c.emptied[7] = n
            yield
        c.steps["sums_spread"] = wide
        c.steps["heads_divided"] = n
        m = c.product(c.psum[:, 7, :], [(w["wo_rows"][:, g * P:(g + 1) * P], self.normed[g][:, :])
                                        for g in range(QUADS0)], [n, c.emptied[7]])
        c.steps["heads_projected"] = m
        self.done[b] = c.act.do([m], lambda e: e.activation(self.out[:, b, :], c.psum[:, 7, :], ACT.Identity, bias=w["bo"]))
        c.emptied[7] = self.done[b]
        yield

    def weigh(self, b, quad, block, exps):
        c, values = self.c, self.values[b % SLOTS0]
        c.pe.wait(self.values_filled[b], exps[1][1])
        if block == 0:
            c.pe.wait(c.emptied[6])
        for half in range(2):
            for j in range(2):
                i, head = 2 * half + j, 4 * quad + 2 * half + j
                m = c.product(c.psum[32 * i:32 * i + 32, 6, :],
                              [(values[:, block, head, :], self.exps[exps[half][0]][:, j, :])], [],
                              start=block == 0, stop=block == BLOCKS - 1)
            self.exps_weighed[exps[half][0]] = m
        if block == BLOCKS - 1:
            self.heads_kept = c.dve.do([m, c.steps.get("heads_divided")], lambda e: e.tensor_copy(
                self.heads[quad][:, :], c.psum[:, 6, :]))
            c.emptied[6] = self.heads_kept

    def run(self):
        def on(stage, b):
            if 0 <= b < SEQS:
                yield from stage(b)

        weave(on(self.project, 0))
        weave(on(self.maxima, 0), on(self.project, 1))
        for b in range(SEQS + 1):
            weave(on(self.divide, b - 1), on(self.attend, b), on(self.maxima, b + 1), on(self.project, b + 2))


def swiglu(c, w_in, rhs, after, bank_a, bank_b, silu_buf, out, free):
    a, b = c.psum[:, bank_a, :], c.psum[:, bank_b, :]
    ma = c.product(a, [(w_in[:, 0:P], rhs)], [*after, c.emptied[bank_a]])
    mb = c.product(b, [(w_in[:, P:2 * P], rhs)], [c.emptied[bank_b]])
    yield
    m = c.act.do([ma, *free], lambda e: e.activation(silu_buf, a, SILU))
    c.emptied[bank_a] = m
    yield
    m = c.dve.do([m, mb, *free], lambda e: e.tensor_tensor(out, silu_buf, b, ALU.mult))
    c.emptied[bank_b] = m
    yield m


def ffn0(c, ctx, x, xn, xn_marks, attn, attn_marks, w, w_ready):
    rows, rows_ready = route_top_two(c, ctx, xn, xn_marks, w["w_gate"], w["gate_bias_rows"], w_ready, False)
    buf = lambda name, s=[P, SEQ]: [c.buffer(ctx, f"{name}{i}", s) for i in range(2)]
    silu, shared, hidden, gated, scaled = buf("silu"), buf("shared"), buf("hidden"), buf("gated"), buf("scaled", [P, 2, SEQ])
    marks = [None] * SEQS

    def tile(b, slot):
        base = 4 * slot
        rhs, total = xn[:, b, :], c.psum[:, base + 2, :]
        free = [c.steps.get(f"ffn_summed{slot}")]
        for name, out in (("w_shared_in", shared), ("w1_shared", hidden)):
            for m in swiglu(c, w[name], rhs, [w_ready], base, base + 1, silu[slot][:, :], out[slot][:, :], free):
                yield
            free.append(m)
            if name == "w_shared_in":
                shared_ready = m
        hidden_ready = m
        c.product(total, [(w["w_shared_out"], shared[slot][:, :])], [shared_ready, c.emptied[base + 2]], stop=False)
        summed = [None, None]
        for n in range(EXPERTS):
            wide_bank, half = base + n % 2, n % 2
            wide = c.psum[:, wide_bank, :]
            m = c.product(wide, [(c.pick[0:3 * EXPERTS, n:n + 1].broadcast_to([3 * EXPERTS, P]), rows[:, b * SEQ:(b + 1) * SEQ])],
                          [rows_ready[b], c.emptied[wide_bank]])
            m = c.dve.do([m, hidden_ready, summed[half], *free], lambda e: e.tensor_tensor(
                scaled[slot][:, half, :], hidden[slot][:, :], wide, ALU.mult))
            c.emptied[wide_bank] = m
            yield
            m = c.product(total, [(w["w2"][:, n * P:(n + 1) * P], scaled[slot][:, half, :])], [m],
                          start=False, stop=n == EXPERTS - 1)
            summed[half] = m
        c.steps[f"ffn_summed{slot}"] = m
        yield
        marks[b] = update(c, gated[slot], x, b, attn[:, b, :], attn_marks[b], total, m, base + 2, slot)
        yield

    weave(in_flight(tile, SEQS, 2, lead=6))
    return marks


def layer0(c, x, xn, attn, x_marks, attn_weights, ffn_weights):
    with ExitStack() as layer_ctx:
        w, w_ready = attn_weights.load(layer_ctx)
        wf, wf_ready = ffn_weights.load(layer_ctx)
        with ExitStack() as ctx:
            xn_marks = normalise_all(c, ctx, x, xn, x_marks)
        c.barrier()
        with ExitStack() as ctx:
            attention = Attention0(c, ctx, xn, xn_marks, w, w_ready, attn)
            attention.run()
        c.barrier()
        with ExitStack() as ctx:
            return ffn0(c, ctx, x, xn, xn_marks, attn, attention.done, wf, wf_ready)


CHUNKS = P // EXPERTS
CHUNK = TOKENS // CHUNKS
HIDDEN1 = 512
HID_BLOCKS1 = HIDDEN1 // P
CAPACITY = TOKENS * 2 // EXPERTS


def attention1(c, ctx, xn, xn_marks, w, w_ready, out, done, beside):
    mamba = Mamba(c, ctx, w, w_ready, 2, 4)
    for name in ("fwd_", "bwd_"):
        mamba.decay_rates(name)
    turned = c.buffer(ctx, "turned", [P, SEQ])
    backward = c.buffer(ctx, "backward", [P, SEQ])
    merged = [None]

    def front(u):
        if u >= 2 * SEQS:
            return
        b, backwards = divmod(u, 2)
        src, ready = xn[:, b, :], xn_marks[b]
        if backwards:
            ready = c.act.do([ready, c.steps.get("turned_projected")], lambda e: e.activation(turned[:, :], xn[:, b, ::-1], ACT.Copy))
            src = turned[:, :]
        yield from mamba.front(("fwd_", "bwd_")[backwards], u % 2, src, ready)
        if backwards:
            c.steps["turned_projected"] = c.pe.last()
            c.fronted[b] = [ready, c.pe.last()]

    def finish(u):
        b, backwards = divmod(u, 2)
        yield from mamba.back(("fwd_", "bwd_")[backwards], u % 2, (out[:, b, :], backward[:, :])[backwards], merged[0], backwards)
        if backwards:
            at, bank = c.brief()
            m = c.product(bank, [(w["merge"][:, i * P:(i + 1) * P], (out[:, b, :], backward[:, :])[i]) for i in range(2)],
                          [mamba.out_ready, c.emptied[at]])
            merged[0] = m
            done[b] = c.emptied[at] = c.act.do([m], lambda e: e.activation(out[:, b, :], bank, ACT.Copy))

    weave(behind(mamba.run(("fwd_", "bwd_") * SEQS, front, finish), beside, every=SCAN_STEPS))


def choose_tokens(c, ctx, xn, xn_marks, w, w_ready):
    buf = lambda name, s, d=F32: c.buffer(ctx, name, s, d)
    score, hit, tie, rank = (buf(f"choose_{n}", [P, CHUNK]) for n in ("score", "hit", "tie", "rank"))
    col = buf("choose_columns", [P, 8])
    bits = buf("choose_bits", [P, 5], I32)
    level, step, trial = bits[:, 0:1], bits[:, 1:2], bits[:, 2:5]
    dve, bank = c.dve, c.psum[:, 7, 0:3]
    gate = w["gate_wide"]
    per_seq = SEQ // CHUNK
    at, scores = c.brief()
    scores = scores[:, 0:CHUNK]
    m = c.product(scores, [
        (gate[:, (CHUNKS - 1 - k) * EXPERTS:(2 * CHUNKS - 1 - k) * EXPERTS],
         xn[:, k // per_seq, (k % per_seq) * CHUNK:(k % per_seq + 1) * CHUNK]) for k in range(CHUNKS)],
        [w_ready, xn_marks, c.emptied[at]])
    m = scored = c.emptied[at] = c.act.do([m], lambda e: e.activation(score[:, :], scores, ACT.Sigmoid))
    t = dve.do([], lambda e: e.memset(level, 0))
    for bit in range(28, -1, -2):
        for n in range(3):
            m = dve.do([t], lambda e: e.tensor_scalar(trial[:, n:n + 1], level, (n + 1) << bit, None, ALU.bitwise_or))
            m = dve.do([m, scored], lambda e: e.tensor_scalar(
                hit[:, :], score[:, :], trial[:, n:n + 1].bitcast(F32), 0.0, ALU.is_ge, ALU.add, accum_out=col[:, n:n + 1]))
        m = c.product(bank, [(w["same_expert"], col[:, 0:3])], [m, c.emptied[7]])
        yield
        m = dve.do([m], lambda e: e.tensor_scalar(col[:, 4:7], bank, CAPACITY - 0.5, float(1 << bit), ALU.is_ge, ALU.mult))
        c.emptied[7] = m
        m = dve.do([m], lambda e: e.tensor_reduce(col[:, 7:8], col[:, 4:7], AX.X, ALU.add))
        m = dve.do([m], lambda e: e.tensor_copy(step, col[:, 7:8]))
        t = dve.do([m], lambda e: e.tensor_tensor(level, level, step, ALU.bitwise_or))
    least = level.bitcast(F32)
    m = dve.do([t], lambda e: e.tensor_scalar(hit[:, :], score[:, :], least, 0.0, ALU.is_gt, ALU.add, accum_out=col[:, 1:2]))
    m = dve.do([m], lambda e: e.tensor_scalar(tie[:, :], score[:, :], least, 0.0, ALU.is_equal, ALU.add, accum_out=col[:, 2:3]))
    m = c.product(bank[:, 0:1], [(w["same_expert"], col[:, 1:2]), (w["before"], col[:, 2:3])], [m, c.emptied[7]])
    m = dve.do([m], lambda e: e.tensor_scalar(col[:, 3:4], bank[:, 0:1], -1.0, float(CAPACITY), ALU.mult, ALU.add))
    c.emptied[7] = m
    m = dve.do([m], lambda e: e.memset(rank[:, :], 1.0))
    m = dve.do([m], lambda e: e.tensor_tensor_scan(rank[:, :], rank[:, :], tie[:, :], 0.0, ALU.mult, ALU.add))
    m = dve.do([m], lambda e: e.scalar_tensor_tensor(tie[:, :], rank[:, :], col[:, 3:4], tie[:, :], ALU.is_le, ALU.mult))
    m = dve.do([m], lambda e: e.tensor_tensor(hit[:, :], hit[:, :], tie[:, :], ALU.add))
    m = dve.do([m], lambda e: e.tensor_tensor(score[:, :], score[:, :], hit[:, :], ALU.mult))
    c.chosen = score, m
    yield


def ffn1(c, ctx, x, xn, xn_marks, attn, attn_marks, w, w_ready):
    chosen, chosen_ready = c.chosen
    buf = lambda name, n: [c.buffer(ctx, f"{name}{i}", [P, SEQ]) for i in range(n)]
    hidden, given, total = buf("hidden", HID_BLOCKS1), buf("given", 1), buf("total", 1)
    hidden_used = given_added = total_added = None
    per_seq = SEQ // CHUNK
    out = c.psum[:, 7, :]
    for b, n in ((b, n) for b in range(SEQS) for n in range(EXPERTS)):
        made = []
        for f in range(HID_BLOCKS1):
            at, bank = c.brief()
            first = n * HIDDEN1 + f * P
            m = c.product(bank, [(w["w1"][:, first:first + P], xn[:, b, :])], [xn_marks[b], w_ready, c.emptied[at]])
            bias = w["b1"][:, n * HID_BLOCKS1 + f:n * HID_BLOCKS1 + f + 1]
            m = c.act.do([m, hidden_used], lambda e: e.activation(hidden[f][:, :], bank, GELU, bias=bias))
            c.emptied[at] = m
            made.append(m)
        yield
        hidden_used = m = c.product(out, [(w["w2"][:, (n * HID_BLOCKS1 + f) * P:(n * HID_BLOCKS1 + f + 1) * P], hidden[f][:, :])
                                          for f in range(HID_BLOCKS1)], [made, c.emptied[7]])
        at, bank = c.brief()
        c.pe.wait(chosen_ready, c.emptied[at])
        for k in range(per_seq):
            row = (b * per_seq + k) * EXPERTS + n
            wide = c.product(bank[:, k * CHUNK:(k + 1) * CHUNK],
                             [(c.ident[:, row:row + 1].broadcast_to([P, P]), chosen[:, :])], [])
        m = c.act.do([m, given_added], lambda e: e.activation(given[0][:, :], out, ACT.Identity, bias=w["b2"][:, n:n + 1]))
        c.emptied[7] = m
        acc = total[0]
        goal = acc if n == 0 else given[0]
        m = c.dve.do([m, wide, total_added if n == 0 else None], lambda e: e.tensor_tensor(
            goal[:, :], given[0][:, :], bank, ALU.mult))
        c.emptied[at] = m
        yield
        if n:
            m = c.dve.do([m], lambda e: e.tensor_tensor(acc[:, :], acc[:, :], given[0][:, :], ALU.add))
        given_added = m
        if n == EXPERTS - 1:
            while not c.fronted[b]:
                yield
            total_added = c.act.do([m, c.fronted[b]], lambda e: e.activation(xn[:, b, :], acc[:, :], ACT.Copy))
            c.ffn_done[b] = total_added


def update_from(c, x, b, attn, attn_ready, ffn, ffn_ready):
    m = c.act.do([ffn_ready], lambda e: e.activation(ffn[:, :], ffn[:, :], SILU))
    m = c.pool.do([m, attn_ready], lambda e: e.tensor_tensor(ffn[:, :], ffn[:, :], attn, ALU.mult))
    return c.pool.do([m], lambda e: e.tensor_tensor(x[:, b, :], x[:, b, :], ffn[:, :], ALU.add))


SCAN_STEPS = 7


def layer1(c, x, xn, attn, x_marks, attn_weights, ffn_weights):
    with ExitStack() as layer_ctx:
        w, w_ready = attn_weights.load(layer_ctx)
        wf, wf_ready = ffn_weights.load(layer_ctx)
        with ExitStack() as ctx:
            xn_marks = normalise_all(c, ctx, x, xn, x_marks)
        c.barrier()
        done, c.ffn_done, c.fronted = [None] * SEQS, [None] * SEQS, [None] * SEQS
        with ExitStack() as ctx:
            def ffn():
                yield from choose_tokens(c, ctx, xn, xn_marks, wf, wf_ready)
                yield from ffn1(c, ctx, x, xn, xn_marks, attn, done, wf, wf_ready)

            beside = ffn()
            attention1(c, ctx, xn, xn_marks, w, w_ready, attn, done, beside)
            weave(beside)
            return [update_from(c, x, b, attn[:, b, :], done[b], xn[:, b, :], c.ffn_done[b]) for b in range(SEQS)]


SPAN2 = 32


def attention2(c, ctx, xn, xn_marks, w, w_ready, out):
    buf = lambda name, s=[P, SEQ]: [c.buffer(ctx, f"{name}{i}", s) for i in range(2)]
    q, k, v, own, last, raw = (buf(n) for n in ("q", "k", "v", "own", "last", "raw"))
    norm = norm_buffers(c, ctx, 2)
    done = [None] * SEQS
    scale = 1.0 / float(np.sqrt(P * SPAN2).astype(np.float32))
    blocks = lambda t: t.rearrange("p (b t) -> p b t", b=BLOCKS)

    def tile(b, s):
        x = xn[:, b, :]
        bank = [c.psum[:, 4 * s + i, :] for i in range(4)]
        free = lambda i: c.emptied[4 * s + i]
        wait = [xn_marks[b], w_ready]
        before = c.steps.get(f"bands_weighed{s}")
        made = []
        for i, (name, dst) in enumerate((("q", q), ("k", k))):
            m = c.product(bank[i], [(w["w_" + name], x)], [*wait, free(i)])
            made.append(c.act.do([m, before], lambda e: e.activation(dst[s][:, :], bank[i], ACT.Identity, bias=w["b_" + name])))
            c.emptied[4 * s + i] = made[-1]
        yield
        c.pe.wait(free(2))
        for t in range(BLOCKS):
            m = c.product(bank[2][:, t * P:(t + 1) * P], [(x[:, t * P:(t + 1) * P], w["w_v"])], [])
        bias = w["b_v_rows"].rearrange("p (o d) -> p o d", o=1).broadcast_to([P, BLOCKS, P])
        v_ready = c.dve.do([m, before], lambda e: e.tensor_tensor(blocks(v[s][:, :]), blocks(bank[2]), bias, ALU.add))
        c.emptied[4 * s + 2] = v_ready
        yield
        c.pe.wait(*made, free(0), free(1))
        for t in range(BLOCKS):
            here = slice(t * P, (t + 1) * P)
            m = c.product(bank[0][:, here], [(k[s][:, here], q[s][:, here])], [])
            if t:
                m = c.product(bank[1][:, here], [(k[s][:, (t - 1) * P:t * P], q[s][:, here])], [])
        for i, (dst, name, first) in enumerate(((own, "own_band", 0), (last, "last_band", 1))):
            n = BLOCKS - first
            band = w[name].rearrange("p (o t) -> p o t", o=1).broadcast_to([P, n, P])
            masked = c.dve.do([m, before], lambda e: e.scalar_tensor_tensor(
                blocks(dst[s][:, :])[:, first:, :], blocks(bank[i])[:, first:, :], scale, band, ALU.mult, ALU.mult))
            c.emptied[4 * s + i] = masked
        yield
        c.pe.wait(masked, v_ready, free(3))
        for t in range(BLOCKS):
            here = slice(t * P, (t + 1) * P)
            pairs = [(v[s][:, here], own[s][:, here])]
            if t:
                pairs.append((v[s][:, (t - 1) * P:t * P], last[s][:, here]))
            m = c.product(bank[3][:, here], pairs, [])
        c.steps[f"bands_weighed{s}"] = m
        m = c.act.do([m, c.steps.get(norm[s]["written"])], lambda e: e.activation(raw[s][:, :], bank[3], ACT.Copy))
        c.emptied[4 * s + 3] = m
        yield
        yield from normalise(c, raw[s][:, :], out[:, b, :], m, 4 * s, 4 * s + 1, norm[s], w["ln_w"], w["ln_b"])
        done[b] = norm[s]["done"]

    weave(in_flight(tile, SEQS, 2, lead=6))
    return done


def ffn2(c, ctx, x, xn, xn_marks, attn, attn_marks, w, w_ready):
    rows, rows_ready, whole, whole_ready = route_top_two(
        c, ctx, xn, xn_marks, w["w_gate"], w["gate_bias_rows"], w_ready, True, whole_rows=True)
    gated = [c.buffer(ctx, f"gated{i}", [P, SEQ]) for i in range(2)]
    scaled = [c.buffer(ctx, f"scaled{i}", [P, 2, SEQ]) for i in range(2)]
    marks = [None] * SEQS

    def tile(b, slot):
        base = 4 * slot
        total = c.psum[:, base + 2, :]
        here = slice(b * SEQ, (b + 1) * SEQ)
        c.product(total, [(w["be"][0:EXPERTS, :], whole[:, here])], [w_ready, whole_ready[b], c.emptied[base + 2]], stop=False)
        summed = [c.steps.get(f"ffn_summed{slot}")] * 2
        for n in range(EXPERTS):
            at, half = base + n % 2, n % 2
            wide = c.psum[:, at, :]
            m = c.product(wide, [(c.pick[0:3 * EXPERTS, n:n + 1].broadcast_to([3 * EXPERTS, P]), rows[:, here])],
                          [rows_ready[b], c.emptied[at]])
            m = c.dve.do([m, summed[half]], lambda e: e.tensor_tensor(scaled[slot][:, half, :], xn[:, b, :], wide, ALU.mult))
            c.emptied[at] = m
            yield
            summed[half] = m = c.product(total, [(w["we"][:, n * P:(n + 1) * P], scaled[slot][:, half, :])], [m],
                                       start=False, stop=n == EXPERTS - 1)
        c.steps[f"ffn_summed{slot}"] = m
        yield
        marks[b] = update(c, gated[slot], x, b, attn[:, b, :], attn_marks[b], total, m, base + 2, slot)
        yield

    weave(in_flight(tile, SEQS, 2, lead=4))
    return marks


def layer2(c, x, xn, attn, x_marks, attn_weights, ffn_weights):
    with ExitStack() as layer_ctx:
        w, w_ready = attn_weights.load(layer_ctx)
        wf, wf_ready = ffn_weights.load(layer_ctx)
        with ExitStack() as ctx:
            xn_marks = normalise_all(c, ctx, x, xn, x_marks)
        c.barrier()
        with ExitStack() as ctx:
            done = attention2(c, ctx, xn, xn_marks, w, w_ready, attn)
        c.barrier()
        with ExitStack() as ctx:
            return ffn2(c, ctx, x, xn, xn_marks, attn, done, wf, wf_ready)


HIDDEN3 = 512
HEADS3, DIM3, WINDOW = 8, 64, 64
PAIRS3 = HEADS3 // 2
KEYS3 = P + WINDOW
DEPTH = 2
QK_SCALE = 8.0
GLU3 = 341
GLU_ROWS = (P, P, GLU3 - 2 * P)
MASKED = -1e30


def attention3(c, ctx, xn, xn_marks, w, w_ready, out):
    normed = c.buffer(ctx, "normed", [P, SEQS, SEQ])
    normed_ready, mamba_done, done = [None] * SEQS, [None] * SEQS, [None] * SEQS

    def opening(b, slot):
        yield from normalise(c, xn[:, b, :], normed[:, b, :], xn_marks[b], 2 * slot, 2 * slot + 1, norm[slot],
                             w["ln1_g"], w["ln1_b"])
        normed_ready[b] = norm[slot]["done"]

    with ExitStack() as inner:
        norm = norm_buffers(c, inner, 3)
        c.pe.wait(w_ready)
        c.dve.wait(w_ready)
        c.act.wait(w_ready)
        weave(in_flight(opening, SEQS, 3, lead=3))
    c.barrier()
    with ExitStack() as inner:
        mamba = Mamba(c, inner, w, w_ready, 1, 8)
        mamba.decay_rates("")

        def front(b):
            if b < SEQS:
                yield from mamba.front("", b % 2, normed[:, b, :], normed_ready[b])

        def finish(b):
            yield from mamba.back("", b % 2, out[:, b, :], None, False)
            mamba_done[b] = c.pool.do([mamba.out_ready], lambda e: e.tensor_tensor(
                out[:, b, :], out[:, b, :], xn[:, b, :], ALU.add))
            yield

        weave(mamba.run([""] * SEQS, front, finish))
    c.barrier()
    with ExitStack() as inner:
        c.prefix += "mlp_"
        norm = norm_buffers(c, inner, 2)
        hidden = [c.buffer(inner, f"hidden{s}", [P, HIDDEN3 // P, SEQ]) for s in range(2)]
        more = [c.buffer(inner, f"more{s}", [P, SEQ]) for s in range(2)]

        def mlp(b, s):
            h = normed[:, b, :]
            yield from normalise(c, out[:, b, :], h, mamba_done[b], 4 * s, 4 * s + 1, norm[s], w["ln2_g"], w["ln2_b"])
            m = norm[s]["done"]
            made, free = [], c.steps.get(f"mlp_biased{s}")
            for f in range(HIDDEN3 // P):
                at = 4 * s + f % 3
                m2 = c.product(c.psum[:, at, :], [(w["w1"][:, f * P:(f + 1) * P], h)], [m, c.emptied[at]])
                m2 = c.act.do([m2, free], lambda e: e.activation(hidden[s][:, f, :], c.psum[:, at, :], ACT.Relu, bias=w["b1"][:, f:f + 1]))
                c.emptied[at] = m2
                made.append(m2)
                yield
            total = c.psum[:, 4 * s + 3, :]
            m = c.product(total, [(w["w2"][:, f * P:(f + 1) * P], hidden[s][:, f, :]) for f in range(HIDDEN3 // P)],
                          [made, c.emptied[4 * s + 3]])
            yield
            m = c.act.do([m, c.steps.get(f"mlp_added{s}")], lambda e: e.activation(more[s][:, :], total, ACT.Identity, bias=w["b2"]))
            c.steps[f"mlp_biased{s}"] = c.emptied[4 * s + 3] = m
            m = c.pool.do([m], lambda e: e.tensor_tensor(out[:, b, :], out[:, b, :], more[s][:, :], ALU.add))
            c.steps[f"mlp_added{s}"] = done[b] = m
            yield

        weave(in_flight(mlp, SEQS, 2, lead=7))
    return done


class Ffn3:

    def __init__(self, c, ctx, x, y, y_marks, attn, attn_marks, w, w_ready):
        self.c, self.x, self.y, self.marks, self.attn, self.attn_marks = c, x, y, list(y_marks), attn, attn_marks
        self.w, self.w_ready = w, w_ready
        buf = lambda name, s, d=F32: c.buffer(ctx, name, s, d)
        two = range(2)
        self.h = [buf(f"shifted{s}", [P, SEQ]) for s in two]
        self.q = [buf(f"q{s}", [P, PAIRS3, SEQ]) for s in two]
        self.k = [buf(f"k{s}", [P, PAIRS3, SEQ]) for s in two]
        self.v = [buf(f"v{s}", [P, BLOCKS + 1, HEADS3 * DIM3]) for s in two]
        self.o = self.q
        self.scale = [buf(f"qk_scale{s}", [P, 3, BLOCKS, 2 * HEADS3]) for s in two]
        self.k_parts = [buf(f"k_parts{s}", [P, BLOCKS, 3, HEADS3], BF16) for s in two]
        self.k_rows = [buf(f"k_rows{s}", [3 * HEADS3, SEQ], BF16) for s in two]
        self.square = [buf(f"square{i}", [P, SEQ]) for i in two]
        self.turned = [buf(f"turned{i}", [P, SEQ]) for i in two]
        self.p = [buf(f"p{i}", [P, 4, KEYS3]) for i in range(4)]
        self.p_t = [buf(f"p_t{i}", [P, 2, 4 * P]) for i in range(4)]
        self.stats = [buf(f"stats{i}", [P, 4, 4]) for i in range(4)]
        self.norm = [{"written": f"norm_written{s}", "centred": self.k[s][:, 0, :], "square": self.k[s][:, 1, :],
                      "scale": buf(f"norm_scale{s}", [P, 2, BLOCKS])} for s in two]
        self.mask = buf("mask16", [P, 2 * 2 * KEYS3], BF16)
        self.pick_head = buf("pick_head16", [3 * HEADS3, PAIRS3 * P], BF16)
        c.pool.do([w_ready], lambda e: e.tensor_copy(self.mask[:, :], w["masks"]))
        c.pool.do([w_ready], lambda e: e.tensor_copy(self.pick_head[:, :], w["pick_head"]))
        for s in two:
            self.set_up = c.pool.do([], lambda e: e.memset(self.v[s][0:WINDOW, 0, :], 0.0))
        self.bank = 0
        self.scales_cut, self.rotated, self.qk_ready, self.v_ready, self.o_ready = ([None] * 2 for _ in range(5))

    def one(self):
        self.bank = (self.bank + 1) % 6
        return self.bank

    def pair(self):
        self.bank = (self.bank // 2 * 2 + 3) % 6
        return self.bank - 1

    def shift(self, b, s):
        c, y, h, half = self.c, self.y, self.h[s], P // 2
        free = [self.marks[b], self.set_up, c.steps.get(f"shifted_used{s}")]
        c.dve.do(free, lambda e: e.tensor_copy(h[0:half, :], y[0:half, b, :]))
        c.dve.do([], lambda e: e.memset(h[half:P, 0:1], 0.0))
        return c.dve.do([], lambda e: e.tensor_copy(h[half:P, 1:SEQ], y[half:P, b, 0:SEQ - 1]))

    def queries_keys(self, b, s, d, ready):
        c, w, h = self.c, self.w, self.h[s][:, :]
        own = 6 + s
        sums = c.psum[:, own, 0:BLOCKS * 2 * HEADS3].rearrange("p (b n) -> p b n", b=BLOCKS)
        rotated = []
        turn = 0
        for i in range(PAIRS3):
            for which, dst in (("q", self.q), ("k", self.k)):
                n, at = turn % 2, self.pair()
                turn += 1
                a, a2 = c.psum[:, at, :], c.psum[:, at + 1, :]
                cols = slice(i * P, (i + 1) * P)
                m = c.product(a, [(w[f"w{which}{d}"][:, cols], h)], [ready, self.w_ready, c.emptied[at]])
                m2 = c.product(a2, [(w[f"w{which}_turned{d}"][:, cols], h)], [c.emptied[at + 1]])
                sq = c.act.do([m, c.steps.get(f"square_used{n}")], lambda e: e.activation(self.square[n][:, :], a, ACT.Square))
                out = dst[s][:, i, :]
                m = c.dve.do([m, sq, c.steps.get(f"keys_values_used{s}"), c.steps.get(f"norm_written{s}")], lambda e: e.scalar_tensor_tensor(
                    out, a, w[f"{which}_scale{d}"], w[f"{which}_cos"], ALU.mult, ALU.mult))
                c.emptied[at] = m
                m2 = c.dve.do([m2, c.steps.get(f"turned_added{n}")], lambda e: e.scalar_tensor_tensor(
                    self.turned[n][:, :], a2, w[f"{which}_scale_turned{d}"], w[f"{which}_sin"], ALU.mult, ALU.mult))
                c.emptied[at + 1] = m2
                m = c.pool.do([m, m2], lambda e: e.tensor_tensor(out, out, self.turned[n][:, :], ALU.add))
                c.steps[f"turned_added{n}"] = m
                rotated.append(m)
                yield
                c.pe.wait(sq, c.emptied[own])
                first = (HEADS3 if which == "k" else 0) + 2 * i
                for t in range(BLOCKS):
                    m = c.product(sums[:, t, first:first + 2], [(self.square[n][:, t * P:(t + 1) * P], w["two_heads"])], [])
                c.steps[f"square_used{n}"] = m
        scale = self.scale[s]
        m = c.act.do([m, c.steps.get(f"exps_made{s}")], lambda e: e.activation(scale[:, 0, :, :], sums, ACT.Sqrt))
        c.emptied[own] = m
        m = c.dve.do([m], lambda e: e.tensor_scalar(scale[:, 1, :, :], scale[:, 0, :, :], 1e-12, None, ALU.max))
        m = c.dve.do([m], lambda e: e.reciprocal(scale[:, 2, :, :], scale[:, 1, :, :]))
        yield
        parts = self.k_parts[s]
        k_scale = scale[:, 2, :, HEADS3:2 * HEADS3]
        m = split3(c, c.dve, [parts[:, :, i, :] for i in range(3)], k_scale, [m])
        m = c.dve.do([m], lambda e: e.tensor_scalar(scale[:, 2, :, 0:HEADS3], scale[:, 2, :, 0:HEADS3], QK_SCALE, None, ALU.mult))
        self.scales_cut[s], self.rotated[s] = m, rotated
        yield

    def scale_keys(self, s):
        c, parts, m = self.c, self.k_parts[s], self.scales_cut[s]
        at = self.one()
        rows = c.psum[0:3 * HEADS3, at, 0:SEQ // 2].bitcast(BF16)
        c.pe.wait(m, c.emptied[at])
        for t in range(BLOCKS):
            m = c.pe.do([], lambda e: e.transpose(rows[:, t * P:(t + 1) * P], parts[:, t, :, :].rearrange("p i n -> p (i n)"), c.ident16[:, :]))
        m = c.act.do([m, c.steps.get(f"keys_spread{s}")], lambda e: e.activation(self.k_rows[s][:, :], rows, ACT.Copy))
        c.emptied[at] = m
        yield
        for i in range(PAIRS3):
            at = self.one()
            wide = c.product(c.psum[:, at, :], [(self.pick_head[:, i * P:(i + 1) * P], self.k_rows[s][:, :])], [m, self.set_up, c.emptied[at]])
            k = self.k[s][:, i, :]
            ready = c.dve.do([wide, self.rotated[s]], lambda e: e.tensor_tensor(k, k, c.psum[:, at, :], ALU.mult))
            c.emptied[at] = ready
        c.steps[f"keys_spread{s}"] = wide
        self.qk_ready[s] = ready
        yield

    def values(self, b, s, d, ready):
        c, w, h = self.c, self.w, self.h[s]
        for t in range(BLOCKS + 1):
            at = self.one()
            first, rows = t * P - WINDOW, slice(0, P)
            tokens = slice(max(first, 0), min(first + P, SEQ))
            if t == 0:
                rows = slice(WINDOW, P)
            elif t == BLOCKS:
                rows = slice(0, WINDOW)
            m = c.product(c.psum[rows, at, :], [(h[:, tokens], w[f"wv{d}"])], [ready, self.w_ready, c.emptied[at]])
            m = c.act.do([m, c.steps.get(f"keys_values_used{s}")], lambda e: e.activation(self.v[s][rows, t, :], c.psum[rows, at, :], ACT.Copy))
            c.emptied[at] = m
            if t % 2:
                yield
        self.v_ready[s] = m
        c.steps[f"shifted_used{s}"] = c.pe.last()
        yield

    def attend(self, b, s):
        quads = [(t, quad) for t in range(BLOCKS) for quad in range(2)]
        qk_ready, v_ready = self.qk_ready[s], self.v_ready[s]
        normed, turned = {}, {}
        for turn in range(len(quads) + 2):
            if turn < len(quads):
                normed[turn] = self.weights(s, 2 * s + turn % 2, *quads[turn], qk_ready)
                yield
            if 1 <= turn <= len(quads):
                turned[turn - 1] = self.turn_weights(2 * s + (turn - 1) % 2, normed.pop(turn - 1))
                yield
            if turn >= 2:
                self.weigh_values(s, 2 * s + turn % 2, *quads[turn - 2], [turned.pop(turn - 2), v_ready])
                yield
        c = self.c
        c.steps[f"keys_values_used{s}"] = c.pe.last()

    def weights(self, s, n, t, quad, qk_ready):
        c, q, k, scale = self.c, self.q[s], self.k[s], self.scale[s]
        here, keys = slice(t * P, (t + 1) * P), slice(max(t * P - WINDOW, 0), (t + 1) * P)
        gap = KEYS3 - (keys.stop - keys.start)
        mask = self.mask[:, (t == 0) * 2 * KEYS3:((t == 0) + 1) * 2 * KEYS3]
        at = self.pair()
        for j in range(2):
            c.pe.wait(qk_ready, c.emptied[at + j])
            c.pe.queue.matmul(c.psum[:, at + j, 0:2 * KEYS3], c.ident16[:, :], mask, start=True, stop=False)
            for i in range(2):
                rows, pair = slice(DIM3 * j, DIM3 * (j + 1)), 2 * quad + i
                m = c.product(c.psum[:, at + j, i * KEYS3 + gap:(i + 1) * KEYS3],
                              [(q[rows, pair, here], k[rows, pair, keys])], [], start=False, stop=i == 1)
        scores = c.psum[:, at:at + 2, 0:2 * KEYS3].rearrange("p j (i n) -> p j i n", i=2)
        stats, p = self.stats[n], self.p[n]
        factor = scale[:, 2, t, 4 * quad:4 * quad + 4].rearrange("p (i j) -> p j i", j=2)
        by_bank = lambda row: stats[:, row, :].rearrange("p (j i) -> p j i", j=2)
        m = c.dve.do([m, c.steps.get(f"p_normed{n}")], lambda e: e.tensor_reduce(by_bank(0), scores, AX.X, ALU.max))
        m = c.dve.do([m], lambda e: e.scalar_tensor_tensor(by_bank(1), by_bank(0), -1.0, factor, ALU.mult, ALU.mult))
        for n4 in range(4):
            j, i = divmod(n4, 2)
            m2 = c.act.do([m, c.steps.get(f"p_transposed{n}")], lambda e: e.activation(
                p[:, n4, :], scores[:, j, i, :], ACT.Exp, bias=stats[:, 1, n4:n4 + 1],
                scale=factor[:, j, i:i + 1], accum_out=stats[:, 2, n4:n4 + 1]))
        c.emptied[at] = c.emptied[at + 1] = m2
        c.steps[f"exps_made{s}"] = m2
        m = c.dve.do([m2], lambda e: e.reciprocal(stats[:, 3, :], stats[:, 2, :]))
        wide = stats[:, 3, :].rearrange("p (n o) -> p n o", o=1).broadcast_to([P, 4, KEYS3])
        m = c.steps[f"p_normed{n}"] = c.pool.do([m], lambda e: e.tensor_tensor(p[:, :, :], p[:, :, :], wide, ALU.mult))
        return m

    def turn_weights(self, n, normed):
        c, p, p_t, at = self.c, self.p[n], self.p_t[n], self.pair()
        c.pe.wait(normed, c.emptied[at], c.emptied[at + 1])
        for i in range(4):
            m = c.pe.do([], lambda e: e.transpose(c.psum[:, at, i * P:(i + 1) * P], p[:, i, 0:P], c.ident[:, :]))
        for i in range(4):
            m2 = c.pe.do([], lambda e: e.transpose(c.psum[0:WINDOW, at + 1, i * P:(i + 1) * P], p[:, i, P:KEYS3], c.ident[:, :]))
        c.steps[f"p_transposed{n}"] = m2
        weighed = c.steps.get(f"p_weighed{n}")
        a = c.emptied[at] = c.dve.do([m, weighed], lambda e: e.tensor_copy(p_t[:, 0, :], c.psum[:, at, :]))
        z = c.emptied[at + 1] = c.act.do([m2, weighed], lambda e: e.activation(
            p_t[0:WINDOW, 1, :], c.psum[0:WINDOW, at + 1, :], ACT.Copy))
        return [a, z]

    def weigh_values(self, s, n, t, quad, ready):
        c, v, p_t, own = self.c, self.v[s], self.p_t[n], 6 + s
        c.pe.wait(ready, c.emptied[own] if quad == 0 else None)
        for i in range(2):
            pair = 2 * quad + i
            for part, keys in enumerate((slice(0, P), slice(0, WINDOW))):
                for j in range(2):
                    head, place, rows = 2 * pair + j, 2 * j + i, slice(DIM3 * j, DIM3 * (j + 1))
                    m = c.product(c.psum[rows, own, pair * P:(pair + 1) * P],
                                  [(v[keys, t + part, head * DIM3:(head + 1) * DIM3], p_t[keys, part, place * P:(place + 1) * P])],
                                  [], start=part == 0, stop=part == 1)
        c.steps[f"p_weighed{n}"] = m
        if quad == 1:
            here = slice(t * P, (t + 1) * P)
            m = c.act.do([m, c.steps.get(f"heads_projected{s}")], lambda e: e.activation(
                self.o[s][:, :, here], c.psum[:, own, :].rearrange("p (i t) -> p i t", i=PAIRS3), ACT.Copy))
            c.emptied[own] = self.o_ready[s] = m

    def attention_out(self, b, s, d):
        c, w = self.c, self.w
        at = self.one()
        m = c.product(c.psum[:, at, :], [(w[f"wo{d}"][:, i * P:(i + 1) * P], self.o[s][:, i, :]) for i in range(PAIRS3)],
                      [self.o_ready[s], c.emptied[at]])
        c.steps[f"heads_projected{s}"] = m
        m = c.dve.do([m], lambda e: e.tensor_tensor(self.y[:, b, :], self.y[:, b, :], c.psum[:, at, :], ALU.add))
        c.emptied[at] = self.marks[b] = m
        yield

    def gated_mlp(self, b, s, d):
        c, w, h, hidden = self.c, self.w, self.h[s], self.q[s]
        ready = self.shift(b, s)
        a1, a2 = self.pair(), 6 + s
        yield from normalise(c, h[:, :], h[:, :], ready, a2, a2, self.norm[s], w[f"ln_g{d}"], w[f"ln_b{d}"])
        ready = self.norm[s]["done"]
        for i, rows in enumerate(GLU_ROWS):
            at, n = self.pair(), i % 2
            cols = slice(i * P, i * P + rows)
            ma = c.product(c.psum[0:rows, at, :], [(w[f"w1_a{d}"][:, cols], h[:, :])], [ready, c.emptied[at]])
            mg = c.product(c.psum[0:rows, at + 1, :], [(w[f"w1_g{d}"][:, cols], h[:, :])], [c.emptied[at + 1]])
            gate = self.square[n]
            mg = c.act.do([mg, c.steps.get(f"square_used{n}")], lambda e: e.activation(
                gate[0:rows, :], c.psum[0:rows, at + 1, :], GELU, bias=w[f"b1_g{d}"][0:rows, i:i + 1]))
            c.emptied[at + 1] = mg
            m = c.dve.do([ma, mg, c.steps.get(f"keys_values_used{s}")], lambda e: e.scalar_tensor_tensor(
                hidden[0:rows, i, :], c.psum[0:rows, at, :], w[f"b1_a{d}"][0:rows, i:i + 1], gate[0:rows, :], ALU.add, ALU.mult))
            c.emptied[at] = c.steps[f"square_used{n}"] = m
            yield
        c.steps[f"shifted_used{s}"] = ma
        at = self.one()
        m = c.product(c.psum[:, at, :], [(w[f"w2{d}"][0:rows, i * P:(i + 1) * P], hidden[0:rows, i, :]) for i, rows in enumerate(GLU_ROWS)],
                      [m, c.emptied[at]])
        c.steps[f"keys_values_used{s}"] = m
        m = c.dve.do([m], lambda e: e.scalar_tensor_tensor(
            self.y[:, b, :], c.psum[:, at, :], w[f"b2{d}"], self.y[:, b, :], ALU.add, ALU.add))
        c.emptied[at] = self.marks[b] = m
        yield

    def tile(self, b, s):
        c = self.c
        for d in range(DEPTH):
            ready = self.shift(b, s)
            yield from self.queries_keys(b, s, d, ready)
            yield from self.values(b, s, d, ready)
            yield from self.scale_keys(s)
            yield from self.attend(b, s)
            yield from self.attention_out(b, s, d)
            yield from self.gated_mlp(b, s, d)
        gated = self.square[s]
        m = c.act.do([self.marks[b], c.steps.get(f"square_used{s}")], lambda e: e.activation(gated[:, :], self.y[:, b, :], SILU))
        m = c.pool.do([m, self.attn_marks[b]], lambda e: e.tensor_tensor(gated[:, :], gated[:, :], self.attn[:, b, :], ALU.mult))
        m = c.pool.do([m], lambda e: e.tensor_tensor(self.x[:, b, :], self.x[:, b, :], gated[:, :], ALU.add))
        c.steps[f"square_used{s}"] = self.marks[b] = m
        yield


def layer3(c, x, xn, attn, x_marks, attn_weights, ffn_weights):
    with ExitStack() as layer_ctx:
        wf, wf_ready = ffn_weights.load(layer_ctx)
        with ExitStack() as attn_ctx:
            w, w_ready = attn_weights.load(attn_ctx)
            with ExitStack() as ctx:
                xn_marks = normalise_all(c, ctx, x, xn, x_marks)
            c.barrier()
            c.prefix = "layer3_attn_"
            with ExitStack() as ctx:
                done = attention3(c, ctx, xn, xn_marks, w, w_ready, attn)
        c.barrier()
        c.prefix = "layer3_ffn_"
        run = Ffn3(c, layer_ctx, x, xn, xn_marks, attn, done, wf, wf_ready)
        weave(in_flight(run.tile, SEQS, 2, lead=40))
        return run.marks


def columns(a):
    return np.ascontiguousarray(np.moveaxis(a, 0, 1)).reshape(a.shape[1], -1)


def layer0_pieces(i):
    head_pad = lambda a: np.pad(a.reshape(QUADS0, 4, DIM0, -1), ((0, 0), (0, 0), (0, 32 - DIM0), (0, 0)))
    sum_rows = np.zeros((P, QUADS0, HEADS0), np.float32)
    head_rows = np.zeros((HEADS0, QUADS0, P), np.float32)
    for head in range(HEADS0):
        g, j = divmod(head, 4)
        sum_rows[32 * j + DIM0, g, head] = 1.0
        head_rows[head, g, 32 * j:32 * j + 32] = 1.0
    return {
        "wq": i["L0_attn_Wq"].T, "wk": i["L0_attn_Wk"].T, "wv": i["L0_attn_Wv"].T,
        "bq": i["L0_attn_bq"][:, None], "bk": i["L0_attn_bk"][:, None], "bo": i["L0_attn_bo"][:, None],
        "bv_rows": np.broadcast_to(i["L0_attn_bv"], (P, P)),
        "wo_rows": columns(head_pad(i["L0_attn_Wo"].T).reshape(QUADS0, P, P)),
        "mask_rows": np.repeat(i["L0_attn_head_mask"].reshape(QUADS0, 4), 32, axis=1).T,
        "sum_rows": sum_rows.reshape(P, -1), "head_rows": head_rows.reshape(HEADS0, -1),
    }, {
        "w_shared_in": i["L0_ffn_w_shared_in"], "w_shared_out": i["L0_ffn_w_shared_out"],
        "w1_shared": i["L0_ffn_w1_shared"], "w2": columns(i["L0_ffn_w2"]),
        "w_gate": i["L0_ffn_w_gate"], "gate_bias_rows": np.broadcast_to(i["L0_ffn_gate_bias"], (P, EXPERTS)),
    }




def mamba_pieces(i, at, name, names):
    w_in, conv_w, conv_b, x_proj, dt_w, dt_b, a_log, skip, w_out = (i[at + n] for n in names)
    rank = x_proj.shape[0] - BC_ROWS
    halves = w_out.shape[1] // P
    proj = np.concatenate([x_proj[rank:]] * 3 + [x_proj[:rank]], axis=0)
    vector = lambda a: columns(a.reshape(halves, P, -1))
    dt_rows = np.zeros((P, dt_w.shape[0]), np.float32)
    dt_rows[DT_AT:DT_AT + rank] = dt_w.T
    pieces = {"w_in": w_in.T, "conv_w": vector(conv_w), "conv_b": vector(conv_b), "x_proj": vector(proj.T),
              "dt_w": dt_rows, "dt_b": vector(dt_b), "a_log": vector(a_log), "skip": vector(skip),
              "w_out": vector(w_out.T)}
    return {name + n: a for n, a in pieces.items()}


def layer1_pieces(i):
    names = ("in_proj", "conv_w", "conv_b", "x_proj", "dt_w", "dt_b", "A_log", "D", "out_proj")
    pick_state = np.zeros((3 * BC_ROWS, BC_ROWS), np.float32)
    pick_state[np.arange(3 * BC_ROWS), np.arange(3 * BC_ROWS) % BC_ROWS] = 1.0
    row = np.arange(P)
    same = (row[:, None] % EXPERTS == row[None, :] % EXPERTS)
    return {
        **mamba_pieces(i, "L1_attn_fwd_", "fwd_", names), **mamba_pieces(i, "L1_attn_bwd_", "bwd_", names),
        "pick_state": pick_state,
        "merge": columns(i["L1_attn_merge_w"].T.reshape(2, P, P)),
    }, {
        "gate_wide": np.pad(i["L1_ffn_Wg"], ((0, 0), (EXPERTS * (CHUNKS - 1),) * 2)),
        "same_expert": same.astype(np.float32),
        "before": (same & (row[:, None] < row[None, :])).astype(np.float32),
        "w1": columns(i["L1_ffn_W1"]), "b1": columns(i["L1_ffn_b1"].reshape(-1, P, 1)),
        "w2": columns(i["L1_ffn_W2"].reshape(-1, P, P)), "b2": columns(i["L1_ffn_b2"][:, :, None]),
    }


def layer2_pieces(i):
    w, b = i["L2_attn_W_qkv"], i["L2_attn_b_qkv"]
    key, query = np.arange(P)[:, None], np.arange(P)[None, :]
    return {
        "w_q": w[:, 0:P], "w_k": w[:, P:2 * P], "w_v": w[:, 2 * P:3 * P],
        "b_q": b[0:P, None], "b_k": b[P:2 * P, None], "b_v_rows": np.broadcast_to(b[2 * P:3 * P], (P, P)),
        "own_band": ((query >= key) & (query - key < SPAN2)).astype(np.float32),
        "last_band": (query + P - key < SPAN2).astype(np.float32),
        "ln_w": i["L2_attn_ln_w"][:, None], "ln_b": i["L2_attn_ln_b"][:, None],
    }, {
        "w_gate": i["L2_ffn_Wg"], "gate_bias_rows": np.broadcast_to(i["L2_ffn_bg"], (P, EXPERTS)),
        "we": columns(np.swapaxes(i["L2_ffn_We"], 1, 2)), "be": i["L2_ffn_be"],
    }


def rotary_tables():
    half = np.arange(0, DIM3, 2, dtype=np.float32)
    inverse = (np.float32(1.0) / np.float32(10000.0) ** (half / np.float32(DIM3))).astype(np.float32)
    t = np.arange(SEQ, dtype=np.float32)
    turn = t[:, None] * inverse[None, :]
    base = (half + np.float32(0.4 * DIM3)) / np.float32(1.4 * DIM3)
    scale = base[None, :] ** ((t - SEQ // 2) / np.float32(WINDOW // 2))[:, None]
    cos, sin, scale = (np.concatenate([a, a], axis=1).T for a in (np.cos(turn), np.sin(turn), scale))
    sin = sin * np.where(np.arange(DIM3) < DIM3 // 2, -1.0, 1.0)[:, None]
    two = lambda a: np.concatenate([a, a], axis=0).astype(np.float32)
    return {"q_cos": two(cos * scale), "q_sin": two(sin * scale), "k_cos": two(cos / scale), "k_sin": two(sin / scale)}


def layer3_pieces(i):
    names = ("in_proj_w", "conv_w", "conv_b", "x_proj_w", "dt_proj_w", "dt_proj_b", "A_log", "D_param", "out_proj_w")
    pick_state = np.zeros((3 * BC_ROWS, BC_ROWS), np.float32)
    pick_state[np.arange(3 * BC_ROWS), np.arange(3 * BC_ROWS) % BC_ROWS] = 1.0
    attn = {**mamba_pieces(i, "L3_attn_", "", names), "pick_state": pick_state}
    for name in ("ln1_g", "ln1_b", "ln2_g", "ln2_b", "b2"):
        attn[name] = i["L3_attn_" + name][:, None]
    attn["w1"], attn["b1"] = i["L3_attn_w1"].T, i["L3_attn_b1"].reshape(-1, P).T
    attn["w2"] = columns(i["L3_attn_w2"].T.reshape(-1, P, P))

    turned = (np.arange(HEADS3)[:, None] * DIM3 + (np.arange(DIM3) + DIM3 // 2) % DIM3).reshape(-1)
    query, key = np.arange(P)[:, None], np.arange(KEYS3)[None, :] - WINDOW
    seen = (key <= query) & (key >= query - WINDOW)
    masks = [np.where(s, 0.0, MASKED).astype(np.float32) for s in (seen, seen & (key >= 0))]
    pick_head = np.zeros((3, HEADS3, PAIRS3, P), np.float32)
    for head in range(HEADS3):
        pick_head[:, head, head // 2, DIM3 * (head % 2):DIM3 * (head % 2 + 1)] = 1.0
    ffn = {**rotary_tables(), "masks": np.concatenate([m for m in masks for _ in range(2)], axis=1),
           "pick_head": pick_head.reshape(3 * HEADS3, -1),
           "two_heads": (np.arange(P)[:, None] // DIM3 == np.arange(2)[None, :]).astype(np.float32)}
    inner = HEADS3 * DIM3
    vector = lambda a: np.concatenate([a, a])[:, None]
    thirds = lambda a: np.pad(a, (0, 3 * P - GLU3)).reshape(3, P).T
    for d in range(DEPTH):
        qkv = i["L3_ffn_wqkv"][d]
        for n, which in enumerate("qk"):
            part, scale = qkv[:, n * inner:(n + 1) * inner], i[f"L3_ffn_{which}_scale"][d]
            ffn[f"w{which}{d}"], ffn[f"w{which}_turned{d}"] = part, part[:, turned]
            ffn[f"{which}_scale{d}"] = vector(scale)
            ffn[f"{which}_scale_turned{d}"] = vector(scale[turned[:DIM3]])
        ffn[f"wv{d}"] = qkv[:, 2 * inner:]
        ffn[f"wo{d}"] = columns(i["L3_ffn_wo"][d].reshape(PAIRS3, P, P))
        ffn[f"ln_g{d}"], ffn[f"ln_b{d}"] = i["L3_ffn_ln_g"][d][:, None], i["L3_ffn_ln_b"][d][:, None]
        w1, b1 = i["L3_ffn_w1"][d], i["L3_ffn_b1"][d]
        ffn[f"w1_a{d}"], ffn[f"w1_g{d}"] = w1[:, :GLU3], w1[:, GLU3:]
        ffn[f"b1_a{d}"], ffn[f"b1_g{d}"] = thirds(b1[:GLU3]), thirds(b1[GLU3:])
        ffn[f"w2{d}"] = columns(np.pad(i["L3_ffn_w2"][d], ((0, 3 * P - GLU3), (0, 0))).reshape(3, P, P))
        ffn[f"b2{d}"] = i["L3_ffn_b2"][d][:, None]
    return attn, ffn


PIECES = [layer0_pieces, layer1_pieces, layer2_pieces, layer3_pieces]
LAYERS = [layer0, layer1, layer2, layer3]


def program(nc, x_dram, weight_drams, out_dram, places):
    with ExitStack() as ctx:
        c = Chip(nc, ctx)
        buf = lambda name, s, d=F32: c.buffer(ctx, name, s, d)
        x, xn, attn = buf("x", [P, SEQS, SEQ]), buf("xn", [P, SEQS, SEQ]), buf("attn", [P, SEQS, SEQ])
        c.rank, c.pick = buf("rank", [P, EXPERTS]), buf("pick", [P, EXPERTS], BF16)
        x_marks = []
        loads = [Transfers(c.sem(f"x_loaded{b}")) for b in range(SEQS)]
        for b in range(SEQS):
            x_marks.append(loads[b].start(c.sync, x[:, b, :], x_dram[:, b * SEQ:(b + 1) * SEQ]))
        constants(c)
        for n in range(EXPERTS):
            c.pool.do([], lambda e: e.memset(c.rank[:, n:n + 1], float(EXPERTS - n)))
        parts = c.ident[:, 0:3 * EXPERTS].rearrange("p (i e) -> p i e", e=EXPERTS)
        m = c.pool.do([c.constants_ready], lambda e: e.tensor_tensor(c.pick[:, :], parts[:, 0, :], parts[:, 1, :], ALU.add))
        c.constants_ready = c.pool.do([m], lambda e: e.tensor_tensor(c.pick[:, :], c.pick[:, :], parts[:, 2, :], ALU.add))
        for n, (layer, dram, place) in enumerate(zip(LAYERS, weight_drams, places)):
            c.prefix = f"layer{n}_"
            x_marks = layer(c, x, xn, attn, x_marks, *[Weights(c, f"weights{i}", *p) for i, p in enumerate(zip(dram, place))])
            c.barrier()
        stores = Transfers(c.sem("out_stored"))
        for b in range(SEQS):
            stored = stores.start(c.sync, out_dram[:, b * SEQ:(b + 1) * SEQ], x[:, b, :], [x_marks[b]])
        c.sync.wait(stored)


def kernel(**inputs):
    import concourse.bacc as bacc
    from concourse.bass_utils import run_bass_kernel_spmd

    inputs = {name: np.asarray(a) for name, a in inputs.items()}
    x = inputs["L0_attn_x"]
    arrays = {"x_dram": np.ascontiguousarray(x.reshape(TOKENS, P).T)}
    nc = bacc.Bacc("TRN2", target_bir_lowering=False, num_devices=1)
    x_dram = nc.dram_tensor("x_dram", (P, TOKENS), F32, kind="ExternalInput").ap()
    places, drams = [], []
    for n, layer_pieces in enumerate(PIECES):
        places.append([])
        drams.append([])
        for part, pieces in enumerate(layer_pieces(inputs)):
            place, at = {}, 0
            packed = np.zeros((P, sum(a.shape[1] for a in pieces.values())), np.float32)
            for name, a in pieces.items():
                place[name] = (at, a.shape[0], a.shape[1])
                packed[0:a.shape[0], at:at + a.shape[1]] = a
                at += a.shape[1]
            name = f"weights{n}_{part}_dram"
            arrays[name] = packed
            places[-1].append(place)
            drams[-1].append(nc.dram_tensor(name, packed.shape, F32, kind="ExternalInput").ap())
    out_dram = nc.dram_tensor("out_dram", (P, TOKENS), F32, kind="ExternalOutput").ap()
    program(nc, x_dram, drams, out_dram, places)
    result = run_bass_kernel_spmd(nc, [arrays], core_ids=[0])
    return np.ascontiguousarray(result.results[0]["out_dram"].T).reshape(x.shape)
```
